# Optimizing a Trainium2 kernel written in Bass

```python
import numpy as np
import jax
import jax.numpy as jnp

def _softmax(x, axis=-1):
    return jax.nn.softmax(x, axis=axis)

def _gelu(x):
    return jax.nn.gelu(x, approximate=True)

def _silu(x):
    return jax.nn.silu(x)

def _sigmoid(x):
    return jax.nn.sigmoid(x)

def _layernorm(x, axis=-1, eps=1e-05):
    m = jnp.mean(x, axis=axis, keepdims=True)
    v = jnp.var(x, axis=axis, keepdims=True)
    return (x - m) / jnp.sqrt(v + eps)

def _scatter_add(tgt, idx, src, axis=0):
    return tgt.at[idx].add(src)

def _segment_sum(src, seg, n):
    return jax.ops.segment_sum(src, seg, n)
kernel_name = 'mk_early_fusion_embed_d1_tok_img1024_r4_8ea54d'

def setup_inputs(seed: int=0):
    np.random.seed(seed)
    _w = jnp.asarray

    def _rec_inputs():
        import jax
        import jax.numpy as jnp
        _rk = jax.random.key(seed)
        x = -0.000222058 + 0.999998 * jax.random.normal(jax.random.fold_in(_rk, 1), (8, 3, 224, 224), jnp.float32)
        x_txt = jax.random.randint(jax.random.fold_in(_rk, 51), (8, 512), 0, 64, jnp.int32)
        return (x, x_txt)
    x, x_txt = _rec_inputs()

    def _L0_tok_setup():
        import jax, jax.numpy as jnp
        import numpy as np
        P = 16
        C = 3
        D = 256

        def _patchify(x, p):
            B, Cc, H, W = x.shape
            gh, gw = (H // p, W // p)
            x = x.reshape(B, Cc, gh, p, gw, p)
            x = x.transpose(0, 2, 4, 1, 3, 5)
            return x.reshape(B, gh * gw, Cc * p * p)
        key = jax.random.key(seed)
        k1, k2, k3, k4, k5 = jax.random.split(key, 5)
        patch_dim = C * P * P
        s1 = 1.0 / np.sqrt(patch_dim)
        s2 = 1.0 / np.sqrt(D)
        return {'x': jax.random.normal(k1, (32, C, 128, 128), dtype=jnp.float32), 'W1': jax.random.uniform(k2, (patch_dim, D), jnp.float32, -s1, s1), 'b1': jax.random.uniform(k3, (D,), jnp.float32, -s1, s1), 'W2': jax.random.uniform(k4, (D, D), jnp.float32, -s2, s2), 'b2': jax.random.uniform(k5, (D,), jnp.float32, -s2, s2)}
    _L0_tok_all = _L0_tok_setup()
    _L0_tok_in = {k: v for k, v in _L0_tok_all.items() if k in ('W1', 'b1', 'W2', 'b2')}
    del _L0_tok_all

    def _L0_txt_setup():
        import jax, jax.numpy as jnp
        import numpy as np
        N_FFT = 64
        HOP = 64
        NUM_FREQ = N_FFT // 2 + 1

        def _stft_mag(sig, window):
            L = sig.shape[1]
            pad = N_FFT // 2
            x = jnp.pad(sig, ((0, 0), (pad, pad)), mode='reflect')
            n_frames = 1 + L // HOP
            idx = jnp.arange(n_frames)[:, None] * HOP + jnp.arange(N_FFT)[None, :]
            frames = x[:, idx] * window
            spec = jnp.fft.rfft(frames, axis=-1)
            r, im = (spec.real, spec.imag)
            m2 = r * r + im * im
            mag = jnp.where(m2 == 0, 0.0, jnp.sqrt(jnp.where(m2 == 0, 1.0, m2)))
            return (mag, n_frames)

        def _linear_interp_last(feat, out_len):
            in_len = feat.shape[-1]
            coord = jnp.clip((jnp.arange(out_len) + 0.5) * (in_len / out_len) - 0.5, 0.0, in_len - 1.0)
            i0 = jnp.floor(coord).astype(jnp.int32)
            i1 = jnp.minimum(i0 + 1, in_len - 1)
            w = (coord - i0).astype(feat.dtype)
            return feat[..., i0] * (1.0 - w) + feat[..., i1] * w
        key = jax.random.key(seed)
        k0, k1, k2 = jax.random.split(key, 3)
        B, L, V, d_model = (2, 256, 64, 256)
        d_emb = int(d_model * 0.7)
        d_stft = d_model - d_emb
        input_ids = jax.random.randint(k0, (B, L), 0, V)
        emb_table = jax.random.normal(k1, (V, d_emb), jnp.float32) * 0.02
        proj_w = jax.random.normal(k2, (d_stft, V * NUM_FREQ), jnp.float32) * 0.02
        proj_b = jnp.zeros((d_stft,), jnp.float32)
        n = jnp.arange(N_FFT, dtype=jnp.float32)
        window = 0.5 * (1.0 - jnp.cos(2.0 * jnp.pi * n / N_FFT))
        return {'input_ids': input_ids, 'emb_table': emb_table, 'proj_w': proj_w, 'proj_b': proj_b, 'window': window}
    _L0_txt_all = _L0_txt_setup()
    _L0_txt_in = {k: v for k, v in _L0_txt_all.items() if k in ('emb_table', 'proj_w', 'proj_b', 'window')}
    del _L0_txt_all

    def _L0_attn_setup():
        import math
        import jax, jax.numpy as jnp
        import numpy as np
        B, L, D = (4, 1024, 256)
        HID, PE, SHORT = (64, 3, 3)
        WIDTH = 3 * D

        def _gen_filter(length, W1, b1, f1, W2, b2, f2, W3, b3):
            t = jnp.arange(length, dtype=jnp.float32) / (length - 1)
            ang = 2.0 * math.pi * jnp.arange(length, dtype=jnp.float32) / length
            phase = 0.0001 * ang
            pe = jnp.stack([t, jnp.cos(phase), -jnp.sin(phase)], axis=-1)
            h = jnp.sin((pe @ W1 + b1) * f1)
            h = jnp.sin((h @ W2 + b2) * f2)
            k = h @ W3 + b3
            dmax, dmin = (math.log(0.01) / 0.3, math.log(0.01) / 1.5)
            deltas = jnp.abs(jnp.linspace(dmax, dmin, D).astype(jnp.float32))
            return k * jnp.exp(-t[:, None] * deltas[None, :])

        def _causal_fft_conv(v, k, bias):
            length = v.shape[1]
            n = 2 * length
            vp = jnp.pad(v, ((0, 0), (length - 1, 0), (0, 0)))
            Vf = jnp.fft.rfft(vp, n=n, axis=1)
            Kf = jnp.fft.rfft(k, n=n, axis=0)
            out = jnp.fft.irfft(Vf * jnp.conj(Kf)[None], n=n, axis=1)[:, :length]
            return out + bias

        def _short_conv(u, w, b):
            length = u.shape[1]
            up = jnp.pad(u, ((0, 0), (2, 2), (0, 0)))
            out = up[:, 0:length] * w[:, 0] + up[:, 1:length + 1] * w[:, 1] + up[:, 2:length + 2] * w[:, 2]
            return out + b
        key = jax.random.key(seed)
        ks = jax.random.split(key, 12)

        def nrm(k, shape, s):
            return jax.random.normal(k, shape, jnp.float32) * s
        return {'x': jax.random.normal(ks[0], (B, L, D), jnp.float32), 'W_in': nrm(ks[1], (D, WIDTH), 0.02), 'b_in': jnp.zeros((WIDTH,), jnp.float32), 'short_w': nrm(ks[2], (WIDTH, SHORT), 0.3), 'short_b': jnp.zeros((WIDTH,), jnp.float32), 'W1': nrm(ks[3], (PE, HID), 0.5), 'b1': jnp.zeros((HID,), jnp.float32), 'f1': jax.random.uniform(ks[4], (HID,), jnp.float32, 0.001, 10.0), 'W2': nrm(ks[5], (HID, HID), 0.3), 'b2': jnp.zeros((HID,), jnp.float32), 'f2': jax.random.uniform(ks[6], (HID,), jnp.float32, 0.001, 10.0), 'W3': nrm(ks[7], (HID, D), 0.3), 'b3': jnp.zeros((D,), jnp.float32), 'filter_bias': jnp.zeros((D,), jnp.float32), 'W_out': nrm(ks[8], (D, D), 0.02), 'b_out': jnp.zeros((D,), jnp.float32)}
    _L0_attn_all = _L0_attn_setup()
    _L0_attn_in = {k: v for k, v in _L0_attn_all.items() if k in ('W_in', 'b_in', 'short_w', 'short_b', 'W1', 'b1', 'f1', 'W2', 'b2', 'f2', 'W3', 'b3', 'filter_bias', 'W_out', 'b_out')}
    del _L0_attn_all

    def _L0_ffn_setup():
        import jax, jax.numpy as jnp
        import numpy as np
        B, S, H, F, G = (8, 512, 256, 1024, 128)
        EPS = 1e-05

        def _dequant(q, scales, g):
            K, N = q.shape
            w = (q.astype(jnp.float32) - 128.0).reshape(K // g, g, N) * scales[:, None, :]
            return w.reshape(K, N)
        key = jax.random.key(seed)
        ks = jax.random.split(key, 8)
        x = jax.random.normal(ks[0], (B, S, H), dtype=jnp.float32)
        ln_gamma = jnp.ones((H,), jnp.float32)
        ln_beta = jnp.zeros((H,), jnp.float32)
        fc1_q = jax.random.randint(ks[1], (H, F), 0, 64, dtype=jnp.int32)
        fc2_q = jax.random.randint(ks[2], (F, H), 0, 64, dtype=jnp.int32)
        fc1_scales = jax.random.uniform(ks[3], (H // G, F), jnp.float32) * 0.02 + 0.001
        fc2_scales = jax.random.uniform(ks[4], (F // G, H), jnp.float32) * 0.02 + 0.001
        fc1_bias = jax.random.normal(ks[5], (F,), jnp.float32) * 0.02
        fc2_bias = jax.random.normal(ks[6], (H,), jnp.float32) * 0.02
        return {'x': x, 'ln_gamma': ln_gamma, 'ln_beta': ln_beta, 'fc1_q': fc1_q, 'fc1_scales': fc1_scales, 'fc1_bias': fc1_bias, 'fc2_q': fc2_q, 'fc2_scales': fc2_scales, 'fc2_bias': fc2_bias}
    _L0_ffn_all = _L0_ffn_setup()
    _L0_ffn_in = {k: v for k, v in _L0_ffn_all.items() if k in ('ln_gamma', 'ln_beta', 'fc1_q', 'fc1_scales', 'fc1_bias', 'fc2_q', 'fc2_scales', 'fc2_bias')}
    del _L0_ffn_all
    return {'x': x, 'x_txt': x_txt, 'L0_tok_W1': _L0_tok_in['W1'], 'L0_tok_b1': _L0_tok_in['b1'], 'L0_tok_W2': _L0_tok_in['W2'], 'L0_tok_b2': _L0_tok_in['b2'], 'L0_txt_emb_table': _L0_txt_in['emb_table'], 'L0_txt_proj_w': _L0_txt_in['proj_w'], 'L0_txt_proj_b': _L0_txt_in['proj_b'], 'L0_txt_window': _L0_txt_in['window'], 'L0_attn_W_in': _L0_attn_in['W_in'], 'L0_attn_b_in': _L0_attn_in['b_in'], 'L0_attn_short_w': _L0_attn_in['short_w'], 'L0_attn_short_b': _L0_attn_in['short_b'], 'L0_attn_W1': _L0_attn_in['W1'], 'L0_attn_b1': _L0_attn_in['b1'], 'L0_attn_f1': _L0_attn_in['f1'], 'L0_attn_W2': _L0_attn_in['W2'], 'L0_attn_b2': _L0_attn_in['b2'], 'L0_attn_f2': _L0_attn_in['f2'], 'L0_attn_W3': _L0_attn_in['W3'], 'L0_attn_b3': _L0_attn_in['b3'], 'L0_attn_filter_bias': _L0_attn_in['filter_bias'], 'L0_attn_W_out': _L0_attn_in['W_out'], 'L0_attn_b_out': _L0_attn_in['b_out'], 'L0_ffn_ln_gamma': _L0_ffn_in['ln_gamma'], 'L0_ffn_ln_beta': _L0_ffn_in['ln_beta'], 'L0_ffn_fc1_q': _L0_ffn_in['fc1_q'], 'L0_ffn_fc1_scales': _L0_ffn_in['fc1_scales'], 'L0_ffn_fc1_bias': _L0_ffn_in['fc1_bias'], 'L0_ffn_fc2_q': _L0_ffn_in['fc2_q'], 'L0_ffn_fc2_scales': _L0_ffn_in['fc2_scales'], 'L0_ffn_fc2_bias': _L0_ffn_in['fc2_bias']}

def reference(x, x_txt, L0_tok_W1, L0_tok_b1, L0_tok_W2, L0_tok_b2, L0_txt_emb_table, L0_txt_proj_w, L0_txt_proj_b, L0_txt_window, L0_attn_W_in, L0_attn_b_in, L0_attn_short_w, L0_attn_short_b, L0_attn_W1, L0_attn_b1, L0_attn_f1, L0_attn_W2, L0_attn_b2, L0_attn_f2, L0_attn_W3, L0_attn_b3, L0_attn_filter_bias, L0_attn_W_out, L0_attn_b_out, L0_ffn_ln_gamma, L0_ffn_ln_beta, L0_ffn_fc1_q, L0_ffn_fc1_scales, L0_ffn_fc1_bias, L0_ffn_fc2_q, L0_ffn_fc2_scales, L0_ffn_fc2_bias):
    import jax
    import jax.numpy as jnp

    def _L0_tok_ref(x, W1, b1, W2, b2):
        import jax, jax.numpy as jnp
        import numpy as np
        P = 16
        C = 3
        D = 256

        def _patchify(x, p):
            B, Cc, H, W = x.shape
            gh, gw = (H // p, W // p)
            x = x.reshape(B, Cc, gh, p, gw, p)
            x = x.transpose(0, 2, 4, 1, 3, 5)
            return x.reshape(B, gh * gw, Cc * p * p)
        patches = _patchify(x, P)
        h = jax.nn.silu(jnp.einsum('blk,kd->bld', patches, W1) + b1)
        return jnp.einsum('bld,de->ble', h, W2) + b2

    def _L0_txt_ref(input_ids, emb_table, proj_w, proj_b, window):
        import jax, jax.numpy as jnp
        import numpy as np
        N_FFT = 64
        HOP = 64
        NUM_FREQ = N_FFT // 2 + 1

        def _stft_mag(sig, window):
            L = sig.shape[1]
            pad = N_FFT // 2
            x = jnp.pad(sig, ((0, 0), (pad, pad)), mode='reflect')
            n_frames = 1 + L // HOP
            idx = jnp.arange(n_frames)[:, None] * HOP + jnp.arange(N_FFT)[None, :]
            frames = x[:, idx] * window
            spec = jnp.fft.rfft(frames, axis=-1)
            r, im = (spec.real, spec.imag)
            m2 = r * r + im * im
            mag = jnp.where(m2 == 0, 0.0, jnp.sqrt(jnp.where(m2 == 0, 1.0, m2)))
            return (mag, n_frames)

        def _linear_interp_last(feat, out_len):
            in_len = feat.shape[-1]
            coord = jnp.clip((jnp.arange(out_len) + 0.5) * (in_len / out_len) - 0.5, 0.0, in_len - 1.0)
            i0 = jnp.floor(coord).astype(jnp.int32)
            i1 = jnp.minimum(i0 + 1, in_len - 1)
            w = (coord - i0).astype(feat.dtype)
            return feat[..., i0] * (1.0 - w) + feat[..., i1] * w
        B, L = input_ids.shape
        V = emb_table.shape[0]
        word_embeds = emb_table[input_ids]
        sig = jax.nn.one_hot(input_ids, V, dtype=jnp.float32)
        sig = jnp.transpose(sig, (0, 2, 1)).reshape(B * V, L)
        mag, T = _stft_mag(sig, window)
        feat = mag.reshape(B, V, T, NUM_FREQ).transpose(0, 3, 1, 2)
        feat = feat.reshape(B, NUM_FREQ * V, T)
        up = _linear_interp_last(feat, L)
        stft_feat = jnp.transpose(up, (0, 2, 1))
        stft_enc = stft_feat @ proj_w.T + proj_b
        return jnp.concatenate([word_embeds, stft_enc], axis=-1)

    def _L0_attn_ref(x, W_in, b_in, short_w, short_b, W1, b1, f1, W2, b2, f2, W3, b3, filter_bias, W_out, b_out):
        import math
        import jax, jax.numpy as jnp
        import numpy as np
        B, L, D = (4, 1024, 256)
        HID, PE, SHORT = (64, 3, 3)
        WIDTH = 3 * D

        def _gen_filter(length, W1, b1, f1, W2, b2, f2, W3, b3):
            t = jnp.arange(length, dtype=jnp.float32) / (length - 1)
            ang = 2.0 * math.pi * jnp.arange(length, dtype=jnp.float32) / length
            phase = 0.0001 * ang
            pe = jnp.stack([t, jnp.cos(phase), -jnp.sin(phase)], axis=-1)
            h = jnp.sin((pe @ W1 + b1) * f1)
            h = jnp.sin((h @ W2 + b2) * f2)
            k = h @ W3 + b3
            dmax, dmin = (math.log(0.01) / 0.3, math.log(0.01) / 1.5)
            deltas = jnp.abs(jnp.linspace(dmax, dmin, D).astype(jnp.float32))
            return k * jnp.exp(-t[:, None] * deltas[None, :])

        def _causal_fft_conv(v, k, bias):
            length = v.shape[1]
            n = 2 * length
            vp = jnp.pad(v, ((0, 0), (length - 1, 0), (0, 0)))
            Vf = jnp.fft.rfft(vp, n=n, axis=1)
            Kf = jnp.fft.rfft(k, n=n, axis=0)
            out = jnp.fft.irfft(Vf * jnp.conj(Kf)[None], n=n, axis=1)[:, :length]
            return out + bias

        def _short_conv(u, w, b):
            length = u.shape[1]
            up = jnp.pad(u, ((0, 0), (2, 2), (0, 0)))
            out = up[:, 0:length] * w[:, 0] + up[:, 1:length + 1] * w[:, 1] + up[:, 2:length + 2] * w[:, 2]
            return out + b
        u = x @ W_in + b_in
        uc = _short_conv(u, short_w, short_b)
        x0, x1, v = jnp.split(uc, 3, axis=-1)
        v = v * x1
        k = _gen_filter(x.shape[1], W1, b1, f1, W2, b2, f2, W3, b3)
        v = _causal_fft_conv(v, k, filter_bias)
        y = v * x0
        return y @ W_out + b_out

    def _L0_ffn_ref(x, ln_gamma, ln_beta, fc1_q, fc1_scales, fc1_bias, fc2_q, fc2_scales, fc2_bias):
        import jax, jax.numpy as jnp
        import numpy as np
        B, S, H, F, G = (8, 512, 256, 1024, 128)
        EPS = 1e-05

        def _dequant(q, scales, g):
            K, N = q.shape
            w = (q.astype(jnp.float32) - 128.0).reshape(K // g, g, N) * scales[:, None, :]
            return w.reshape(K, N)
        residual = x
        mu = jnp.mean(x, axis=-1, keepdims=True)
        var = jnp.mean(jnp.square(x - mu), axis=-1, keepdims=True)
        h = (x - mu) * jax.lax.rsqrt(var + EPS) * ln_gamma + ln_beta
        hf = h.reshape(-1, H)
        w1 = _dequant(fc1_q, fc1_scales, G)
        y = hf @ w1 + fc1_bias
        y = jax.nn.silu(y)
        w2 = _dequant(fc2_q, fc2_scales, G)
        z = y @ w2 + fc2_bias
        return residual + 0.5 * z.reshape(residual.shape)
    h = _L0_tok_ref(x, L0_tok_W1, L0_tok_b1, L0_tok_W2, L0_tok_b2)
    h = jnp.concatenate([h, _L0_txt_ref(x_txt, L0_txt_emb_table, L0_txt_proj_w, L0_txt_proj_b, L0_txt_window)], axis=1)
    h = h + _L0_attn_ref(_layernorm(h, axis=-1), L0_attn_W_in, L0_attn_b_in, L0_attn_short_w, L0_attn_short_b, L0_attn_W1, L0_attn_b1, L0_attn_f1, L0_attn_W2, L0_attn_b2, L0_attn_f2, L0_attn_W3, L0_attn_b3, L0_attn_filter_bias, L0_attn_W_out, L0_attn_b_out)
    h = h + _L0_ffn_ref(_layernorm(h, axis=-1), L0_ffn_ln_gamma, L0_ffn_ln_beta, L0_ffn_fc1_q, L0_ffn_fc1_scales, L0_ffn_fc1_bias, L0_ffn_fc2_q, L0_ffn_fc2_scales, L0_ffn_fc2_bias)
    return h

_drawn_inputs = setup_inputs


def setup_inputs(seed=0):
    import zlib

    import numpy as np

    out = dict(_drawn_inputs(seed))
    spreads = {'L0_txt_proj_b': (0.0, 0.277),
     'L0_attn_b_in': (0.0, 0.281),
     'L0_attn_short_b': (0.0, 0.1),
     'L0_attn_b1': (0.0, 0.1),
     'L0_attn_b2': (0.0, 0.1),
     'L0_attn_b3': (0.0, 0.746),
     'L0_attn_filter_bias': (0.0, 0.587),
     'L0_attn_b_out': (0.0, 0.1),
     'L0_ffn_ln_gamma': (1.0, 0.2),
     'L0_ffn_ln_beta': (0.0, 0.1)}
    factors = {'L0_tok_b1': 8.0, 'L0_tok_b2': 3.451, 'L0_ffn_fc1_bias': 64.0, 'L0_ffn_fc2_bias': 64.0}
    for name, (base, spread) in spreads.items():
        noise = np.random.default_rng([zlib.crc32(name.encode()), seed]).standard_normal(out[name].shape)
        drawn = base * np.exp(spread * noise) if base else spread * noise
        out[name] = jnp.asarray(drawn.astype(out[name].dtype))
    for name, factor in factors.items():
        out[name] = (out[name] * factor).astype(out[name].dtype)
    return out
```

```python
from contextlib import ExitStack

import numpy as np

import concourse.bass as bass
from concourse import mybir

F32 = mybir.dt.float32
I32 = mybir.dt.int32
ALU = mybir.AluOpType
ACT = mybir.ActivationFunctionType

B = 8
NPATCH = 196
NTXT = 512
L = NPATCH + NTXT
D = 256
KP = 768
WID = 3 * D
HID = 64
FF = 1024
V = 64
DEMB = 179
DST = D - DEMB
NF = 64
FR = 1 + NTXT // NF
KF = NF // 2 + 1
T = 118
NT = L // T
NQ = 3
BL = L // NQ
ND = 2 * BL
CH = L // 2
RB = V + FR + 2
EPS = 1e-5
MAGIC = 1.5 * 2.0 ** 23
SIN_C = (6.28125, 0.0019350051879882812, 3.019916e-07)


def bc(ap, axis, n):
    ap = ap.unsqueeze(axis)
    shape = list(ap.shape)
    shape[axis] = n
    return ap.broadcast_to(shape)


class Semaphores:

    def __init__(self, sem):
        self.loads_text = sem("loads_text")
        self.loads_filter = sem("loads_filter")
        self.loads_mats = sem("loads_mats")
        self.loads_q1 = sem("loads_q1")
        self.loads_q2 = sem("loads_q2")
        self.rows_in = sem("rows_in")
        self.xp_in = sem("xp_in")
        self.ids_in = sem("ids_in")
        self.out_done = sem("out_done")
        self.memsets = sem("memsets")
        self.window_done = sem("window_done")
        self.onehot_frames = sem("onehot_frames")
        self.stft = sem("stft")
        self.squares = sem("squares")
        self.sums = sem("sums")
        self.roots = sem("roots")
        self.mags = sem("mags")
        self.enc_ready = sem("enc_ready")
        self.enc_done = sem("enc_done")
        self.fil_ready = sem("fil_ready")
        self.fil_steps = sem("fil_steps")
        self.reduced = sem("reduced")
        self.sin_done = sem("sin_done")
        self.kt_ready = sem("kt_ready")
        self.kt_done = sem("kt_done")
        self.kraw_ready = sem("kraw_ready")
        self.kraw_done = sem("kraw_done")
        self.kf_steps = sem("kf_steps")
        self.deq = sem("deq")
        self.gbias_done = sem("gbias_done")
        self.pwr_const = sem("pwr_const")
        self.h1_ready = sem("h1_ready")
        self.h1_done = sem("h1_done")
        self.onehot_done = sem("onehot_done")
        self.h_ready = sem("h_ready")
        self.h_done = sem("h_done")
        self.hb_done = sem("hb_done")
        self.st1_done = sem("st1_done")
        self.mv1_done = sem("mv1_done")
        self.va1_done = sem("va1_done")
        self.rs1_done = sem("rs1_done")
        self.ln1_done = sem("ln1_done")
        self.xt_ready = sem("xt_ready")
        self.xt_done = sem("xt_done")
        self.u_ready = sem("u_ready")
        self.u_first = sem("u_first")
        self.u_tap1 = sem("u_tap1")
        self.u_done = sem("u_done")
        self.u_edge = sem("u_edge")
        self.v_done = sem("v_done")
        self.vt_ready = sem("vt_ready")
        self.vt_done = sem("vt_done")
        self.vf_ready = sem("vf_ready")
        self.vf_done = sem("vf_done")
        self.pw_done = sem("pw_done")
        self.y_ready = sem("y_ready")
        self.y_done = sem("y_done")
        self.o_ready = sem("o_ready")
        self.h2_done = sem("h2_done")
        self.st2_done = sem("st2_done")
        self.mv2_done = sem("mv2_done")
        self.va2_done = sem("va2_done")
        self.rs2_done = sem("rs2_done")
        self.ln2_done = sem("ln2_done")
        self.r_done = sem("r_done")
        self.rb_done = sem("rb_done")
        self.res_done = sem("res_done")
        self.zt_ready = sem("zt_ready")
        self.zt_done = sem("zt_done")
        self.f1_ready = sem("f1_ready")
        self.f1_done = sem("f1_done")
        self.f2_ready = sem("f2_ready")
        self.ob_done = sem("ob_done")


def program(nc, a, out):
    with ExitStack() as ctx:
        def sb(name, shape, dt=F32):
            return ctx.enter_context(nc.sbuf_tensor(name, shape, dt))

        def sem(name):
            return ctx.enter_context(nc.semaphore(name))

        bk = ctx.enter_context(nc.psum_tensor("banks", [128, 8, 512], F32))

        ident = sb("ident", [128, 128])
        w1 = sb("w1", [128, KP // 128, D])
        b1 = sb("b1", [128, 2])
        w2 = sb("w2", [128, 2, D])
        win = sb("win", [128, 2, WID])
        gate = sb("gate", [128, 6, 5])
        gbias = sb("gbias", [128, 6, 3])
        fbias = sb("fbias", [128, 2])
        wout = sb("wout", [128, 2, D])
        bout = sb("bout", [T, D])
        gamma = sb("gamma", [128, 2])
        beta = sb("beta", [128, 2])
        fc1 = sb("fc1", [128, 2, FF])
        fb1 = sb("fb1", [128, 8])
        fc2 = sb("fc2", [128, 8, D])
        fb2 = sb("fb2", [T, D])
        dft = sb("dft", [T, 2, 4, T])
        idft = sb("idft", [T, 4, BL])
        sgn = sb("sgn", [T, 2])
        kf = sb("kf", [T, 2, NQ, 3, D])
        rowb = sb("rowb", [RB, B, D])
        iotap = sb("iotap", [V, 1])
        mhalf = sb("mhalf", [T, 12])

        xp = sb("xp", [128, KP // 128, NPATCH])
        ids = sb("ids", [V, NTXT], I32)
        h1t = sb("h1t", [128, 2, 2 * T])
        oht = sb("oht", [RB, L])
        h = sb("h", [T, NT, D])
        hb_all = sb("hb", [128, NT * D])
        ln = sb("ln", [T, NT, D])
        xt = sb("xt", [128, 2, L + 2])
        uc_all = sb("uc", [128, 6 * L])
        vy = sb("vy", [128, 2 * NQ * D])
        vf = sb("vf", [T, 2, 2, NQ, D])
        xf_all = sb("xf", [128, 4 * NQ * D])
        ta = sb("ta", [T, 2, NQ, D])
        tb = sb("tb", [T, 2, 2, D])
        h2 = sb("h2", [T, NT, D])
        res = sb("res", [T, NT, D])
        zt = sb("zt", [128, 2, L])
        at = sb("at", [128, 8, L])
        ob = sb("ob", [T, NT, D])
        st = sb("st", [T, NT, 6])
        dif = sb("dif", [T, NT, 2])
        mv1 = sb("mv1", [T, NT, 2])
        va1 = sb("va1", [T, NT])
        rs1 = sb("rs1", [T, NT])
        mv2 = sb("mv2", [T, NT, 2])
        va2 = sb("va2", [T, 2, NT])
        rs2 = sb("rs2", [T, 2, NT])

        vt = vy[0:T, :].rearrange("p (r q c) -> p r q c", r=2, q=NQ)
        yt = vy[:, 0:2 * L].rearrange("p (h t) -> p h t", h=2)

        hb = hb_all[0:T, :].rearrange("p (t c) -> p t c", t=NT)
        uc = uc_all[:, :].rearrange("p (m t) -> p m t", m=6)
        xf = xf_all[0:T, :].rearrange("p (j r q c) -> p j r q c", j=2, r=2, q=NQ)

        iotar = sb("iotar", [NF, V])
        dftw = sb("dftw", [NF, 2 * KF])
        wnd = sb("wnd", [NF, 1])
        fw1 = sb("fw1", [4, HID])
        fw2 = sb("fw2", [HID + 1, HID])
        fw3 = ln[0:HID + 1, 1, :]
        ffreq = sb("ffreq", [HID, 2])
        enc = ln[0:36, :, :].rearrange("p t c -> p (t c)")[:, 0:2 * DST].rearrange("p (g o) -> p g o", g=2)
        at_all = at[:, :, :].rearrange("p a t -> p (a t)")
        ohf = at_all[0:NF, 0:FR * B * V].rearrange("p (f v) -> p f v", v=V)
        quant = at_all[:, 0:2 * FF].bitcast(I32)
        scale = at_all[:, 2 * FF:4 * FF]
        idf = ids[:, 0:FR * B]
        sqv = uc_all[:, 0:36 * 2 * KF].rearrange("p (g k) -> p g k", g=36)
        mag = hb_all[:, 0:36 * KF].rearrange("p (g k) -> p g k", g=36)
        root, inv = sqv[:, :, 0:KF], sqv[:, :, KF:2 * KF]
        proj = xf_all[:, 0:KF * DST].rearrange("p (k o) -> p k o", k=KF)
        pet = h2[0:4, :, :].rearrange("p t c -> p (t c)")[:, 0:L]
        fh1, fh2 = zt[0:HID + 1, 0, :], zt[0:HID + 1, 1, :]
        ob_all = ob[:, :, :].rearrange("p t c -> p (t c)")
        ang = ob_all[0:HID, 0:L].rearrange("p (c t) -> p c t", c=2)
        turns = ob_all[0:HID, L:2 * L].rearrange("p (c t) -> p c t", c=2)
        decay = res[:, :, :]
        krt = vt

        text_loads = [(idf, a["ids_frames"]), (iotar[:], a["iota_row"]), (dftw[:], a["stft_mat"]),
                      (wnd[:], a["window"]), (iotap[:], a["iota_col"]), (ident[:], a["ident"]),
                      (proj[0:V], a["proj"]), (proj[V:2 * V], a["proj"])]
        filter_loads = [(pet, a["features"]), (fw1[0:3, :], a["L0_attn_W1"]), (fw1[3:4, :], a["f_b1"]),
                        (ffreq[:, 0:1], a["f_f1"]), (ffreq[:, 1:2], a["f_f2"]),
                        (fw2[0:HID, :], a["L0_attn_W2"]), (fw2[HID:HID + 1, :], a["f_b2"]),
                        (fw3[0:HID, :], a["L0_attn_W3"]), (fw3[HID:HID + 1, :], a["f_b3"]),
                        (decay, a["decay"]), (dft[:], a["dft"]), (sgn[:], a["signs"])]
        mat_loads = [(w1[:], a["w1"]), (b1[:], a["b1"]), (w2[:], a["w2"]), (win[:], a["win"]),
                     (gate[:], a["gate"]), (fbias[:], a["fbias"]), (idft[:], a["idft"]), (wout[:], a["wout"]),
                     (bout[:], a["bout"].partition_broadcast(T)), (gamma[:], a["gamma"]), (beta[:], a["beta"]),
                     (fb1[:], a["fb1"]), (fb2[:], a["fb2"].partition_broadcast(T))]
        TEXT, FILTER, MATS = 16 * len(text_loads), 16 * len(filter_loads), 16 * len(mat_loads)

        s = Semaphores(sem)
        block = ctx.enter_context(nc.Block())
        out_v = out.rearrange("b (t p) c -> b p t c", p=T)

        @block.sync
        def _(sp):
            for dst, src in text_loads:
                sp.dma_start(dst, src).then_inc(s.loads_text, 16)
            for dst, src in filter_loads:
                sp.dma_start(dst, src).then_inc(s.loads_filter, 16)
            sp.dma_start(xp[:], a["x"][0]).then_inc(s.xp_in, 16)
            for dst, src in mat_loads:
                sp.dma_start(dst, src).then_inc(s.loads_mats, 16)
            sp.wait_ge(s.memsets, 2)
            for b in range(B):
                sp.dma_start(rowb[0:V, b, 0:DEMB], a["table"]).then_inc(s.rows_in, 16)
            sp.dma_start(rowb[V + FR:V + FR + 1, :, DEMB:D], a["proj_bias"]).then_inc(s.rows_in, 16)
            sp.dma_start(rowb[V + FR + 1:RB, :, :], a["tok_bias"]).then_inc(s.rows_in, 16)
            sp.dma_start(oht[V:RB, :], a["interp"]).then_inc(s.rows_in, 16)
            sp.wait_ge(s.onehot_frames, 1)
            sp.dma_start(ids[:], a["ids"][0]).then_inc(s.ids_in, 16)
            sp.wait_ge(s.stft, 6)
            sp.dma_start(quant, a["fc1_q"]).then_inc(s.loads_q1, 16)
            sp.dma_start(scale, a["fc1_scales"].partition_broadcast(128)).then_inc(s.loads_q1, 16)
            sp.wait_ge(s.enc_done, 2)
            for bb in range(4):
                sp.dma_start(rowb[V:V + FR, bb::4, DEMB:D],
                             enc[FR * bb:FR * bb + FR, :, :]).then_inc(s.rows_in, 16)
            sp.wait_ge(s.deq, 1)
            sp.dma_start(quant, a["fc2_q"]).then_inc(s.loads_q2, 16)
            sp.dma_start(scale, a["fc2_scales"].partition_broadcast(128)).then_inc(s.loads_q2, 16)

            def step(i, front, back):
                if back:
                    c = i - 1
                    for j in range(3):
                        sp.wait_ge(s.ob_done, 3 * c + j + 1)
                        sp.dma_start(out_v[c, :, 2 * j:2 * j + 2, :] if isinstance(c, int)
                                     else out_v[bass.ds(c, 1), :, 2 * j:2 * j + 2, :].rearrange("b p t c -> (b p) t c"),
                                     ob[:, 2 * j:2 * j + 2, :]).then_inc(s.out_done, 16)

            def prefetch(i):
                sp.wait_ge(s.h1_ready, 2 * i + 2)
                n = i + 1
                sp.dma_start(xp[:], a["x"][n] if isinstance(n, int) else
                             a["x"][bass.ds(n, 1)].rearrange("b p k t -> (b p) k t")).then_inc(s.xp_in, 16)
                sp.wait_ge(s.onehot_done, i + 1)
                sp.dma_start(ids[:], a["ids"][n] if isinstance(n, int) else
                             a["ids"][bass.ds(n, 1)].rearrange("b p t -> (b p) t")).then_inc(s.ids_in, 16)

            prefetch(0)
            with sp.Fori(1, B - 1) as i:
                prefetch(i)
                step(i, True, True)
            step(B - 1, True, True)
            step(B, False, True)
            sp.wait_ge(s.out_done, 16 * 3 * B)

        @block.tensor
        def _(pe):
            mm = nc.tensor.matmul

            def spectrum(ready, copied, i):
                for n in range(6):
                    j, part = n // 3, n % 3
                    if n >= 4:
                        pe.wait_ge(copied, 6 * i + n - 3)
                    bank = bk[0:T, (2 + n) % 4, :]
                    pieces = [(part, bank, 0, 2)] if part < 2 else [(0, bank[:, 0:D], 2, 3), (1, bank[:, D:2 * D], 2, 3)]
                    for p, dst, q0, q1 in pieces:
                        for r in range(2):
                            o = mm(dst, dft[:, r, 2 * j + p, :], vt[:, r, q0:q1, :].rearrange("p q c -> p (q c)"),
                                   start=(r == 0), stop=(r == 1))
                    o.then_inc(ready, 1)

            pe.wait_ge(s.loads_filter, FILTER)
            for c in range(2):
                mm(bk[0:HID, c, 0:CH], fw1[:], pet[:, c * CH:(c + 1) * CH], start=True, stop=True
                   ).then_inc(s.fil_ready, 1)
            for c in range(2):
                pe.wait_ge(s.sin_done, c + 1)
                mm(bk[0:HID, 2 + c, 0:CH], fw2[:], fh1[:, c * CH:(c + 1) * CH], start=True, stop=True
                   ).then_inc(s.fil_ready, 1)
            for t in range(NT):
                pe.wait_ge(s.sin_done, 3 + t // 3)
                mm(bk[0:T, 4 + t // 2, (t % 2) * D:(t % 2 + 1) * D], fh2[:, t * T:(t + 1) * T], fw3,
                   start=True, stop=True).then_inc(s.kt_ready, 1)

            pe.wait_ge(s.onehot_frames, 1)
            pe.wait_ge(s.window_done, 1)
            for g in range(6):
                bank = (0, 1, 2, 3, 7, 0)[g]
                if g == 0:
                    pe.wait_ge(s.fil_steps, 20)
                if g == 5:
                    pe.wait_ge(s.squares, 1)
                for j in range(6):
                    jj = 6 * g + j
                    m = mm(bk[:, bank, j * 2 * KF:(j + 1) * 2 * KF], at_all[0:NF, jj * 128:(jj + 1) * 128], dftw[:],
                           start=True, stop=True)
                m.then_inc(s.stft, 1)

            pe.wait_ge(s.kt_done, 3)
            pe.wait_ge(s.squares, 6)
            spectrum(s.kraw_ready, s.kraw_done, 0)

            pe.wait_ge(s.mags, 4)
            pe.wait_ge(s.kraw_done, 6)
            for k in range(KF):
                for g in range(2):
                    m = mm(bk[0:36, g, 0:DST], mag[V * g:V * g + V, :, k], proj[V * g:V * g + V, k, :],
                           start=(k == 0), stop=(k == KF - 1))
                    if k == KF - 1:
                        m.then_inc(s.enc_ready, 1)

            pe.wait_ge(s.loads_mats, MATS)
            pe.wait_ge(s.loads_text, TEXT)
            pe.wait_ge(s.enc_done, 2)
            pe.wait_ge(s.rows_in, 16 * (B + 7))

            def patches_up(i):
                pe.wait_ge(s.xp_in, 16 * i + 16)
                pe.wait_ge(s.h2_done, 3 * i)
                for m in range(2):
                    for k in range(KP // 128):
                        o = mm(bk[:, 0, m * NPATCH:(m + 1) * NPATCH], w1[:, k, m * 128:(m + 1) * 128], xp[:, k, :],
                               start=(k == 0), stop=(k == KP // 128 - 1))
                    o.then_inc(s.h1_ready, 1)

            def rows(i):
                pe.wait_ge(s.onehot_done, i + 1)
                for t in range(NT):
                    dst = bk[0:T, 1 + t // 2, (t % 2) * D:(t % 2 + 1) * D]
                    if t == 0:
                        pe.wait_ge(s.h1_done, 2 * i + 2)
                    rhs = rowb[:, i, :] if isinstance(i, int) else \
                        rowb[:, bass.ds(i, 1), :].rearrange("p b c -> p (b c)")
                    o = mm(dst, oht[:, t * T:(t + 1) * T], rhs, start=True, stop=(t > 1))
                    for k in range(2 if t < 2 else 0):
                        o = mm(dst, h1t[:, k, t * T:(t + 1) * T], w2[:, k, :], start=False, stop=(k == 1))
                    if t % 2:
                        o.then_inc(s.h_ready, 1)

            def turn_pair(j, bank):
                for t in range(2):
                    for k in range(2):
                        o = nc.tensor.transpose(bk[:, bank, k * BL + t * T:k * BL + (t + 1) * T],
                                                ln[:, 2 * j + t, k * 128:(k + 1) * 128], ident[0:T, 0:T])
                return o

            def turn_front(i):
                for j in range(3):
                    pe.wait_ge(s.ln1_done, 6 * i + 2 * j + 2)
                    if j:
                        pe.wait_ge(s.h_done, 3 * i + j)
                    turn_pair(j, j).then_inc(s.xt_ready, 1)

            def gates(i):
                for u in range(12):
                    c, m = u // 6, (4, 5, 2, 3, 0, 1)[u % 6]
                    pe.wait_ge(s.xt_done, 3 * i + 2 + c)
                    if u == 0:
                        pe.wait_ge(s.h_done, 3 * i + 3)
                    if u == 3:
                        pe.wait_ge(s.xt_done, 3 * i + 3)
                    if u >= 4:
                        pe.wait_ge(s.u_done, 12 * i + u - 3)
                    for k in range(2):
                        o = mm(bk[:, (3 + u) % 4, 0:CH + 2], win[:, k, m * 128:(m + 1) * 128],
                               xt[:, k, c * CH:c * CH + CH + 2], start=(k == 0), stop=(k == 1))
                    o.then_inc(s.u_ready, 1)

            def turn_v(i):
                for q in range(NQ):
                    pe.wait_ge(s.v_done, 2 * i + 1 + (q > 0))
                    pe.wait_ge(s.u_done, 12 * i + 9 + q)
                    for r in range(2):
                        for k in range(2):
                            t = 2 * q + r
                            o = nc.tensor.transpose(bk[0:T, (3 + q) % 4, r * D + k * 128:r * D + (k + 1) * 128],
                                                    uc[:, 4 + k, t * T:(t + 1) * T], ident[:])
                    o.then_inc(s.vt_ready, 1)

            def inverse(i):
                pe.wait_ge(s.pw_done, 22 * i + 22)
                for q in range(NQ):
                    for k in range(2):
                        for f in range(4):
                            o = mm(bk[:, q, k * BL:(k + 1) * BL], xf[:, f // 2, f % 2, q, k * 128:(k + 1) * 128],
                                   idft[:, f, :], start=(f == 0), stop=(f == 3))
                    o.then_inc(s.y_ready, 1)

            def output(i):
                for j in range(3):
                    pe.wait_ge(s.y_done, 6 * i + 2 * j + 2)
                    for t in (2 * j, 2 * j + 1):
                        for k in range(2):
                            o = mm(bk[0:T, (3 + j) % 4, (t % 2) * D:(t % 2 + 1) * D],
                                   yt[:, k, t * T:(t + 1) * T], wout[:, k, :], start=(k == 0), stop=(k == 1))
                    o.then_inc(s.o_ready, 1)

            def turn_back(c):
                pe.wait_ge(s.ob_done, 3 * c)
                pe.wait_ge(s.f1_done, 16 * c)
                for j in range(3):
                    pe.wait_ge(s.ln2_done, 6 * c + 2 * j + 2)
                    turn_pair(j, 4 + j).then_inc(s.zt_ready, 1)

            def up(c, lo, hi):
                for u in range(lo, hi):
                    ch, m = u // 8, u % 8
                    pe.wait_ge(s.zt_done, 6 * c + 4 if ch == 0 else 6 * c + 6)
                    if u == 3:
                        pe.wait_ge(s.zt_done, 6 * c + 6)
                    if u >= 4:
                        pe.wait_ge(s.f1_done, 16 * c + u - 3)
                    for k in range(2):
                        o = mm(bk[:, 4 + (3 + u) % 4, 0:CH], fc1[:, k, m * 128:(m + 1) * 128],
                               zt[:, k, ch * CH:(ch + 1) * CH], start=(k == 0), stop=(k == 1))
                    o.then_inc(s.f1_ready, 1)

            def down(c):
                pe.wait_ge(s.f1_done, 16 * c + 16)
                for j in range(3):
                    for t in (2 * j, 2 * j + 1):
                        for k in range(8):
                            o = mm(bk[0:T, 4 + (3 + j) % 4, (t % 2) * D:(t % 2 + 1) * D],
                                   at[:, k, t * T:(t + 1) * T], fc2[:, k, :], start=(k == 0), stop=(k == 7))
                    o.then_inc(s.f2_ready, 1)

            def step(i, front, back):
                c = i - 1
                if front:
                    patches_up(i)
                    rows(i)
                if back:
                    turn_back(c)
                    up(c, 0, 10)
                if front:
                    turn_front(i)
                    gates(i)
                if back:
                    up(c, 10, 12)
                if front:
                    turn_v(i)
                if back:
                    up(c, 12, 14)
                if front:
                    pe.wait_ge(s.vt_done, 3 * i + 3)
                    pe.wait_ge(s.u_done, 12 * i + 12)
                    spectrum(s.vf_ready, s.vf_done, i)
                if back:
                    up(c, 14, 16)
                    down(c)
                if front:
                    inverse(i)
                    output(i)

            step(0, True, False)
            pe.wait_ge(s.deq, 2)
            step(1, True, True)
            with pe.Fori(2, B) as i:
                step(i, True, True)
            step(B, False, True)

        @block.scalar
        def _(act):
            A = nc.scalar.activation

            def spectrum_out(n, done):
                j, part = n // 3, n % 3
                bank = bk[0:T, (2 + n) % 4, :].rearrange("p (x c) -> p x c", x=2)
                A(vf[:, j, part, 0:2, :] if part < 2 else vf[:, j, :, 2, :], bank, ACT.Copy).then_inc(done, 1)

            act.wait_ge(s.loads_filter, FILTER)
            for c in range(4):
                act.wait_ge(s.fil_steps, 5 * c + 5)
                A((fh1 if c < 2 else fh2)[0:HID, (c % 2) * CH:(c % 2 + 1) * CH], ang[:, c % 2, :], ACT.Sin
                  ).then_inc(s.sin_done, 1)
            for g in range(6):
                act.wait_ge(s.stft, g + 1)
                A(sqv[:, 6 * g:6 * g + 6, :], bk[:, (0, 1, 2, 3, 7, 0)[g], 0:12 * KF].rearrange("p (g k) -> p g k", g=6),
                  ACT.Square
                  ).then_inc(s.squares, 1)
            act.wait_ge(s.sums, 1)
            A(root, mag, ACT.Sqrt).then_inc(s.roots, 1)
            for n in range(6):
                act.wait_ge(s.kraw_ready, n + 1)
                spectrum_out(n, s.kraw_done)
            for g in range(2):
                act.wait_ge(s.enc_ready, 2)
                A(enc[:, g, :], bk[0:36, g, 0:DST], ACT.Copy).then_inc(s.enc_done, 1)
            act.wait_ge(s.loads_mats, MATS)
            act.wait_ge(s.gbias_done, 5)

            def step(i, front, back):
                c = i - 1
                if front:
                    act.wait_ge(s.h_ready, 3 * i)
                    for m in range(2):
                        act.wait_ge(s.h1_ready, 2 * i + 2)
                        A(h1t[:, m, 0:NPATCH], bk[:, 0, m * NPATCH:(m + 1) * NPATCH], ACT.Silu, bias=b1[:, m:m + 1]
                          ).then_inc(s.h1_done, 1)
                    act.wait_ge(s.ln1_done, 6 * i)
                    act.wait_ge(s.hb_done, i)
                    for j in range(3):
                        act.wait_ge(s.h_ready, 3 * i + j + 1)
                        A(h[:, 2 * j:2 * j + 2, :], bk[0:T, 1 + j, :], ACT.Copy).then_inc(s.h_done, 1)
                if back:
                    act.wait_ge(s.f1_ready, 16 * c)
                    for j in range(3):
                        act.wait_ge(s.zt_ready, 3 * c + j + 1)
                        for k in range(2):
                            A(zt[:, k, j * BL:(j + 1) * BL], bk[:, 4 + j, k * BL:(k + 1) * BL], ACT.Identity,
                              scale=gamma[:, k:k + 1], bias=beta[:, k:k + 1]).then_inc(s.zt_done, 1)
                    act.wait_ge(s.f2_ready, 3 * c)

                def silu(lo, hi):
                    for u in range(lo, hi):
                        ch, m = u // 8, u % 8
                        act.wait_ge(s.f1_ready, 16 * c + u + 1)
                        A(at[:, m, ch * CH:(ch + 1) * CH], bk[:, 4 + (3 + u) % 4, 0:CH], ACT.Silu,
                          bias=fb1[:, m:m + 1]).then_inc(s.f1_done, 1)

                if back:
                    silu(0, 10)
                if front:
                    act.wait_ge(s.u_ready, 12 * i)
                    for j in range(3):
                        act.wait_ge(s.xt_ready, 3 * i + j + 1)
                        A(xt[:, :, 2 + j * BL:2 + (j + 1) * BL],
                          bk[:, j, 0:2 * BL].rearrange("p (k t) -> p k t", k=2), ACT.Copy).then_inc(s.xt_done, 1)
                    act.wait_ge(s.y_done, 6 * i)
                    for u in range(12):
                        ch, m = u // 6, (4, 5, 2, 3, 0, 1)[u % 6]
                        act.wait_ge(s.u_ready, 12 * i + u + 1)
                        A(uc[:, m, ch * CH:(ch + 1) * CH], bk[:, (3 + u) % 4, 2:CH + 2], ACT.Identity,
                          scale=gate[:, m, 3:4], bias=gbias[:, m, 0:1]).then_inc(s.u_first, 1)
                if back:
                    silu(10, 12)
                if front:
                    act.wait_ge(s.o_ready, 3 * i)
                    for q in range(NQ):
                        act.wait_ge(s.vt_ready, 3 * i + q + 1)
                        A(vt[:, :, q, :], bk[0:T, (3 + q) % 4, :].rearrange("p (r c) -> p r c", r=2), ACT.Copy
                          ).then_inc(s.vt_done, 1)
                if back:
                    silu(12, 14)
                if front:
                    act.wait_ge(s.pw_done, 22 * i)
                    for n in range(6):
                        act.wait_ge(s.vf_ready, 6 * i + n + 1)
                        spectrum_out(n, s.vf_done)
                if back:
                    silu(14, 16)

            step(0, True, False)
            step(1, True, True)
            with act.Fori(2, B) as i:
                step(i, True, True)
            step(B, False, True)

        @block.vector
        def _(dve):
            v = nc.vector
            v.memset(rowb[:], 0.0).then_inc(s.memsets, 1)
            v.memset(oht[:], 0.0).then_inc(s.memsets, 1)
            v.memset(h1t[:, :, NPATCH:2 * T], 0.0).then_inc(s.memsets, 1)
            v.memset(xt[:, :, 0:2], 0.0).then_inc(s.memsets, 1)
            v.memset(fh1, 1.0).then_inc(s.memsets, 1)
            v.memset(fh2, 1.0).then_inc(s.memsets, 1)

            dve.wait_ge(s.loads_text, TEXT)
            v.tensor_tensor(ohf, bc(idf, 2, V), bc(iotar[:], 1, FR * B), ALU.is_equal).then_inc(s.onehot_frames, 1)
            v.tensor_scalar(dftw[:], dftw[:], wnd[:, 0:1], None, ALU.mult).then_inc(s.window_done, 1)

            dve.wait_ge(s.loads_filter, FILTER)
            dve.wait_ge(s.memsets, 6)
            for c in range(4):
                dve.wait_ge(s.fil_ready, c + 1)
                x, n = ang[:, c % 2, :], turns[:, c % 2, :]
                if c >= 2:
                    dve.wait_ge(s.sin_done, c - 1)
                v.tensor_scalar(x, bk[0:HID, c, 0:CH], ffreq[:, c // 2:c // 2 + 1], None, ALU.mult
                                ).then_inc(s.fil_steps, 1)
                dve.wait_ge(s.fil_steps, 5 * c + 1)
                v.tensor_scalar(n, x, 1.0 / (2.0 * np.pi), MAGIC, ALU.mult, ALU.add).then_inc(s.fil_steps, 1)
                dve.wait_ge(s.fil_steps, 5 * c + 2)
                v.tensor_scalar(n, n, MAGIC, None, ALU.subtract).then_inc(s.fil_steps, 1)
                dve.wait_ge(s.fil_steps, 5 * c + 3)
                for p in range(2):
                    v.scalar_tensor_tensor(out=x, in0=n, scalar=-SIN_C[p], in1=x, op0=ALU.mult, op1=ALU.add
                                           ).then_inc(s.kf_steps, 1)
                    dve.wait_ge(s.kf_steps, 3 * c + p + 1)
                v.scalar_tensor_tensor(out=x, in0=n, scalar=-SIN_C[2], in1=x, op0=ALU.mult, op1=ALU.add
                                       ).then_inc(s.kf_steps, 1)
                dve.wait_ge(s.kf_steps, 3 * c + 3)
                v.tensor_scalar(x, x, float(np.float32(3.1415925)), -float(np.float32(3.1415925)), ALU.min, ALU.max
                                ).then_inc(s.fil_steps, 2)
            for j in range(3):
                dve.wait_ge(s.kt_ready, 2 * j + 2)
                v.tensor_tensor(krt[:, :, j, :], bk[0:T, 4 + j, :].rearrange("p (r c) -> p r c", r=2),
                                decay[:, 2 * j:2 * j + 2, :], ALU.mult).then_inc(s.kt_done, 1)
            dve.wait_ge(s.squares, 6)
            v.tensor_tensor(mag, sqv[:, :, 0:KF], sqv[:, :, KF:2 * KF], ALU.add).then_inc(s.sums, 1)
            dve.wait_ge(s.roots, 1)
            v.tensor_scalar(inv, root, 1e-30, None, ALU.max).then_inc(s.mags, 1)
            dve.wait_ge(s.mags, 1)
            v.reciprocal(inv, inv).then_inc(s.mags, 1)
            dve.wait_ge(s.mags, 2)
            v.scalar_tensor_tensor(out=inv, in0=mag, scalar=0.5, in1=inv, op0=ALU.mult, op1=ALU.mult
                                   ).then_inc(s.mags, 1)
            dve.wait_ge(s.mags, 3)
            v.scalar_tensor_tensor(out=mag, in0=root, scalar=0.5, in1=inv, op0=ALU.mult, op1=ALU.add
                                   ).then_inc(s.mags, 1)
            dve.wait_ge(s.kraw_done, 6)
            KS = 12
            for j in range(2):
                re, im = vf[:, j, 0], vf[:, j, 1]
                v.tensor_copy(kf[:, j, 0, 1, :], re[:, 0, :]).then_inc(s.kf_steps, 1)
                v.tensor_copy(kf[:, j, 0, 2, :], im[:, 0, :]).then_inc(s.kf_steps, 1)
                v.tensor_scalar(kf[:, j, 0, 0, :], im[:, 0, :], -1.0, None, ALU.mult).then_inc(s.kf_steps, 1)
                for d in (1, 2):
                    v.scalar_tensor_tensor(out=kf[:, j, d, 1, :], in0=im[:, d - 1, :], scalar=sgn[:, 1:2],
                                           in1=re[:, d, :], op0=ALU.mult, op1=ALU.add).then_inc(s.kf_steps, 1)
                    v.scalar_tensor_tensor(out=kf[:, j, d, 2, :], in0=re[:, d - 1, :], scalar=sgn[:, 0:1],
                                           in1=im[:, d, :], op0=ALU.mult, op1=ALU.add).then_inc(s.kf_steps, 1)
                    KS += 2
                KS += 3
            dve.wait_ge(s.kf_steps, KS)
            for j in range(2):
                v.tensor_scalar(kf[:, j, 1:3, 0, :], kf[:, j, 1:3, 2, :], -1.0, None, ALU.mult
                                ).then_inc(s.kf_steps, 1)
            KS += 2
            dve.wait_ge(s.loads_mats, MATS)
            G = lambda n: gate[:, :, n:n + 1]
            v.tensor_tensor(gbias[:, :, 1:2], G(1), G(2), ALU.add).then_inc(s.gbias_done, 1)
            dve.wait_ge(s.gbias_done, 1)
            v.tensor_tensor(gbias[:, :, 0:1], gbias[:, :, 1:2], G(3), ALU.add).then_inc(s.gbias_done, 1)
            dve.wait_ge(s.gbias_done, 2)
            v.tensor_tensor(gbias[:, :, 0:1], gbias[:, :, 0:1], G(0), ALU.mult).then_inc(s.gbias_done, 1)
            v.tensor_tensor(gbias[:, :, 1:2], gbias[:, :, 1:2], G(0), ALU.mult).then_inc(s.gbias_done, 1)
            dve.wait_ge(s.gbias_done, 4)
            v.tensor_tensor(gbias[:, :, 0:1], gbias[:, :, 0:1], G(4), ALU.add).then_inc(s.gbias_done, 1)
            v.tensor_tensor(gbias[:, :, 2:3], G(1), G(0), ALU.mult).then_inc(s.gbias_done, 1)
            for n, w in enumerate((fc1, fc2)):
                dve.wait_ge(s.loads_q1 if n == 0 else s.loads_q2, 32)
                v.scalar_tensor_tensor(out=w[:, :, :].rearrange("p a n -> p (a n)"), in0=quant, scalar=-128.0,
                                       in1=scale, op0=ALU.add, op1=ALU.mult).then_inc(s.deq, 1)
            v.memset(mhalf[:], -0.5).then_inc(s.pwr_const, 1)
            v.tensor_scalar(fb2[:], fb2[:], 0.5, None, ALU.mult).then_inc(s.pwr_const, 1)
            dve.wait_ge(s.gbias_done, 6)
            dve.wait_ge(s.kf_steps, KS)
            dve.wait_ge(s.deq, 2)

            def onehot(i):
                dve.wait_ge(s.ids_in, 16 * i + 16)
                dve.wait_ge(s.h_ready, 3 * i)
                v.tensor_scalar(oht[0:V, NPATCH:L], ids[:], iotap[:, 0:1], None, ALU.is_equal
                                ).then_inc(s.onehot_done, 1)

            def statistics(i, src, mv, rows_done, mv_done):
                for t in range(NT):
                    v.bn_stats(st[:, t, :], src[:, t, :]).then_inc(rows_done, 1)
                dve.wait_ge(rows_done, 6 * i + 6)
                v.tensor_tensor(mv[:, :, 0], st[:, :, 1], st[:, :, 4], ALU.add).then_inc(mv_done, 1)
                v.tensor_tensor(dif[:, :, 0], st[:, :, 1], st[:, :, 4], ALU.subtract).then_inc(mv_done, 1)
                v.tensor_tensor(dif[:, :, 1], st[:, :, 2], st[:, :, 5], ALU.add).then_inc(mv_done, 1)
                dve.wait_ge(mv_done, 6 * i + 3)
                v.tensor_scalar(mv[:, :, 0], mv[:, :, 0], 0.5, None, ALU.mult).then_inc(mv_done, 1)
                v.scalar_tensor_tensor(out=dif[:, :, 0], in0=dif[:, :, 0], scalar=0.25, in1=dif[:, :, 0],
                                       op0=ALU.mult, op1=ALU.mult).then_inc(mv_done, 1)
                dve.wait_ge(mv_done, 6 * i + 5)
                v.scalar_tensor_tensor(out=mv[:, :, 1], in0=dif[:, :, 1], scalar=1.0 / D, in1=dif[:, :, 0],
                                       op0=ALU.mult, op1=ALU.add).then_inc(mv_done, 1)
                dve.wait_ge(mv_done, 6 * i + 6)

            def norm2(c):
                dve.wait_ge(s.h2_done, 3 * c + 3)
                dve.wait_ge(s.res_done, c)
                statistics(c, h2, mv2, s.st2_done, s.mv2_done)
                v.tensor_scalar(va2[:, 0, :], mv2[:, :, 1], EPS, None, ALU.add).then_inc(s.va2_done, 1)
                v.tensor_scalar(va2[:, 1, :], mv2[:, :, 1], 1.0 + EPS, EPS * EPS, ALU.mult, ALU.add
                                ).then_inc(s.va2_done, 1)

            def apply2(c):
                dve.wait_ge(s.rs2_done, c + 1)
                dve.wait_ge(s.xt_ready, 3 * c + 3)
                for t in range(NT):
                    v.tensor_scalar(ln[:, t, :], h2[:, t, :], mv2[:, t, 0:1], rs2[:, 1, t:t + 1],
                                    ALU.subtract, ALU.mult).then_inc(s.ln2_done, 1)

            def norm1(i):
                dve.wait_ge(s.h_done, 3 * i + 3)
                statistics(i, h, mv1, s.st1_done, s.mv1_done)
                v.tensor_scalar(va1[:], mv1[:, :, 1], EPS, None, ALU.add).then_inc(s.va1_done, 1)

            def apply1(i):
                dve.wait_ge(s.rs1_done, i + 1)
                dve.wait_ge(s.zt_ready, 3 * i)
                dve.wait_ge(s.ln2_done, 6 * i)
                for t in range(NT):
                    v.tensor_scalar(ln[:, t, :], h[:, t, :], mv1[:, t, 0:1], rs1[:, t:t + 1],
                                    ALU.subtract, ALU.mult).then_inc(s.ln1_done, 1)

            def taps(i):
                for u in range(12):
                    ch, m = u // 6, (4, 5, 2, 3, 0, 1)[u % 6]
                    dst = uc[:, m, ch * CH:(ch + 1) * CH]
                    dve.wait_ge(s.u_first, 12 * i + u + 1)
                    v.scalar_tensor_tensor(out=dst, in0=bk[:, (3 + u) % 4, 1:CH + 1], scalar=gate[:, m, 2:3],
                                           in1=dst, op0=ALU.mult, op1=ALU.add).then_inc(s.u_tap1, 1)
                    dve.wait_ge(s.u_tap1, 12 * i + u + 1)
                    v.scalar_tensor_tensor(out=dst, in0=bk[:, (3 + u) % 4, 0:CH], scalar=gate[:, m, 1:2],
                                           in1=dst, op0=ALU.mult, op1=ALU.add).then_inc(s.u_done, 1)
                    if u == 5:
                        dve.wait_ge(s.u_done, 12 * i + 6)
                        v.tensor_tensor(uc[:, :, 0:2], uc[:, :, 0:2], gbias[:, :, 1:3], ALU.subtract
                                        ).then_inc(s.u_edge, 1)

            def product(i, j):
                base = 22 * i + 11 * j
                dve.wait_ge(s.vf_done, 6 * i + 3 + 3 * j)
                if j == 0:
                    dve.wait_ge(s.y_ready, 3 * i)
                n = 0
                for d in range(NQ):
                    nq = NQ - d
                    x = xf[:, j, :, d:NQ, :]
                    t0 = x if d == 0 else ta[:, :, 0:nq, :]
                    t1 = ta[:, :, :, :] if d == 0 else tb[:, :, 0:nq, :]
                    for r, t in ((0, t0), (1, t1)):
                        vv = bc(vf[:, j, r, 0:nq, :], 1, 2)
                        kk = bc(kf[:, j, d, 1 - r:3 - r, :], 2, nq)
                        if d == 1 and r == 0:
                            dve.wait_ge(s.pw_done, base + 3)
                        if d == 2 and r == 0:
                            dve.wait_ge(s.pw_done, base + 7)
                        v.tensor_tensor(t, vv, kk, ALU.mult).then_inc(s.pw_done, 1)
                        n += 1
                    for t in ((t1,) if d == 0 else (t0, t1)):
                        dve.wait_ge(s.pw_done, base + n)
                        v.tensor_tensor(x, x, t, ALU.add).then_inc(s.pw_done, 1)
                        n += 1
                dve.wait_ge(s.pw_done, base + n)

            def finish(c):
                for j in range(3):
                    dve.wait_ge(s.f2_ready, 3 * c + j + 1)
                    if j == 0:
                        dve.wait_ge(s.res_done, c + 1)
                        dve.wait_ge(s.out_done, 48 * c)
                    v.scalar_tensor_tensor(out=ob[:, 2 * j:2 * j + 2, :].rearrange("p t c -> p (t c)"),
                                           in0=bk[0:T, 4 + (3 + j) % 4, :], scalar=0.5,
                                           in1=res[:, 2 * j:2 * j + 2, :].rearrange("p t c -> p (t c)"),
                                           op0=ALU.mult, op1=ALU.add).then_inc(s.ob_done, 1)

            def gate_y(i):
                dve.wait_ge(s.u_done, 12 * i + 12)
                dve.wait_ge(s.u_edge, i + 1)
                for q in range(NQ):
                    dve.wait_ge(s.y_ready, 3 * i + q + 1)
                    for k in range(2):
                        v.scalar_tensor_tensor(out=yt[:, k, q * BL:(q + 1) * BL], in0=bk[:, q, k * BL:(k + 1) * BL],
                                               scalar=fbias[:, k:k + 1], in1=uc[:, k, q * BL:(q + 1) * BL],
                                               op0=ALU.add, op1=ALU.mult).then_inc(s.y_done, 1)

            def residual(i):
                for j in range(3):
                    dve.wait_ge(s.o_ready, 3 * i + j + 1)
                    if j == 0:
                        dve.wait_ge(s.hb_done, i + 1)
                        dve.wait_ge(s.res_done, i)
                    v.tensor_tensor(h2[:, 2 * j:2 * j + 2, :], bk[0:T, (3 + j) % 4, :].rearrange(
                        "p (t c) -> p t c", t=2), hb[:, 2 * j:2 * j + 2, :], ALU.add).then_inc(s.h2_done, 1)

            def step(i, front, back):
                c = i - 1
                if front:
                    onehot(i)
                if back:
                    norm2(c)
                if back:
                    apply2(c)
                if front:
                    norm1(i)
                    apply1(i)
                    taps(i)
                    product(i, 0)
                    product(i, 1)
                if back:
                    finish(c)
                if front:
                    gate_y(i)
                    residual(i)

            step(0, True, False)
            step(1, True, True)
            with dve.Fori(2, B) as i:
                step(i, True, True)
            step(B, False, True)

        @block.gpsimd
        def _(pool):
            g = nc.gpsimd
            pool.wait_ge(s.pwr_const, 2)
            pool.wait_ge(s.loads_mats, MATS)

            def step(i, front, back):
                c = i - 1
                if back:
                    pool.wait_ge(s.va2_done, 2 * i)
                    g.tensor_tensor(rs2[:].rearrange("p a t -> p (a t)"), va2[:].rearrange("p a t -> p (a t)"),
                                    mhalf[:, 0:12], ALU.pow).then_inc(s.rs2_done, 1)
                if front:
                    pool.wait_ge(s.va1_done, i + 1)
                    g.tensor_tensor(rs1[:], va1[:], mhalf[:, 0:NT], ALU.pow).then_inc(s.rs1_done, 1)
                if back:
                    pool.wait_ge(s.ob_done, 3 * c)
                    pool.wait_ge(s.rs2_done, i)
                    pool.wait_ge(s.mv2_done, 6 * i)
                if front:
                    pool.wait_ge(s.h_done, 3 * i + 3)
                    pool.wait_ge(s.h2_done, 3 * i)
                    g.tensor_tensor(hb, h[:], bc(bout[:], 1, NT), ALU.add).then_inc(s.hb_done, 1)
                if back:
                    for t in range(NT):
                        g.tensor_scalar(res[:, t, :], h2[:, t, :], mv2[:, t, 0:1], rs2[:, 0, t:t + 1],
                                        ALU.subtract, ALU.mult).then_inc(s.r_done, 1)
                    pool.wait_ge(s.r_done, 6 * i)
                    g.tensor_tensor(res[:], res[:], h2[:], ALU.add).then_inc(s.rb_done, 1)
                    pool.wait_ge(s.rb_done, i)
                    g.tensor_tensor(res[:], res[:], bc(fb2[:], 1, NT), ALU.add).then_inc(s.res_done, 1)
                if front:
                    for ch in range(2):
                        pool.wait_ge(s.u_done, 12 * i + 6 * ch + 4)
                        pool.wait_ge(s.u_edge, i + 1)
                        vv = uc[:, 4:6, ch * CH:(ch + 1) * CH]
                        g.tensor_tensor(vv, vv, uc[:, 2:4, ch * CH:(ch + 1) * CH], ALU.mult
                                        ).then_inc(s.v_done, 1)

            step(0, True, False)
            step(1, True, True)
            with pool.Fori(2, B) as i:
                step(i, True, True)
            step(B, False, True)


def constants():
    f64 = np.float64
    n = np.arange(NF, dtype=f64)
    k = np.arange(KF, dtype=f64)
    w = 2.0 * np.pi * n[:, None] * k[None, :] / NF
    stft = np.concatenate([np.cos(w), -np.sin(w)], axis=1)
    t = np.arange(L, dtype=np.float32) / np.float32(L - 1)
    phase = np.float32(1e-4) * (np.float32(2.0 * np.pi) * np.arange(L, dtype=np.float32) / np.float32(L))
    features = np.stack([t, np.cos(phase), -np.sin(phase), np.ones_like(t)])[:, ::-1]
    delta = np.abs(np.linspace(np.log(0.01) / 0.3, np.log(0.01) / 1.5, D).astype(np.float32))
    decay = np.exp(-t[:, None] * delta[None, :])[::-1].reshape(NT, T, D).transpose(1, 0, 2)
    f = np.arange(BL, dtype=f64)
    th = np.pi * (2 * f[None, :] + 1) * np.arange(BL, dtype=f64)[:, None] / ND
    fwd = np.stack([np.cos(th), -np.sin(th)], axis=0).reshape(2, 2, T, 2, T)
    dft = fwd.transpose(2, 1, 3, 0, 4).reshape(T, 2, 4, T)
    inv = np.stack([np.cos(th), -np.sin(th)], axis=0) * (2.0 / ND)
    idft = inv.reshape(2, BL, 2, T).transpose(3, 2, 0, 1).reshape(T, 4, BL)
    sg = (-1.0) ** np.arange(T)
    coord = np.clip((np.arange(NTXT) + 0.5) * (FR / NTXT) - 0.5, 0.0, FR - 1.0)
    i0 = np.floor(coord).astype(int)
    i1 = np.minimum(i0 + 1, FR - 1)
    wt = (coord - i0).astype(np.float32)
    rows = np.zeros((FR + 2, L), np.float32)
    cols = NPATCH + np.arange(NTXT)
    np.add.at(rows, (i0, cols), np.float32(1.0) - wt)
    np.add.at(rows, (i1, cols), wt)
    rows[FR, NPATCH:] = 1.0
    rows[FR + 1, :NPATCH] = 1.0
    c = dict(stft_mat=stft, features=features, decay=decay, dft=dft, idft=idft,
             signs=np.stack([sg, -sg], axis=1), interp=rows, ident=np.eye(128),
             iota_row=np.tile(np.arange(V), (NF, 1)), iota_col=np.arange(V)[:, None])
    return {k: np.ascontiguousarray(v, dtype=np.float32) for k, v in c.items()}


def layout(i):
    x = i["x"].reshape(B, 3, 14, 16, 14, 16).transpose(0, 1, 3, 5, 2, 4).reshape(B, KP // 128, 128, NPATCH)
    pos = np.arange(FR)[None, :] * NF + np.arange(NF)[:, None] - NF // 2
    pos = np.abs(pos)
    pos = np.where(pos >= NTXT, 2 * (NTXT - 1) - pos, pos)
    frames = i["x_txt"][:, pos].transpose(1, 0, 2).reshape(NF, 2, 4 * FR).transpose(0, 2, 1).reshape(NF, B * FR)
    tiles = lambda w, k=128: w.reshape(w.shape[0] // k, k, w.shape[1]).transpose(1, 0, 2)
    cols = lambda v: v.reshape(-1, 128).T
    gate = np.stack([cols(i["L0_attn_b_in"]), *(cols(i["L0_attn_short_w"][:, t]) for t in range(3)),
                     cols(i["L0_attn_short_b"])], axis=2)
    o = dict(
        x=x.transpose(0, 2, 1, 3), ids=np.repeat(i["x_txt"][:, None, :], V, axis=1), ids_frames=frames,
        window=i["L0_txt_window"][:, None], proj=i["L0_txt_proj_w"].reshape(DST, KF, V).transpose(2, 1, 0),
        table=i["L0_txt_emb_table"], proj_bias=np.tile(i["L0_txt_proj_b"], (1, B, 1)),
        tok_bias=np.tile(i["L0_tok_b2"], (1, B, 1)),
        w1=tiles(i["L0_tok_W1"]), b1=cols(i["L0_tok_b1"]), w2=tiles(i["L0_tok_W2"]),
        win=tiles(i["L0_attn_W_in"]), gate=gate, fbias=cols(i["L0_attn_filter_bias"]),
        wout=tiles(i["L0_attn_W_out"]), bout=i["L0_attn_b_out"], gamma=cols(i["L0_ffn_ln_gamma"]),
        beta=cols(i["L0_ffn_ln_beta"]), fb1=cols(i["L0_ffn_fc1_bias"]), fb2=i["L0_ffn_fc2_bias"],
        fc1_q=tiles(i["L0_ffn_fc1_q"]).reshape(128, -1), fc2_q=tiles(i["L0_ffn_fc2_q"]).reshape(128, -1),
        fc1_scales=i["L0_ffn_fc1_scales"].reshape(-1), fc2_scales=i["L0_ffn_fc2_scales"].reshape(-1),
        L0_attn_W1=i["L0_attn_W1"], L0_attn_W2=i["L0_attn_W2"], L0_attn_W3=i["L0_attn_W3"],
        f_b1=i["L0_attn_b1"][None, :], f_b2=i["L0_attn_b2"][None, :], f_b3=i["L0_attn_b3"][None, :],
        f_f1=i["L0_attn_f1"][:, None], f_f2=i["L0_attn_f2"][:, None])
    return {k: np.ascontiguousarray(v) for k, v in o.items()}


def kernel(**inputs):
    import concourse.bacc as bacc
    from concourse.bass_utils import run_bass_kernel_spmd

    nc = bacc.Bacc("TRN2", target_bir_lowering=False, num_devices=1)
    data = {**layout({k: np.asarray(v) for k, v in inputs.items()}), **constants()}
    arrays = {"in_" + k: v for k, v in data.items()}
    aps = {k: nc.dram_tensor("in_" + k, v.shape, mybir.dt.from_np(v.dtype), kind="ExternalInput").ap()
           for k, v in data.items()}
    out = nc.dram_tensor("out", (B, L, D), F32, kind="ExternalOutput").ap()
    program(nc, aps, out)
    r = run_bass_kernel_spmd(nc, [arrays], core_ids=[0])
    return r.results[0]["out"]
```

```python
from contextlib import ExitStack

import numpy as np

import concourse.bass as bass
from concourse import mybir

F32 = mybir.dt.float32
F32R = mybir.dt.float32r
I32 = mybir.dt.int32
ALU = mybir.AluOpType
ACT = mybir.ActivationFunctionType

B = 8
NPATCH = 196
NTXT = 512
L = NPATCH + NTXT
D = 256
KP = 768
WID = 3 * D
HID = 64
FF = 1024
V = 64
DEMB = 179
DST = D - DEMB
NF = 64
FR = 1 + NTXT // NF
KF = NF // 2 + 1
T = 118
NT = L // T
NQ = 3
BL = L // NQ
ND = 2 * BL
CH = L // 2
RB = V + FR + 2
EPS = 1e-5
MAGIC = 1.5 * 2.0 ** 23
SIN_C = (6.28125, 0.0019350051879882812, 3.019916e-07)


PARTS = ((0, 0), (0, 1), (1, 0))


def bc(ap, axis, n):
    ap = ap.unsqueeze(axis)
    shape = list(ap.shape)
    shape[axis] = n
    return ap.broadcast_to(shape)


class Semaphores:

    def __init__(self, sem):
        self.loads_text = sem("loads_text")
        self.loads_filter = sem("loads_filter")
        self.loads_mats = sem("loads_mats")
        self.loads_up = sem("loads_up")
        self.loads_raw = sem("loads_raw")
        self.loads_q1 = sem("loads_q1")
        self.loads_q2 = sem("loads_q2")
        self.rows_in = sem("rows_in")
        self.xp_in = sem("xp_in")
        self.ids_in = sem("ids_in")
        self.out_done = sem("out_done")
        self.memsets = sem("memsets")
        self.window_done = sem("window_done")
        self.onehot_frames = sem("onehot_frames")
        self.stft = sem("stft")
        self.squares = sem("squares")
        self.sums = sem("sums")
        self.roots = sem("roots")
        self.mags = sem("mags")
        self.enc_ready = sem("enc_ready")
        self.enc_done = sem("enc_done")
        self.fil_ready = sem("fil_ready")
        self.fil_steps = sem("fil_steps")
        self.angle_steps = sem("angle_steps")
        self.reduced = sem("reduced")
        self.sin_done = sem("sin_done")
        self.kt_ready = sem("kt_ready")
        self.kt_done = sem("kt_done")
        self.kraw_ready = sem("kraw_ready")
        self.kraw_done = sem("kraw_done")
        self.kf_steps = sem("kf_steps")
        self.dft_split = sem("dft_split")
        self.rows_split = sem("rows_split")
        self.win_split = sem("win_split")
        self.fc1_split = sem("fc1_split")
        self.fc1_raw = sem("fc1_raw")
        self.fc1_bias = sem("fc1_bias")
        self.fc1_fold = sem("fc1_fold")
        self.deq = sem("deq")
        self.gbias_done = sem("gbias_done")
        self.pwr_const = sem("pwr_const")
        self.h1_ready = sem("h1_ready")
        self.h1_done = sem("h1_done")
        self.onehot_done = sem("onehot_done")
        self.h_ready = sem("h_ready")
        self.h_done = sem("h_done")
        self.hb_done = sem("hb_done")
        self.st1_done = sem("st1_done")
        self.mv1_done = sem("mv1_done")
        self.va1_done = sem("va1_done")
        self.rs1_done = sem("rs1_done")
        self.ln1_done = sem("ln1_done")
        self.xt_ready = sem("xt_ready")
        self.xt_hi = sem("xt_hi")
        self.xt_done = sem("xt_done")
        self.u_ready = sem("u_ready")
        self.u_first = sem("u_first")
        self.u_tap1 = sem("u_tap1")
        self.u_done = sem("u_done")
        self.u_edge = sem("u_edge")
        self.v_done = sem("v_done")
        self.vt_ready = sem("vt_ready")
        self.vt_hi = sem("vt_hi")
        self.vt_done = sem("vt_done")
        self.vf_ready = sem("vf_ready")
        self.vf_done = sem("vf_done")
        self.pw_done = sem("pw_done")
        self.y_ready = sem("y_ready")
        self.y_done = sem("y_done")
        self.o_ready = sem("o_ready")
        self.h2_done = sem("h2_done")
        self.st2_done = sem("st2_done")
        self.mv2_done = sem("mv2_done")
        self.va2_done = sem("va2_done")
        self.rs2_done = sem("rs2_done")
        self.ln2_done = sem("ln2_done")
        self.r_done = sem("r_done")
        self.rb_done = sem("rb_done")
        self.res_done = sem("res_done")
        self.zt_ready = sem("zt_ready")
        self.zt_hi = sem("zt_hi")
        self.zt_done = sem("zt_done")
        self.f1_ready = sem("f1_ready")
        self.f1_done = sem("f1_done")
        self.f2_ready = sem("f2_ready")
        self.ob_done = sem("ob_done")


def program(nc, a, out):
    with ExitStack() as ctx:
        def sb(name, shape, dt=F32):
            return ctx.enter_context(nc.sbuf_tensor(name, shape, dt))

        def sem(name):
            return ctx.enter_context(nc.semaphore(name))

        bk = ctx.enter_context(nc.psum_tensor("banks", [128, 8, 512], F32))

        ident = sb("ident", [128, 128])
        w1 = sb("w1", [128, KP // 128, D])
        b1 = sb("b1", [128, 2])
        w2 = sb("w2", [128, 2, D])
        win = sb("win", [128, 2, 2, WID], F32R)
        gate = sb("gate", [128, 6, 5])
        gbias = sb("gbias", [128, 6, 3])
        fbias = sb("fbias", [128, 2])
        wout = sb("wout", [128, 2, D])
        bout = sb("bout", [T, D])
        gamma = sb("gamma", [128, 2])
        beta = sb("beta", [128, 2])
        fc1 = sb("fc1", [128, 2, 2, FF], F32R)
        fb1 = sb("fb1", [128, 8])
        fc2 = sb("fc2", [128, 8, D])
        fb2 = sb("fb2", [T, D])
        dft = sb("dft", [T, 2, 2, 4, T], F32R)
        idft = sb("idft", [T, 4, BL])
        sgn = sb("sgn", [T, 2])
        kf = sb("kf", [T, 2, NQ, 2, D])
        rowb = sb("rowb", [RB, 2, D], F32R)
        iotap = sb("iotap", [V, 1])
        mhalf = sb("mhalf", [T, NT])

        xp = sb("xp", [128, KP // 128, NPATCH])
        ids_all = sb("ids", [V + FR, B * DST])
        h1t = sb("h1t", [128, 2, 2 * T])
        oht = sb("oht", [RB, L], F32R)
        h_all = sb("h", [128, NT * D])
        ln = sb("ln", [T, NT, D])
        xt = sb("xt", [128, 2, 2, L + 2], F32R)
        uc_all = sb("uc", [128, 6 * L])
        vt = sb("vt", [T, 2, 2, NQ, D], F32R)
        vf_all = sb("vf", [128, 4 * NQ * D])
        xf_all = sb("xf", [128, 4 * NQ * D])
        h2 = sb("h2", [T, NT, D])
        res = sb("res", [T, NT, D])
        zt = sb("zt", [128, 2, 2, L], F32R)
        at = sb("at", [128, 8, L])
        st = sb("st", [T, NT, 6])
        dif = sb("dif", [T, NT, 2])
        mv1 = sb("mv1", [T, NT, 2])
        va1 = sb("va1", [T, NT])
        rs1 = sb("rs1", [T, NT])
        mv2 = sb("mv2", [T, NT, 2])
        va2 = sb("va2", [T, 2, NT])
        rs2 = sb("rs2", [T, 2, NT])

        ids = ids_all[0:V, 0:NTXT].bitcast(I32)
        rowe = ids_all[V:V + FR, :].rearrange("p (b c) -> p b c", b=B)
        h = h_all[0:T, :].rearrange("p (t c) -> p t c", t=NT)
        vf = vf_all[0:T, :].rearrange("p (j r q c) -> p j r q c", j=2, r=2, q=NQ)
        ob = vf_all[0:T, 0:NT * D].rearrange("p (t c) -> p t c", t=NT)
        yt = vf_all[:, NT * D:NT * D + 2 * L].rearrange("p (h t) -> p h t", h=2)
        ta = h2[:, :, :].rearrange("p (r q) c -> p r q c", r=2)
        tb = ln[:, :, :].rearrange("p (r q) c -> p r q c", r=2)
        uc = uc_all[:, :].rearrange("p (m t) -> p m t", m=6)
        xf = xf_all[0:T, :].rearrange("p (j r q c) -> p j r q c", j=2, r=2, q=NQ)

        dftw = sb("dftw", [NF, 2 * KF])
        wnd = sb("wnd", [NF, 1])
        iotar = ids_all[0:V, NTXT:NTXT + V]
        fw1 = h2[:, :, :].rearrange("p t c -> p (t c)")[0:4, L:L + HID]
        fw2 = h2[:, :, :].rearrange("p t c -> p (t c)")[0:HID + 1, L + HID:L + 2 * HID]
        fw3 = ln[0:HID + 1, 1, :]
        ffreq = sb("ffreq", [HID, 2])
        enc = ln[0:36, :, :].rearrange("p t c -> p (t c)")[:, 0:2 * DST].rearrange("p (g o) -> p g o", g=2)
        at_all = at[:, :, :].rearrange("p a t -> p (a t)")
        ohf = at_all[0:NF, 0:FR * B * V].rearrange("p (f v) -> p f v", v=V)
        quant = at_all[:, 0:2 * FF].bitcast(I32)
        scale = at_all[:, 2 * FF:4 * FF]
        idf = ids[:, 0:FR * B]
        sqv = uc_all[:, 0:36 * 2 * KF].rearrange("p (g k) -> p g k", g=36)
        mag = h_all[:, 0:36 * KF].rearrange("p (g k) -> p g k", g=36)
        root, inv = sqv[:, :, 0:KF], sqv[:, :, KF:2 * KF]
        proj = xf_all[:, 0:KF * DST].rearrange("p (k o) -> p k o", k=KF)
        pet = h2[0:4, :, :].rearrange("p t c -> p (t c)")[:, 0:L]
        fh1 = uc_all[0:HID + 1, 36 * 2 * KF:36 * 2 * KF + L]
        fh2 = uc_all[0:HID + 1, 36 * 2 * KF + L:36 * 2 * KF + 2 * L]
        ang = vf_all[0:HID, 0:L].rearrange("p (c t) -> p c t", c=2)
        turns = vf_all[0:HID, L:2 * L].rearrange("p (c t) -> p c t", c=2)
        win_raw = vf_all[:, 2 * WID:4 * WID].rearrange("p (k n) -> p k n", k=2)
        dft_raw = ln[:, :, :].rearrange("p t c -> p (t c)")[:, 2 * D:2 * D + 8 * T]
        row_raw = at_all[0:RB, FR * B * V:FR * B * V + D]
        oht_raw = at_all[V:RB, FR * B * V + D:FR * B * V + D + L]
        fc1_raw = scale.rearrange("p (k n) -> p k n", k=2)
        decay = res[:, :, :]
        krt = h2[:, :, :].rearrange("p (r q) c -> p r q c", r=2)

        text_loads = [(idf, a["ids_frames"]), (iotar, a["iota_row"]), (dftw[:], a["stft_mat"]),
                      (wnd[:], a["window"]), (iotap[:], a["iota_col"]), (ident[:], a["ident"]),
                      (proj[0:V], a["proj"]), (proj[V:2 * V], a["proj"])]
        filter_loads = [(pet, a["features"]), (fw1[0:3, :], a["L0_attn_W1"]), (fw1[3:4, :], a["f_b1"]),
                        (ffreq[:, 0:1], a["f_f1"]), (ffreq[:, 1:2], a["f_f2"]),
                        (fw2[0:HID, :], a["L0_attn_W2"]), (fw2[HID:HID + 1, :], a["f_b2"]),
                        (fw3[0:HID, :], a["L0_attn_W3"]), (fw3[HID:HID + 1, :], a["f_b3"]),
                        (decay, a["decay"]), (dft_raw, a["dft"]), (sgn[:], a["signs"])]
        up_loads = [(w1[:], a["w1"]), (b1[:], a["b1"]), (w2[:], a["w2"]), (win_raw, a["win"])]
        mat_loads = [(gate[:], a["gate"]), (fbias[:], a["fbias"]), (idft[:], a["idft"]), (wout[:], a["wout"]),
                     (bout[:], a["bout"].partition_broadcast(T)), (gamma[:], a["gamma"]), (beta[:], a["beta"]),
                     (fb1[:], a["fb1"]), (fb2[:], a["fb2"].partition_broadcast(T))]
        TEXT, FILTER = 16 * len(text_loads), 16 * len(filter_loads)
        UP, MATS = 16 * len(up_loads), 16 * len(mat_loads)
        RAW = 16 * 4

        s = Semaphores(sem)
        block = ctx.enter_context(nc.Block())
        out_v = out.rearrange("b (t p) c -> b p t c", p=T)

        @block.sync
        def _(sp):
            for dst, src in text_loads:
                sp.dma_start(dst, src).then_inc(s.loads_text, 16)
            sp.dma_start(xp[:], a["x"][0]).then_inc(s.xp_in, 16)
            for dst, src in up_loads:
                sp.dma_start(dst, src).then_inc(s.loads_up, 16)
            sp.wait_ge(s.memsets, 1)
            sp.dma_start(row_raw[0:V, 0:DEMB], a["table"]).then_inc(s.loads_raw, 16)
            sp.dma_start(row_raw[V + FR:V + FR + 1, DEMB:D], a["proj_bias"]).then_inc(s.loads_raw, 16)
            sp.dma_start(row_raw[V + FR + 1:RB, :], a["tok_bias"]).then_inc(s.loads_raw, 16)
            sp.dma_start(oht_raw, a["interp"]).then_inc(s.loads_raw, 16)
            for dst, src in mat_loads:
                sp.dma_start(dst, src).then_inc(s.loads_mats, 16)
            sp.wait_ge(s.onehot_frames, 1)
            sp.dma_start(ids, a["ids"][0]).then_inc(s.ids_in, 16)
            sp.wait_ge(s.stft, 6)
            sp.dma_start(quant, a["fc1_q"]).then_inc(s.loads_q1, 16)
            sp.dma_start(scale, a["fc1_scales"].partition_broadcast(128)).then_inc(s.loads_q1, 16)
            sp.wait_ge(s.enc_done, 2)
            for bb in range(4):
                sp.dma_start(rowe[:, bb::4, :],
                             enc[FR * bb:FR * bb + FR, :, :]).then_inc(s.rows_in, 16)
            sp.wait_ge(s.fc1_split, 2)
            sp.dma_start(quant, a["fc2_q"]).then_inc(s.loads_q2, 16)
            sp.dma_start(scale, a["fc2_scales"].partition_broadcast(128)).then_inc(s.loads_q2, 16)

            def step(i, front, back):
                if back:
                    c = i - 1
                    for j in range(3):
                        sp.wait_ge(s.ob_done, 3 * c + j + 1)
                        sp.dma_start(out_v[c, :, 2 * j:2 * j + 2, :] if isinstance(c, int)
                                     else out_v[bass.ds(c, 1), :, 2 * j:2 * j + 2, :].rearrange("b p t c -> (b p) t c"),
                                     ob[:, 2 * j:2 * j + 2, :]).then_inc(s.out_done, 16)

            def prefetch(i):
                sp.wait_ge(s.h1_ready, 2 * i + 2)
                n = i + 1
                sp.dma_start(xp[:], a["x"][n] if isinstance(n, int) else
                             a["x"][bass.ds(n, 1)].rearrange("b p k t -> (b p) k t")).then_inc(s.xp_in, 16)
                sp.wait_ge(s.onehot_done, 3 * i + 1)
                sp.dma_start(ids, a["ids"][n] if isinstance(n, int) else
                             a["ids"][bass.ds(n, 1)].rearrange("b p t -> (b p) t")).then_inc(s.ids_in, 16)

            prefetch(0)
            with sp.Fori(1, B - 1) as i:
                prefetch(i)
                step(i, True, True)
            step(B - 1, True, True)
            step(B, False, True)
            sp.wait_ge(s.out_done, 16 * 3 * B)

        @block.tensor
        def _(pe):
            mm = nc.tensor.matmul

            def spectrum(ready, copied, i, j, bank0):
                for part in range(3):
                    n = 3 * j + part
                    if n >= 4:
                        pe.wait_ge(copied, 6 * i + n - 3)
                    bank = bk[0:T, bank0(n), :]
                    pieces = [(part, bank, 0, 2)] if part < 2 else [(0, bank[:, 0:D], 2, 3), (1, bank[:, D:2 * D], 2, 3)]
                    for p, dst, q0, q1 in pieces:
                        for r in range(2):
                            for wp, xq in PARTS:
                                o = mm(dst, dft[:, wp, r, 2 * j + p, :],
                                       vt[:, xq, r, q0:q1, :].rearrange("p q c -> p (q c)"),
                                       start=(r == 0 and (wp, xq) == PARTS[0]), stop=(r == 1 and (wp, xq) == PARTS[-1]))
                    o.then_inc(ready, 1)

            def patches_up(i):
                pe.wait_ge(s.xp_in, 16 * i + 16)
                for m in range(2):
                    for k in range(KP // 128):
                        o = mm(bk[:, 0, m * NPATCH:(m + 1) * NPATCH], w1[:, k, m * 128:(m + 1) * 128], xp[:, k, :],
                               start=(k == 0), stop=(k == KP // 128 - 1))
                    o.then_inc(s.h1_ready, 1)

            def rows(i):
                pe.wait_ge(s.onehot_done, 3 * i + 3)
                pe.wait_ge(s.h2_done, 3 * i)
                for t in range(NT):
                    dst = bk[0:T, 1 + t // 2, (t % 2) * D:(t % 2 + 1) * D]
                    if t == 0:
                        pe.wait_ge(s.h1_done, 2 * i + 2)
                    for p in range(2):
                        o = mm(dst, oht[:, t * T:(t + 1) * T], rowb[:, p, :], start=(p == 0), stop=(p == 1 and t > 1))
                    for k in range(2 if t < 2 else 0):
                        o = mm(dst, h1t[:, k, t * T:(t + 1) * T], w2[:, k, :], start=False, stop=(k == 1))
                    if t % 2:
                        o.then_inc(s.h_ready, 1)

            def turn_pair(j, bank):
                for t in range(2):
                    for k in range(2):
                        o = nc.tensor.transpose(bk[:, bank, k * BL + t * T:k * BL + (t + 1) * T],
                                                ln[:, 2 * j + t, k * 128:(k + 1) * 128], ident[0:T, 0:T])
                return o

            def turn_front(i):
                for j in range(3):
                    pe.wait_ge(s.ln1_done, 6 * i + 2 * j + 2)
                    if j:
                        pe.wait_ge(s.h_done, 3 * i + j)
                    turn_pair(j, j).then_inc(s.xt_ready, 1)

            def gates(i):
                for u in range(12):
                    c, m = u // 6, (4, 5, 2, 3, 0, 1)[u % 6]
                    pe.wait_ge(s.xt_done, 3 * i + 2 + c)
                    if u == 0:
                        pe.wait_ge(s.h_done, 3 * i + 3)
                    if u == 3:
                        pe.wait_ge(s.xt_done, 3 * i + 3)
                    if u >= 4:
                        pe.wait_ge(s.u_done, 12 * i + u - 3)
                    for k in range(2):
                        for wp, xq in PARTS:
                            o = mm(bk[:, (3 + u) % 4, 0:CH + 2], win[:, wp, k, m * 128:(m + 1) * 128],
                                   xt[:, xq, k, c * CH:c * CH + CH + 2],
                                   start=(k == 0 and (wp, xq) == PARTS[0]), stop=(k == 1 and (wp, xq) == PARTS[-1]))
                    o.then_inc(s.u_ready, 1)

            def turn_v(i):
                for q in range(NQ):
                    pe.wait_ge(s.v_done, 2 * i + 1 + (q > 0))
                    pe.wait_ge(s.u_done, 12 * i + 9 + q)
                    for r in range(2):
                        for k in range(2):
                            t = 2 * q + r
                            o = nc.tensor.transpose(bk[0:T, (3 + q) % 4, r * D + k * 128:r * D + (k + 1) * 128],
                                                    uc[:, 4 + k, t * T:(t + 1) * T], ident[:])
                    o.then_inc(s.vt_ready, 1)

            def inverse(i, j):
                if j == 0:
                    pe.wait_ge(s.vf_done, 6 * i + 5)
                pe.wait_ge(s.pw_done, 28 * i + 14 * j + 14)
                for q in range(NQ):
                    for k in range(2):
                        for f in (2 * j, 2 * j + 1):
                            o = mm(bk[:, q, k * BL:(k + 1) * BL], xf[:, f // 2, f % 2, q, k * 128:(k + 1) * 128],
                                   idft[:, f, :], start=(f == 0 and k == 0), stop=(f == 3),
                                   skip_group_check=True)
                    if j == 1:
                        o.then_inc(s.y_ready, 1)

            def output(i):
                for j in range(3):
                    pe.wait_ge(s.y_done, 6 * i + 2 * j + 2)
                    for t in (2 * j, 2 * j + 1):
                        for k in range(2):
                            o = mm(bk[0:T, (3 + j) % 4, (t % 2) * D:(t % 2 + 1) * D],
                                   yt[:, k, t * T:(t + 1) * T], wout[:, k, :], start=(k == 0), stop=(k == 1))
                    o.then_inc(s.o_ready, 1)

            def turn_back(c):
                pe.wait_ge(s.ob_done, 3 * c)
                pe.wait_ge(s.f1_done, 16 * c)
                for j in range(3):
                    pe.wait_ge(s.ln2_done, 6 * c + 2 * j + 2)
                    turn_pair(j, 4 + j).then_inc(s.zt_ready, 1)

            def up(c, lo, hi):
                for u in range(lo, hi):
                    ch, m = u // 8, u % 8
                    pe.wait_ge(s.zt_done, 3 * c + 2 + ch)
                    if u == 3:
                        pe.wait_ge(s.zt_done, 3 * c + 3)
                    if u >= 4:
                        pe.wait_ge(s.f1_done, 16 * c + u - 3)
                    for k in range(2):
                        for wp, xq in PARTS:
                            o = mm(bk[:, 4 + (3 + u) % 4, 0:CH], fc1[:, wp, k, m * 128:(m + 1) * 128],
                                   zt[:, xq, k, ch * CH:(ch + 1) * CH],
                                   start=(k == 0 and (wp, xq) == PARTS[0]), stop=(k == 1 and (wp, xq) == PARTS[-1]))
                    o.then_inc(s.f1_ready, 1)

            def down(c, lo, hi):
                if lo == 0:
                    pe.wait_ge(s.f1_done, 16 * c + 16)
                for t in range(lo, hi):
                    for k in range(8):
                        o = mm(bk[0:T, 4 + (3 + t // 2) % 4, (t % 2) * D:(t % 2 + 1) * D],
                               at[:, k, t * T:(t + 1) * T], fc2[:, k, :], start=(k == 0), stop=(k == 7))
                    if t % 2:
                        o.then_inc(s.f2_ready, 1)

            def step(i, front, back):
                c = i - 1
                if front:
                    pe.wait_ge(s.h2_done, 3 * i - 1)
                    patches_up(i)
                if back:
                    turn_back(c)
                if front:
                    rows(i)
                if back:
                    up(c, 0, 6)
                if front:
                    turn_front(i)
                if back:
                    up(c, 6, 8)
                if front:
                    gates(i)
                if back:
                    up(c, 8, 11)
                if front:
                    turn_v(i)
                if back:
                    up(c, 11, 13)
                if front:
                    spectrum_v(i, 0)
                if back:
                    up(c, 13, 16)
                if front:
                    spectrum_v(i, 1)
                if back:
                    down(c, 0, 4)
                if front:
                    inverse(i, 0)
                if back:
                    down(c, 4, 5)
                if front:
                    inverse(i, 1)
                    output(i)
                if back:
                    down(c, 5, 6)

            def spectrum_v(i, j):
                pe.wait_ge(s.vt_done, 3 * i + 3)
                pe.wait_ge(s.u_done, 12 * i + 12)
                spectrum(s.vf_ready, s.vf_done, i, j, lambda n: (2 + n) % 4)

            pe.wait_ge(s.loads_filter, FILTER)
            pe.wait_ge(s.memsets, 7)
            for c in range(2):
                mm(bk[0:HID, 4 + c, 0:CH], fw1, pet[:, c * CH:(c + 1) * CH], start=True, stop=True
                   ).then_inc(s.fil_ready, 1)
            pe.wait_ge(s.loads_up, UP)
            patches_up(0)
            for c in range(2):
                pe.wait_ge(s.sin_done, c + 1)
                mm(bk[0:HID, 6 + c, 0:CH], fw2, fh1[:, c * CH:(c + 1) * CH], start=True, stop=True
                   ).then_inc(s.fil_ready, 1)
            pe.wait_ge(s.onehot_frames, 1)
            pe.wait_ge(s.window_done, 1)
            pe.wait_ge(s.h1_done, 2)
            for g in range(6):
                if g == 4:
                    pe.wait_ge(s.fil_steps, 10)
                if g == 5:
                    pe.wait_ge(s.squares, 1)
                for j in range(6):
                    jj = 6 * g + j
                    o = mm(bk[:, (0, 1, 2, 3, 7, 0)[g], j * 2 * KF:(j + 1) * 2 * KF],
                           at_all[0:NF, jj * 128:(jj + 1) * 128], dftw[:], start=True, stop=True)
                o.then_inc(s.stft, 1)
            for t in range(NT):
                pe.wait_ge(s.sin_done, 3 + t // 3)
                mm(bk[0:T, 4 + t // 2, (t % 2) * D:(t % 2 + 1) * D], fh2[:, t * T:(t + 1) * T], fw3,
                   start=True, stop=True).then_inc(s.kt_ready, 1)
            pe.wait_ge(s.mags, 4)
            for k in range(KF):
                for g in range(2):
                    o = mm(bk[0:36, g, 0:DST], mag[V * g:V * g + V, :, k], proj[V * g:V * g + V, k, :],
                           start=(k == 0), stop=(k == KF - 1))
                    if k == KF - 1:
                        o.then_inc(s.enc_ready, 1)
            pe.wait_ge(s.kt_done, 9)
            for j in range(2):
                spectrum(s.kraw_ready, s.kraw_done, 0, j, lambda n: 4 + n % 4)
            pe.wait_ge(s.enc_done, 2)
            rows(0)
            turn_front(0)
            pe.wait_ge(s.win_split, 2)
            gates(0)
            turn_v(0)
            spectrum_v(0, 0)
            spectrum_v(0, 1)
            pe.wait_ge(s.fc1_raw, 1)
            pe.wait_ge(s.loads_mats, MATS)
            for m in range(8):
                for k in range(2):
                    o = mm(bk[:, 7, m:m + 1], fc1_raw[:, k, m * 128:(m + 1) * 128], beta[:, k:k + 1],
                           start=(k == 0), stop=(k == 1))
            o.then_inc(s.fc1_bias, 1)
            inverse(0, 0)
            inverse(0, 1)
            output(0)
            pe.wait_ge(s.fc1_split, 2)
            pe.wait_ge(s.fc1_fold, 3)
            pe.wait_ge(s.deq, 1)
            step(1, True, True)
            with pe.Fori(2, B) as i:
                step(i, True, True)
            step(B, False, True)

        @block.scalar
        def _(act):
            A = nc.scalar.activation

            def spectrum_out(n, bank, done):
                j, part = n // 3, n % 3
                bank = bk[0:T, bank, :].rearrange("p (x c) -> p x c", x=2)
                A(vf[:, j, part, 0:2, :] if part < 2 else vf[:, j, :, 2, :], bank, ACT.Copy).then_inc(done, 1)

            for dst, src in filter_loads:
                act.dma_start(dst, src).then_inc(s.loads_filter, 16)

            def sine(c):
                act.wait_ge(s.reduced, c + 1)
                A((fh1 if c < 2 else fh2)[0:HID, (c % 2) * CH:(c % 2 + 1) * CH], ang[:, c % 2, :], ACT.Sin
                  ).then_inc(s.sin_done, 1)

            def patches(i):
                act.wait_ge(s.h_ready, 3 * i)
                act.wait_ge(s.h1_ready, 2 * i + 2)
                for m in range(2):
                    A(h1t[:, m, 0:NPATCH], bk[:, 0, m * NPATCH:(m + 1) * NPATCH], ACT.Silu, bias=b1[:, m:m + 1]
                      ).then_inc(s.h1_done, 1)

            def rows(i):
                act.wait_ge(s.h2_done, 3 * i)
                for j in range(3):
                    act.wait_ge(s.h_ready, 3 * i + j + 1)
                    A(h[:, 2 * j:2 * j + 2, :], bk[0:T, 1 + j, :], ACT.Copy).then_inc(s.h_done, 1)

            def xt_high(i):
                act.wait_ge(s.u_ready, 12 * i)
                for j in range(3):
                    act.wait_ge(s.xt_ready, 3 * i + j + 1)
                    A(xt[:, 0, :, 2 + j * BL:2 + (j + 1) * BL],
                      bk[:, j, 0:2 * BL].rearrange("p (k t) -> p k t", k=2), ACT.Copy).then_inc(s.xt_hi, 1)

            def last_tap(i):
                act.wait_ge(s.y_done, 6 * i)
                for u in range(12):
                    ch, m = u // 6, (4, 5, 2, 3, 0, 1)[u % 6]
                    act.wait_ge(s.u_ready, 12 * i + u + 1)
                    A(uc[:, m, ch * CH:(ch + 1) * CH], bk[:, (3 + u) % 4, 2:CH + 2], ACT.Identity,
                      scale=gate[:, m, 3:4], bias=gbias[:, m, 0:1]).then_inc(s.u_first, 1)

            def vt_high(i):
                act.wait_ge(s.vf_ready, 6 * i)
                for q in range(NQ):
                    act.wait_ge(s.vt_ready, 3 * i + q + 1)
                    A(vt[:, 0, :, q, :], bk[0:T, (3 + q) % 4, :].rearrange("p (r c) -> p r c", r=2), ACT.Copy
                      ).then_inc(s.vt_hi, 1)

            def spectrum_v(i, j, rows_out):
                if j == 0:
                    act.wait_ge(s.pw_done, 28 * i)
                    act.wait_ge(s.o_ready, 3 * i)
                    act.wait_ge(s.out_done, rows_out)
                for n in range(3 * j, 3 * j + 3):
                    act.wait_ge(s.vf_ready, 6 * i + n + 1)
                    spectrum_out(n, (2 + n) % 4, s.vf_done)

            act.wait_ge(s.loads_filter, FILTER)
            sine(0)
            sine(1)
            act.wait_ge(s.loads_up, UP)
            patches(0)
            sine(2)
            sine(3)
            for g in range(6):
                act.wait_ge(s.stft, g + 1)
                A(sqv[:, 6 * g:6 * g + 6, :], bk[:, (0, 1, 2, 3, 7, 0)[g], 0:12 * KF].rearrange("p (g k) -> p g k", g=6),
                  ACT.Square).then_inc(s.squares, 1)
            act.wait_ge(s.sums, 1)
            A(root, mag, ACT.Sqrt).then_inc(s.roots, 1)
            act.wait_ge(s.enc_ready, 2)
            for g in range(2):
                A(enc[:, g, :], bk[0:36, g, 0:DST], ACT.Copy).then_inc(s.enc_done, 1)
            act.wait_ge(s.win_split, 2)
            for n in range(6):
                act.wait_ge(s.kraw_ready, n + 1)
                spectrum_out(n, 4 + n % 4, s.kraw_done)
            rows(0)
            xt_high(0)
            act.wait_ge(s.gbias_done, 6)
            last_tap(0)
            vt_high(0)
            act.wait_ge(s.kf_steps, 12)
            spectrum_v(0, 0, 0)
            spectrum_v(0, 1, 0)

            def silu(c, lo, hi):
                for u in range(lo, hi):
                    ch, m = u // 8, u % 8
                    act.wait_ge(s.f1_ready, 16 * c + u + 1)
                    A(at[:, m, ch * CH:(ch + 1) * CH], bk[:, 4 + (3 + u) % 4, 0:CH], ACT.Silu,
                      bias=fb1[:, m:m + 1]).then_inc(s.f1_done, 1)

            def zt_high(c):
                act.wait_ge(s.f1_ready, 16 * c)
                for j in range(3):
                    act.wait_ge(s.zt_ready, 3 * c + j + 1)
                    A(zt[:, 0, :, j * BL:(j + 1) * BL], bk[:, 4 + j, 0:2 * BL].rearrange("p (k t) -> p k t", k=2),
                      ACT.Copy).then_inc(s.zt_hi, 1)

            def step(i, front, back):
                c = i - 1
                if front:
                    patches(i)
                if back:
                    zt_high(c)
                if front:
                    rows(i)
                if back:
                    act.wait_ge(s.f2_ready, 3 * c)
                    silu(c, 0, 6)
                if front:
                    xt_high(i)
                if back:
                    silu(c, 6, 8)
                if front:
                    last_tap(i)
                if back:
                    silu(c, 8, 11)
                if front:
                    vt_high(i)
                if back:
                    silu(c, 11, 13)
                if front:
                    spectrum_v(i, 0, 48 * c)
                if back:
                    silu(c, 13, 16)
                if front:
                    spectrum_v(i, 1, 48 * c)

            act.wait_ge(s.fc1_fold, 3)
            step(1, True, True)
            with act.Fori(2, B) as i:
                step(i, True, True)
            step(B, False, True)

        @block.vector
        def _(dve):
            v = nc.vector
            v.memset(row_raw, 0.0).then_inc(s.memsets, 1)
            v.memset(oht[:].bitcast(F32), 0.0).then_inc(s.memsets, 1)
            v.memset(h1t[:, :, NPATCH:2 * T], 0.0).then_inc(s.memsets, 1)
            for p in range(2):
                v.memset(xt[:, p, :, 0:2].bitcast(F32), 0.0).then_inc(s.memsets, 1)
            v.memset(fh1, 1.0).then_inc(s.memsets, 1)
            v.memset(fh2, 1.0).then_inc(s.memsets, 1)

            def split(hi, lo, src, done, n):
                v.tensor_copy(hi, src).then_inc(done, 1)
                dve.wait_ge(done, n + 1)
                v.tensor_tensor(lo, src, hi.bitcast(F32), ALU.subtract).then_inc(done, 1)

            dve.wait_ge(s.loads_text, TEXT)
            v.tensor_tensor(ohf, bc(idf, 2, V), bc(iotar, 1, FR * B), ALU.is_equal).then_inc(s.onehot_frames, 1)
            v.tensor_scalar(dftw[:], dftw[:], wnd[:, 0:1], None, ALU.mult).then_inc(s.window_done, 1)

            dve.wait_ge(s.loads_filter, FILTER)
            dve.wait_ge(s.memsets, 7)
            for c in range(4):
                dve.wait_ge(s.fil_ready, c + 1)
                x, n = ang[:, c % 2, :], turns[:, c % 2, :]
                if c >= 2:
                    dve.wait_ge(s.sin_done, c - 1)
                v.tensor_scalar(x, bk[0:HID, 4 + c, 0:CH], ffreq[:, c // 2:c // 2 + 1], None, ALU.mult
                                ).then_inc(s.fil_steps, 1)
                dve.wait_ge(s.fil_steps, 3 * c + 1)
                v.tensor_scalar(n, x, 1.0 / (2.0 * np.pi), MAGIC, ALU.mult, ALU.add).then_inc(s.fil_steps, 1)
                dve.wait_ge(s.fil_steps, 3 * c + 2)
                v.tensor_scalar(n, n, MAGIC, None, ALU.subtract).then_inc(s.fil_steps, 1)
                dve.wait_ge(s.fil_steps, 3 * c + 3)
                for p in range(2):
                    v.scalar_tensor_tensor(out=x, in0=n, scalar=-SIN_C[p], in1=x, op0=ALU.mult, op1=ALU.add
                                           ).then_inc(s.angle_steps, 1)
                    dve.wait_ge(s.angle_steps, 3 * c + p + 1)
                v.scalar_tensor_tensor(out=x, in0=n, scalar=-SIN_C[2], in1=x, op0=ALU.mult, op1=ALU.add
                                       ).then_inc(s.angle_steps, 1)
                dve.wait_ge(s.angle_steps, 3 * c + 3)
                v.tensor_scalar(x, x, float(np.float32(3.1415925)), -float(np.float32(3.1415925)), ALU.min, ALU.max
                                ).then_inc(s.reduced, 1)
            split(dft[:, 0].rearrange("p r f m -> p (r f m)"), dft[:, 1].rearrange("p r f m -> p (r f m)"), dft_raw,
                  s.dft_split, 0)
            dve.wait_ge(s.loads_raw, RAW)
            split(rowb[:, 0, :], rowb[:, 1, :], row_raw, s.rows_split, 0)
            v.tensor_copy(oht[V:RB, :], oht_raw).then_inc(s.rows_split, 1)
            dve.wait_ge(s.squares, 6)
            v.tensor_tensor(mag, sqv[:, :, 0:KF], sqv[:, :, KF:2 * KF], ALU.add).then_inc(s.sums, 1)
            dve.wait_ge(s.roots, 1)
            v.tensor_scalar(inv, root, 1e-30, None, ALU.max).then_inc(s.mags, 1)
            dve.wait_ge(s.mags, 1)
            v.reciprocal(inv, inv).then_inc(s.mags, 1)
            dve.wait_ge(s.mags, 2)
            v.scalar_tensor_tensor(out=inv, in0=mag, scalar=0.5, in1=inv, op0=ALU.mult, op1=ALU.mult
                                   ).then_inc(s.mags, 1)
            dve.wait_ge(s.mags, 3)
            v.scalar_tensor_tensor(out=mag, in0=root, scalar=0.5, in1=inv, op0=ALU.mult, op1=ALU.add
                                   ).then_inc(s.mags, 1)
            for j in range(3):
                dve.wait_ge(s.kt_ready, 2 * j + 2)
                v.tensor_tensor(krt[:, :, j, :], bk[0:T, 4 + j, :].rearrange("p (r c) -> p r c", r=2),
                                decay[:, 2 * j:2 * j + 2, :], ALU.mult).then_inc(s.kt_done, 1)
                dve.wait_ge(s.kt_done, 3 * j + 1)
                split(vt[:, 0, :, j, :], vt[:, 1, :, j, :], krt[:, :, j, :], s.kt_done, 3 * j + 1)
            dve.wait_ge(s.loads_mats, MATS)
            G = lambda n: gate[:, :, n:n + 1]
            v.tensor_tensor(gbias[:, :, 1:2], G(1), G(2), ALU.add).then_inc(s.gbias_done, 1)
            dve.wait_ge(s.gbias_done, 1)
            v.tensor_tensor(gbias[:, :, 0:1], gbias[:, :, 1:2], G(3), ALU.add).then_inc(s.gbias_done, 1)
            dve.wait_ge(s.gbias_done, 2)
            v.tensor_tensor(gbias[:, :, 0:1], gbias[:, :, 0:1], G(0), ALU.mult).then_inc(s.gbias_done, 1)
            v.tensor_tensor(gbias[:, :, 1:2], gbias[:, :, 1:2], G(0), ALU.mult).then_inc(s.gbias_done, 1)
            dve.wait_ge(s.gbias_done, 4)
            v.tensor_tensor(gbias[:, :, 0:1], gbias[:, :, 0:1], G(4), ALU.add).then_inc(s.gbias_done, 1)
            v.tensor_tensor(gbias[:, :, 2:3], G(1), G(0), ALU.mult).then_inc(s.gbias_done, 1)
            v.memset(mhalf[:], -0.5).then_inc(s.pwr_const, 1)
            v.tensor_scalar(fb2[:], fb2[:], 0.5, None, ALU.mult).then_inc(s.pwr_const, 1)

            def filter_spectrum():
                dve.wait_ge(s.kraw_done, 6)
                for j in range(2):
                    re, im = vf[:, j, 0], vf[:, j, 1]
                    v.tensor_copy(kf[:, j, 0, 0, :], re[:, 0, :]).then_inc(s.kf_steps, 1)
                    v.tensor_copy(kf[:, j, 0, 1, :], im[:, 0, :]).then_inc(s.kf_steps, 1)
                    for d in (1, 2):
                        v.scalar_tensor_tensor(out=kf[:, j, d, 0, :], in0=im[:, d - 1, :], scalar=sgn[:, 1:2],
                                               in1=re[:, d, :], op0=ALU.mult, op1=ALU.add).then_inc(s.kf_steps, 1)
                        v.scalar_tensor_tensor(out=kf[:, j, d, 1, :], in0=re[:, d - 1, :], scalar=sgn[:, 0:1],
                                               in1=im[:, d, :], op0=ALU.mult, op1=ALU.add).then_inc(s.kf_steps, 1)

            def onehot(i):
                dve.wait_ge(s.ids_in, 16 * i + 16)
                dve.wait_ge(s.h_ready, 3 * i)
                v.tensor_scalar(oht[0:V, NPATCH:L], ids, iotap[:, 0:1], None, ALU.is_equal
                                ).then_inc(s.onehot_done, 1)
                src = rowe[:, i, :] if isinstance(i, int) else \
                    rowe[:, bass.ds(i, 1), :].rearrange("p b c -> p (b c)")
                split(rowb[V:V + FR, 0, DEMB:D], rowb[V:V + FR, 1, DEMB:D], src, s.onehot_done, 3 * i + 1)

            def moments(i, mv, rows_done, mv_done):
                dve.wait_ge(rows_done, 6 * i + 6)
                v.tensor_tensor(mv[:, :, 0], st[:, :, 1], st[:, :, 4], ALU.add).then_inc(mv_done, 1)
                v.tensor_tensor(dif[:, :, 0], st[:, :, 1], st[:, :, 4], ALU.subtract).then_inc(mv_done, 1)
                v.tensor_tensor(dif[:, :, 1], st[:, :, 2], st[:, :, 5], ALU.add).then_inc(mv_done, 1)
                dve.wait_ge(mv_done, 6 * i + 3)
                v.tensor_scalar(mv[:, :, 0], mv[:, :, 0], 0.5, None, ALU.mult).then_inc(mv_done, 1)
                v.scalar_tensor_tensor(out=dif[:, :, 0], in0=dif[:, :, 0], scalar=0.25, in1=dif[:, :, 0],
                                       op0=ALU.mult, op1=ALU.mult).then_inc(mv_done, 1)
                dve.wait_ge(mv_done, 6 * i + 5)
                v.scalar_tensor_tensor(out=mv[:, :, 1], in0=dif[:, :, 1], scalar=1.0 / D, in1=dif[:, :, 0],
                                       op0=ALU.mult, op1=ALU.add).then_inc(mv_done, 1)
                dve.wait_ge(mv_done, 6 * i + 6)

            def norm2(c):
                dve.wait_ge(s.res_done, c)
                moments(c, mv2, s.st2_done, s.mv2_done)
                v.tensor_scalar(va2[:, 0, :], mv2[:, :, 1], EPS, None, ALU.add).then_inc(s.va2_done, 1)
                v.tensor_scalar(va2[:, 1, :], mv2[:, :, 1], 1.0 + EPS, EPS * EPS, ALU.mult, ALU.add
                                ).then_inc(s.va2_done, 1)

            def apply2(c):
                dve.wait_ge(s.rs2_done, 2 * c + 2)
                dve.wait_ge(s.xt_ready, 3 * c + 3)
                for t in range(NT):
                    v.tensor_scalar(ln[:, t, :], h2[:, t, :], mv2[:, t, 0:1], rs2[:, 1, t:t + 1],
                                    ALU.subtract, ALU.mult).then_inc(s.ln2_done, 1)

            def norm1(i):
                for t in range(NT):
                    dve.wait_ge(s.h_done, 3 * i + t // 2 + 1)
                    v.bn_stats(st[:, t, :], h[:, t, :]).then_inc(s.st1_done, 1)
                moments(i, mv1, s.st1_done, s.mv1_done)
                v.tensor_scalar(va1[:], mv1[:, :, 1], EPS, None, ALU.add).then_inc(s.va1_done, 1)

            def apply1(i):
                dve.wait_ge(s.rs1_done, i + 1)
                dve.wait_ge(s.zt_ready, 3 * i)
                dve.wait_ge(s.ln2_done, 6 * i)
                for t in range(NT):
                    v.tensor_scalar(ln[:, t, :], h[:, t, :], mv1[:, t, 0:1], rs1[:, t:t + 1],
                                    ALU.subtract, ALU.mult).then_inc(s.ln1_done, 1)

            def xt_low(i):
                for j in range(3):
                    dve.wait_ge(s.xt_hi, 3 * i + j + 1)
                    cols = slice(2 + j * BL, 2 + (j + 1) * BL)
                    v.tensor_tensor(xt[:, 1, :, cols], bk[:, j, 0:2 * BL].rearrange("p (k t) -> p k t", k=2),
                                    xt[:, 0, :, cols].bitcast(F32), ALU.subtract).then_inc(s.xt_done, 1)

            def zt_low(c):
                for j in range(3):
                    dve.wait_ge(s.zt_hi, 3 * c + j + 1)
                    cols = slice(j * BL, (j + 1) * BL)
                    v.tensor_tensor(zt[:, 1, :, cols], bk[:, 4 + j, 0:2 * BL].rearrange("p (k t) -> p k t", k=2),
                                    zt[:, 0, :, cols].bitcast(F32), ALU.subtract).then_inc(s.zt_done, 1)

            def vt_low(i):
                for q in range(NQ):
                    dve.wait_ge(s.vt_hi, 3 * i + q + 1)
                    v.tensor_tensor(vt[:, 1, :, q, :], bk[0:T, (3 + q) % 4, :].rearrange("p (r c) -> p r c", r=2),
                                    vt[:, 0, :, q, :].bitcast(F32), ALU.subtract).then_inc(s.vt_done, 1)

            def taps(i):
                for u in range(12):
                    ch, m = u // 6, (4, 5, 2, 3, 0, 1)[u % 6]
                    dst = uc[:, m, ch * CH:(ch + 1) * CH]
                    dve.wait_ge(s.u_first, 12 * i + u + 1)
                    v.scalar_tensor_tensor(out=dst, in0=bk[:, (3 + u) % 4, 1:CH + 1], scalar=gate[:, m, 2:3],
                                           in1=dst, op0=ALU.mult, op1=ALU.add).then_inc(s.u_tap1, 1)
                    dve.wait_ge(s.u_tap1, 12 * i + u + 1)
                    v.scalar_tensor_tensor(out=dst, in0=bk[:, (3 + u) % 4, 0:CH], scalar=gate[:, m, 1:2],
                                           in1=dst, op0=ALU.mult, op1=ALU.add).then_inc(s.u_done, 1)
                    if u == 5:
                        dve.wait_ge(s.u_done, 12 * i + 6)
                        v.tensor_tensor(uc[:, :, 0:2], uc[:, :, 0:2], gbias[:, :, 1:3], ALU.subtract
                                        ).then_inc(s.u_edge, 1)

            def product(i, j):
                base = 28 * i + 14 * j
                dve.wait_ge(s.vf_done, 6 * i + 3 + 3 * j)
                if j == 0:
                    dve.wait_ge(s.y_ready, 3 * i)
                    dve.wait_ge(s.res_done, i)
                    dve.wait_ge(s.xt_ready, 3 * i + 3)
                n = 0
                for d in range(NQ):
                    nq = NQ - d
                    x = xf[:, j, :, d:NQ, :]
                    t0 = x if d == 0 else ta[:, :, 0:nq, :]
                    t1 = tb[:, :, 0:nq, :]
                    for part, t in ((0, t0), (1, t1)):
                        if d == 2 and part == 0:
                            dve.wait_ge(s.pw_done, base + 7)
                        if d and part == 1:
                            dve.wait_ge(s.pw_done, base + 5 * d - 1)
                        v.tensor_tensor(t, bc(vf[:, j, part, 0:nq, :], 1, 2), bc(kf[:, j, d, :, :], 2, nq), ALU.mult
                                        ).then_inc(s.pw_done, 1)
                        n += 1
                    dve.wait_ge(s.pw_done, base + n)
                    if d:
                        v.tensor_tensor(x, x, t0, ALU.add).then_inc(s.pw_done, 1)
                        n += 1
                        dve.wait_ge(s.pw_done, base + n)
                    v.tensor_tensor(x[:, 0], x[:, 0], t1[:, 1], ALU.subtract).then_inc(s.pw_done, 1)
                    v.tensor_tensor(x[:, 1], x[:, 1], t1[:, 0], ALU.add).then_inc(s.pw_done, 1)
                    n += 2
                dve.wait_ge(s.pw_done, base + n)

            def finish(c, lo, hi):
                for j in range(lo, hi):
                    dve.wait_ge(s.f2_ready, 3 * c + j + 1)
                    if j == 0:
                        dve.wait_ge(s.res_done, c + 1)
                        dve.wait_ge(s.out_done, 48 * c)
                    v.scalar_tensor_tensor(out=ob[:, 2 * j:2 * j + 2, :].rearrange("p t c -> p (t c)"),
                                           in0=bk[0:T, 4 + (3 + j) % 4, :], scalar=0.5,
                                           in1=res[:, 2 * j:2 * j + 2, :].rearrange("p t c -> p (t c)"),
                                           op0=ALU.mult, op1=ALU.add).then_inc(s.ob_done, 1)

            def gate_y(i):
                dve.wait_ge(s.u_done, 12 * i + 12)
                dve.wait_ge(s.u_edge, i + 1)
                for q in range(NQ):
                    dve.wait_ge(s.y_ready, 3 * i + q + 1)
                    for k in range(2):
                        v.scalar_tensor_tensor(out=yt[:, k, q * BL:(q + 1) * BL], in0=bk[:, q, k * BL:(k + 1) * BL],
                                               scalar=fbias[:, k:k + 1], in1=uc[:, k, q * BL:(q + 1) * BL],
                                               op0=ALU.add, op1=ALU.mult).then_inc(s.y_done, 1)

            def residual(i):
                for j in range(3):
                    dve.wait_ge(s.o_ready, 3 * i + j + 1)
                    if j == 0:
                        dve.wait_ge(s.hb_done, i + 1)
                        dve.wait_ge(s.res_done, i)
                    v.tensor_tensor(h2[:, 2 * j:2 * j + 2, :], bk[0:T, (3 + j) % 4, :].rearrange(
                        "p (t c) -> p t c", t=2), h[:, 2 * j:2 * j + 2, :], ALU.add).then_inc(s.h2_done, 1)
                    dve.wait_ge(s.h2_done, 3 * i + j + 1)
                    for t in (2 * j, 2 * j + 1):
                        v.bn_stats(st[:, t, :], h2[:, t, :]).then_inc(s.st2_done, 1)

            def step(i, front, back):
                c = i - 1
                if front:
                    onehot(i)
                if back:
                    apply2(c)
                    zt_low(c)
                if front:
                    norm1(i)
                    apply1(i)
                    xt_low(i)
                    taps(i)
                    vt_low(i)
                    product(i, 0)
                    product(i, 1)
                if back:
                    finish(c, 0, 2)
                if front:
                    gate_y(i)
                    residual(i)
                    norm2(i)
                if back:
                    finish(c, 2, 3)

            dve.wait_ge(s.rows_in, 16 * 4)
            onehot(0)
            norm1(0)
            apply1(0)
            xt_low(0)
            dve.wait_ge(s.gbias_done, 6)
            taps(0)
            filter_spectrum()
            vt_low(0)
            dve.wait_ge(s.loads_q1, 32)
            v.scalar_tensor_tensor(out=scale, in0=quant, scalar=-128.0, in1=scale, op0=ALU.add, op1=ALU.mult
                                   ).then_inc(s.fc1_raw, 1)
            dve.wait_ge(s.kf_steps, 12)
            product(0, 0)
            product(0, 1)
            dve.wait_ge(s.fc1_bias, 1)
            for k in range(2):
                v.tensor_scalar(fc1_raw[:, k, :], fc1_raw[:, k, :], gamma[:, k:k + 1], None, ALU.mult
                                ).then_inc(s.fc1_fold, 1)
            v.tensor_tensor(fb1[:], bk[:, 7, 0:8], fb1[:], ALU.add).then_inc(s.fc1_fold, 1)
            gate_y(0)
            residual(0)
            norm2(0)
            dve.wait_ge(s.loads_q2, 32)
            v.scalar_tensor_tensor(out=fc2[:, :, :].rearrange("p a n -> p (a n)"), in0=quant, scalar=-128.0,
                                   in1=scale, op0=ALU.add, op1=ALU.mult).then_inc(s.deq, 1)
            step(1, True, True)
            with dve.Fori(2, B) as i:
                step(i, True, True)
            step(B, False, True)

        @block.gpsimd
        def _(pool):
            g = nc.gpsimd
            pool.wait_ge(s.loads_up, UP)
            g.tensor_copy(win[:, 0], win_raw).then_inc(s.win_split, 1)
            pool.wait_ge(s.win_split, 1)
            g.tensor_tensor(win[:, 1], win_raw, win[:, 0].bitcast(F32), ALU.subtract).then_inc(s.win_split, 1)
            pool.wait_ge(s.pwr_const, 2)
            pool.wait_ge(s.loads_mats, MATS)

            def step(i, front, back):
                c = i - 1
                if back:
                    pool.wait_ge(s.va2_done, 2 * i)
                    g.tensor_tensor(rs2[:, 0, :], va2[:, 0, :], mhalf[:], ALU.pow).then_inc(s.rs2_done, 1)
                    pool.wait_ge(s.rs2_done, 2 * i - 1)
                    pool.wait_ge(s.ob_done, 3 * c)
                    pool.wait_ge(s.mv2_done, 6 * i)
                    g.tensor_tensor(rs2[:, 1, :], va2[:, 1, :], mhalf[:], ALU.pow).then_inc(s.rs2_done, 1)
                    for t in range(NT):
                        g.tensor_scalar(res[:, t, :], h2[:, t, :], mv2[:, t, 0:1], rs2[:, 0, t:t + 1],
                                        ALU.subtract, ALU.mult).then_inc(s.r_done, 1)
                if front:
                    pool.wait_ge(s.va1_done, i + 1)
                    g.tensor_tensor(rs1[:], va1[:], mhalf[:], ALU.pow).then_inc(s.rs1_done, 1)
                if back:
                    pool.wait_ge(s.r_done, 6 * i)
                    g.tensor_tensor(res[:], res[:], h2[:], ALU.add).then_inc(s.rb_done, 1)
                    pool.wait_ge(s.rb_done, i)
                    g.tensor_tensor(res[:], res[:], bc(fb2[:], 1, NT), ALU.add).then_inc(s.res_done, 1)
                if front:
                    pool.wait_ge(s.ln1_done, 6 * i + 6)
                    g.tensor_tensor(h, h, bc(bout[:], 1, NT), ALU.add).then_inc(s.hb_done, 1)
                    for ch in range(2):
                        pool.wait_ge(s.u_done, 12 * i + 6 * ch + 4)
                        pool.wait_ge(s.u_edge, i + 1)
                        vv = uc[:, 4:6, ch * CH:(ch + 1) * CH]
                        g.tensor_tensor(vv, vv, uc[:, 2:4, ch * CH:(ch + 1) * CH], ALU.mult
                                        ).then_inc(s.v_done, 1)

            step(0, True, False)
            pool.wait_ge(s.fc1_fold, 2)
            g.tensor_copy(fc1[:, 0], fc1_raw).then_inc(s.fc1_split, 1)
            pool.wait_ge(s.fc1_split, 1)
            g.tensor_tensor(fc1[:, 1], fc1_raw, fc1[:, 0].bitcast(F32), ALU.subtract).then_inc(s.fc1_split, 1)
            step(1, True, True)
            with pool.Fori(2, B) as i:
                step(i, True, True)
            step(B, False, True)


def constants():
    f64 = np.float64
    n = np.arange(NF, dtype=f64)
    k = np.arange(KF, dtype=f64)
    w = 2.0 * np.pi * n[:, None] * k[None, :] / NF
    stft = np.concatenate([np.cos(w), -np.sin(w)], axis=1)
    t = np.arange(L, dtype=np.float32) / np.float32(L - 1)
    phase = np.float32(1e-4) * (np.float32(2.0 * np.pi) * np.arange(L, dtype=np.float32) / np.float32(L))
    features = np.stack([t, np.cos(phase), -np.sin(phase), np.ones_like(t)])[:, ::-1]
    delta = np.abs(np.linspace(np.log(0.01) / 0.3, np.log(0.01) / 1.5, D).astype(np.float32))
    decay = np.exp(-t[:, None] * delta[None, :])[::-1].reshape(NT, T, D).transpose(1, 0, 2)
    f = np.arange(BL, dtype=f64)
    th = np.pi * (2 * f[None, :] + 1) * np.arange(BL, dtype=f64)[:, None] / ND
    fwd = np.stack([np.cos(th), -np.sin(th)], axis=0).reshape(2, 2, T, 2, T)
    dft = fwd.transpose(2, 1, 3, 0, 4).reshape(T, 8 * T)
    inv = np.stack([np.cos(th), -np.sin(th)], axis=0) * (2.0 / ND)
    idft = inv.reshape(2, BL, 2, T).transpose(3, 2, 0, 1).reshape(T, 4, BL)
    sg = (-1.0) ** np.arange(T)
    coord = np.clip((np.arange(NTXT) + 0.5) * (FR / NTXT) - 0.5, 0.0, FR - 1.0)
    i0 = np.floor(coord).astype(int)
    i1 = np.minimum(i0 + 1, FR - 1)
    wt = (coord - i0).astype(np.float32)
    rows = np.zeros((FR + 2, L), np.float32)
    cols = NPATCH + np.arange(NTXT)
    np.add.at(rows, (i0, cols), np.float32(1.0) - wt)
    np.add.at(rows, (i1, cols), wt)
    rows[FR, NPATCH:] = 1.0
    rows[FR + 1, :NPATCH] = 1.0
    c = dict(stft_mat=stft, features=features, decay=decay, dft=dft, idft=idft,
             signs=np.stack([sg, -sg], axis=1), interp=rows, ident=np.eye(128),
             iota_row=np.tile(np.arange(V), (NF, 1)), iota_col=np.arange(V)[:, None])
    return {k: np.ascontiguousarray(v, dtype=np.float32) for k, v in c.items()}


def layout(i):
    x = i["x"].reshape(B, 3, 14, 16, 14, 16).transpose(0, 1, 3, 5, 2, 4).reshape(B, KP // 128, 128, NPATCH)
    pos = np.arange(FR)[None, :] * NF + np.arange(NF)[:, None] - NF // 2
    pos = np.abs(pos)
    pos = np.where(pos >= NTXT, 2 * (NTXT - 1) - pos, pos)
    frames = i["x_txt"][:, pos].transpose(1, 0, 2).reshape(NF, 2, 4 * FR).transpose(0, 2, 1).reshape(NF, B * FR)
    tiles = lambda w, k=128: w.reshape(w.shape[0] // k, k, w.shape[1]).transpose(1, 0, 2)
    cols = lambda v: v.reshape(-1, 128).T
    gate = np.stack([cols(i["L0_attn_b_in"]), *(cols(i["L0_attn_short_w"][:, t]) for t in range(3)),
                     cols(i["L0_attn_short_b"])], axis=2)
    o = dict(
        x=x.transpose(0, 2, 1, 3), ids=np.repeat(i["x_txt"][:, None, :], V, axis=1), ids_frames=frames,
        window=i["L0_txt_window"][:, None], proj=i["L0_txt_proj_w"].reshape(DST, KF, V).transpose(2, 1, 0),
        table=i["L0_txt_emb_table"], proj_bias=i["L0_txt_proj_b"][None, :],
        tok_bias=i["L0_tok_b2"][None, :],
        w1=tiles(i["L0_tok_W1"]), b1=cols(i["L0_tok_b1"]), w2=tiles(i["L0_tok_W2"]),
        win=tiles(i["L0_attn_W_in"]), gate=gate, fbias=cols(i["L0_attn_filter_bias"]),
        wout=tiles(i["L0_attn_W_out"]), bout=i["L0_attn_b_out"], gamma=cols(i["L0_ffn_ln_gamma"]),
        beta=cols(i["L0_ffn_ln_beta"]), fb1=cols(i["L0_ffn_fc1_bias"]), fb2=i["L0_ffn_fc2_bias"],
        fc1_q=tiles(i["L0_ffn_fc1_q"]).reshape(128, -1), fc2_q=tiles(i["L0_ffn_fc2_q"]).reshape(128, -1),
        fc1_scales=i["L0_ffn_fc1_scales"].reshape(-1), fc2_scales=i["L0_ffn_fc2_scales"].reshape(-1),
        L0_attn_W1=i["L0_attn_W1"], L0_attn_W2=i["L0_attn_W2"], L0_attn_W3=i["L0_attn_W3"],
        f_b1=i["L0_attn_b1"][None, :], f_b2=i["L0_attn_b2"][None, :], f_b3=i["L0_attn_b3"][None, :],
        f_f1=i["L0_attn_f1"][:, None], f_f2=i["L0_attn_f2"][:, None])
    return {k: np.ascontiguousarray(v) for k, v in o.items()}


def kernel(**inputs):
    import concourse.bacc as bacc
    from concourse.bass_utils import run_bass_kernel_spmd

    nc = bacc.Bacc("TRN2", target_bir_lowering=False, num_devices=1)
    data = {**layout({k: np.asarray(v) for k, v in inputs.items()}), **constants()}
    arrays = {"in_" + k: v for k, v in data.items()}
    aps = {k: nc.dram_tensor("in_" + k, v.shape, mybir.dt.from_np(v.dtype), kind="ExternalInput").ap()
           for k, v in data.items()}
    out = nc.dram_tensor("out", (B, L, D), F32, kind="ExternalOutput").ap()
    program(nc, aps, out)
    r = run_bass_kernel_spmd(nc, [arrays], core_ids=[0])
    return r.results[0]["out"]
```

```python
from contextlib import ExitStack

import numpy as np

import concourse.bass as bass
from concourse import mybir

F32 = mybir.dt.float32
F32R = mybir.dt.float32r
I32 = mybir.dt.int32
ALU = mybir.AluOpType
ACT = mybir.ActivationFunctionType

B = 8
NPATCH = 196
NTXT = 512
L = NPATCH + NTXT
D = 256
KP = 768
WID = 3 * D
HID = 64
FF = 1024
V = 64
DEMB = 179
DST = D - DEMB
NF = 64
FR = 1 + NTXT // NF
KF = NF // 2 + 1
T = 118
NT = L // T
NQ = 3
BL = L // NQ
ND = 2 * BL
CH = L // 2
RB = V + FR + 2
EPS = 1e-5
SPREAD = ((0, T // 16 * 16), (T // 16 * 16, T))
SMALL = dict(ident=128, b1=2, fbias=2, gamma=2, beta=2, fb1=8, gate=30, signs=2, iota_col=1)
MAGIC = 1.5 * 2.0 ** 23
SIN_C = (6.28125, 0.0019350051879882812, 3.019916e-07)


PARTS = ((0, 0), (0, 1), (1, 0))


def bc(ap, axis, n):
    ap = ap.unsqueeze(axis)
    shape = list(ap.shape)
    shape[axis] = n
    return ap.broadcast_to(shape)


class Semaphores:

    def __init__(self, sem):
        self.loads_text = sem("loads_text")
        self.loads_filter = sem("loads_filter")
        self.loads_spectrum = sem("loads_spectrum")
        self.loads_proj = sem("loads_proj")
        self.loads_mats = sem("loads_mats")
        self.loads_up = sem("loads_up")
        self.loads_raw = sem("loads_raw")
        self.loads_q1 = sem("loads_q1")
        self.loads_q2 = sem("loads_q2")
        self.rows_in = sem("rows_in")
        self.xp_in = sem("xp_in")
        self.ids_in = sem("ids_in")
        self.out_done = sem("out_done")
        self.memsets = sem("memsets")
        self.window_done = sem("window_done")
        self.onehot_frames = sem("onehot_frames")
        self.stft = sem("stft")
        self.squares = sem("squares")
        self.sums = sem("sums")
        self.roots = sem("roots")
        self.mags = sem("mags")
        self.enc_ready = sem("enc_ready")
        self.enc_done = sem("enc_done")
        self.fil_ready = sem("fil_ready")
        self.fil_steps = sem("fil_steps")
        self.angle_steps = sem("angle_steps")
        self.reduced = sem("reduced")
        self.sin_done = sem("sin_done")
        self.kt_ready = sem("kt_ready")
        self.kt_done = sem("kt_done")
        self.kraw_ready = sem("kraw_ready")
        self.kraw_done = sem("kraw_done")
        self.kf_steps = sem("kf_steps")
        self.dft_split = sem("dft_split")
        self.rows_split = sem("rows_split")
        self.win_split = sem("win_split")
        self.fc1_split = sem("fc1_split")
        self.fc1_raw = sem("fc1_raw")
        self.fc1_bias = sem("fc1_bias")
        self.fc1_fold = sem("fc1_fold")
        self.fc2_raw = sem("fc2_raw")
        self.fc2_split = sem("fc2_split")
        self.gbias_done = sem("gbias_done")
        self.pwr_const = sem("pwr_const")
        self.h1_ready = sem("h1_ready")
        self.h1_done = sem("h1_done")
        self.onehot_done = sem("onehot_done")
        self.h_ready = sem("h_ready")
        self.h_done = sem("h_done")
        self.h_bias_done = sem("h_bias_done")
        self.st1_done = sem("st1_done")
        self.mv1_done = sem("mv1_done")
        self.va1_done = sem("va1_done")
        self.rs1_done = sem("rs1_done")
        self.ln1_done = sem("ln1_done")
        self.xt_ready = sem("xt_ready")
        self.xt_hi = sem("xt_hi")
        self.xt_done = sem("xt_done")
        self.u_ready = sem("u_ready")
        self.u_first = sem("u_first")
        self.u_tap1 = sem("u_tap1")
        self.u_done = sem("u_done")
        self.u_edge = sem("u_edge")
        self.v_done = sem("v_done")
        self.vt_ready = sem("vt_ready")
        self.vt_hi = sem("vt_hi")
        self.vt_done = sem("vt_done")
        self.vf_ready = sem("vf_ready")
        self.vf_done = sem("vf_done")
        self.near_done = sem("near_done")
        self.far_done = sem("far_done")
        self.pw_done = sem("pw_done")
        self.y_ready = sem("y_ready")
        self.y_done = sem("y_done")
        self.o_ready = sem("o_ready")
        self.h2_done = sem("h2_done")
        self.st2_done = sem("st2_done")
        self.mv2_done = sem("mv2_done")
        self.va2_done = sem("va2_done")
        self.rs2_done = sem("rs2_done")
        self.ln2_done = sem("ln2_done")
        self.coef_done = sem("coef_done")
        self.res_norm_done = sem("res_norm_done")
        self.res_done = sem("res_done")
        self.zt_ready = sem("zt_ready")
        self.zt_hi = sem("zt_hi")
        self.zt_done = sem("zt_done")
        self.f1_ready = sem("f1_ready")
        self.f1_done = sem("f1_done")
        self.at_lo_first = sem("at_lo_first")
        self.at_lo = sem("at_lo")
        self.f2_ready = sem("f2_ready")
        self.out_rows_done = sem("out_rows_done")


def program(nc, a, out):
    with ExitStack() as ctx:
        def sb(name, shape, dt=F32):
            return ctx.enter_context(nc.sbuf_tensor(name, shape, dt))

        def sem(name):
            return ctx.enter_context(nc.semaphore(name))

        bk = ctx.enter_context(nc.psum_tensor("banks", [128, 8, 512], F32))
        up_bank = lambda u: (7, 4, 5, 6)[u % 4] if u < 8 else (5, 6, 7)[(u - 8) % 3]
        down_bank = lambda t: (7, 4, 5)[t // 2]

        small = sb("small", [128, sum(SMALL.values())])
        w1 = sb("w1", [128, KP // 128, D])
        w2 = sb("w2", [128, 2, D])
        win = sb("win", [128, 2, 2, WID], F32R)
        gbias = sb("gbias", [128, 6, 3])
        wout = sb("wout", [128, 2, D])
        biases = sb("biases", [T, 2, D])
        fc1 = sb("fc1", [128, 2, 2, FF], F32R)
        fc2 = sb("fc2", [128, 2, 8, D], F32R)
        dft = sb("dft", [T, 2, 2, 4, T], F32R)
        idft = sb("idft", [T, 4, BL])
        kf = sb("kf", [T, 2, NQ, 2, D])
        rowb = sb("rowb", [RB, 2, D], F32R)
        mhalf = sb("mhalf", [T, NT])

        ids_all = sb("ids", [V + FR, B * DST])
        h1t = sb("h1t", [128, 2, NPATCH])
        oht = sb("oht", [RB, L], F32R)
        h_all = sb("h", [128, NT * D])
        ln = sb("ln", [T, NT, D])
        xt = sb("xt", [128, 2, 2, L + 2], F32R)
        uc_all = sb("uc", [128, 6 * L])
        with nc.sbuf_tensor("vt", [T, 2, 2, NQ, D], F32R) as vt:
            pass
        xf1 = sb("xf1", [T, 2, NQ, D])
        xp = sb("xp", [128, KP // 128, NPATCH])
        frame_consts = sb("frame_consts", [128, (4 - 2) * NQ * D - KP // 128 * NPATCH])
        xf0 = sb("xf0", [T, 2, NQ, D])
        vf_all = sb("vf", [128, 4 * NQ * D])
        h2 = sb("h2", [T, NT, D])
        res = sb("res", [T, NT, D])
        with nc.sbuf_tensor("proj", [128, KF, DST], F32) as proj:
            pass
        zt = sb("zt", [128, 2, 2, L], F32R)
        with nc.sbuf_tensor("setup", [128, 2 * 8 * CH], F32) as setup_all:
            pass
        at = sb("at", [128, 2, 8, CH], F32R)
        full = sb("full", [128, 2, CH])
        st = sb("st", [T, NT, 6])
        dif = sb("dif", [T, NT, 2])
        mv1 = sb("mv1", [T, NT, 2])
        va1 = sb("va1", [T, NT])
        rs1 = sb("rs1", [T, NT])
        mv2 = sb("mv2", [T, NT, 2])
        va2 = sb("va2", [T, 2, NT])
        rs2 = sb("rs2", [T, 2, NT])
        coef = sb("coef", [T, 2, NT])

        at_column, view = 0, {}
        for name, width in SMALL.items():
            view[name] = small[:, at_column:at_column + width]
            at_column += width
        ident, b1, fbias, gamma, beta, fb1 = (view[n] for n in ("ident", "b1", "fbias", "gamma", "beta", "fb1"))
        gate = view["gate"].rearrange("p (m n) -> p m n", m=6)
        sgn = view["signs"][0:T, :]
        iotap = view["iota_col"][0:V, :]
        bout, fb2 = biases[:, 0, :], biases[:, 1, :]
        ids = ids_all[0:V, 0:NTXT].bitcast(I32)
        rowe = ids_all[V:V + FR, :].rearrange("p (b c) -> p b c", b=B)
        h = h_all[0:T, :].rearrange("p (t c) -> p t c", t=NT)
        vf = vf_all[0:T, :].rearrange("p (j r q c) -> p j r q c", j=2, r=2, q=NQ)
        yt = vf_all[:, NT * D:NT * D + 2 * L].rearrange("p (h t) -> p h t", h=2)
        ta = h2[:, :, :].rearrange("p (r q) c -> p r q c", r=2)
        tb = ln[:, :, :].rearrange("p (r q) c -> p r q c", r=2)
        uc = uc_all[:, :].rearrange("p (m t) -> p m t", m=6)
        xf = (xf0, xf1)
        near = uc_all[0:T, 2 * L:2 * L + 4 * D].rearrange("p (b q c) -> p b q c", b=2, q=2)
        far = uc_all[0:T, 2 * L:2 * L + 8 * D].rearrange("p (j a b q c) -> p j a b q c", j=2, a=2, b=2, q=1)

        frames_in = frame_consts[0:NF, 0:V + 2 * KF + 1]
        iotar, dftw, wnd = frames_in[:, 0:V], frames_in[:, V:V + 2 * KF], frames_in[:, V + 2 * KF:V + 2 * KF + 1]
        ln_all = ln[:, :, :].rearrange("p t c -> p (t c)")
        enc = ln_all[0:36, 0:2 * DST].rearrange("p (g o) -> p g o", g=2)
        hidden = ln_all[0:HID + 1, 2 * DST:2 * DST + HID + D + 2]
        fw2, fw3, ffreq = hidden[:, 0:HID], hidden[:, HID:HID + D], hidden[0:HID, HID + D:HID + D + 2]
        first = h2[0:4, :, :].rearrange("p t c -> p (t c)")[:, 0:L + HID]
        pet, fw1 = first[:, 0:L], first[:, L:L + HID]
        ohf = setup_all[0:NF, 0:FR * B * V].rearrange("p (f v) -> p f v", v=V)
        quant = setup_all[:, 0:2 * FF].bitcast(I32)
        scale = setup_all[:, 2 * FF:4 * FF]
        idf = ids[:, 0:FR * B]
        sqv = uc_all[:, 0:36 * 2 * KF].rearrange("p (g k) -> p g k", g=36)
        mag = h_all[:, 0:36 * KF].rearrange("p (g k) -> p g k", g=36)
        root, inv = sqv[:, :, 0:KF], sqv[:, :, KF:2 * KF]
        fh1 = uc_all[0:HID + 1, 36 * 2 * KF:36 * 2 * KF + L]
        fh2 = uc_all[0:HID + 1, 36 * 2 * KF + L:36 * 2 * KF + 2 * L]
        ang = vf_all[0:HID, 0:L].rearrange("p (c t) -> p c t", c=2)
        turns = vf_all[0:HID, L:2 * L].rearrange("p (c t) -> p c t", c=2)
        win_raw = vf_all[:, 2 * WID:4 * WID].rearrange("p (k n) -> p k n", k=2)
        dft_raw = ln_all[:, 2 * D:2 * D + 8 * T]
        row_raw = setup_all[0:RB, FR * B * V:FR * B * V + D]
        oht_raw = setup_all[V:RB, FR * B * V + D:FR * B * V + D + L]
        fc1_raw = scale.rearrange("p (k n) -> p k n", k=2)
        decay = res[:, :, :]
        krt = h2[:, :, :].rearrange("p (r q) c -> p r q c", r=2)

        text_loads = [(idf, a["ids_frames"]), (frames_in, a["frame_consts"])]
        filter_loads = [(first, a["filter_first"]), (hidden, a["filter_hidden"])]
        spectrum_loads = [(dft_raw[lo:hi], a["dft"][lo:hi]) for lo, hi in SPREAD] + \
            [(decay[lo:hi], a["decay"][lo:hi]) for lo, hi in SPREAD]
        up_loads = [(small[:], a["small"]), (w1[:], a["w1"]), (w2[:], a["w2"]), (win_raw, a["win"])]
        proj_loads = [(proj[0:V], a["proj"]), (proj[V:2 * V], a["proj"])]
        raw_loads = [(row_raw, a["rows"]), (oht_raw, a["interp"])]
        mat_loads = [(idft[lo:hi], a["idft"][lo:hi]) for lo, hi in SPREAD] + [
            (wout[:], a["wout"]), (biases[:].rearrange("p a c -> p (a c)"), a["biases"].partition_broadcast(T))]
        TEXT, FILTER, SPECTRUM = 16 * len(text_loads), 16 * len(filter_loads), 16 * len(spectrum_loads)
        UP, PROJ = 16 * len(up_loads), 16 * len(proj_loads)
        RAW, MATS = 16 * len(raw_loads), 16 * len(mat_loads)
        PARTS_K = 3

        s = Semaphores(sem)
        block = ctx.enter_context(nc.Block())
        out_v = out.rearrange("b (t p) c -> b p t c", p=T)

        @block.sync
        def _(sp):
            for dst, src in text_loads:
                sp.dma_start(dst, src).then_inc(s.loads_text, 16)
            sp.dma_start(xp[:], a["x"][0]).then_inc(s.xp_in, 16)
            for dst, src in up_loads[0:2]:
                sp.dma_start(dst, src).then_inc(s.loads_up, 16)
            for dst, src in proj_loads:
                sp.dma_start(dst, src).then_inc(s.loads_proj, 16)
            for dst, src in raw_loads:
                sp.dma_start(dst, src).then_inc(s.loads_raw, 16)
            for dst, src in up_loads[2:4]:
                sp.dma_start(dst, src).then_inc(s.loads_up, 16)
            for dst, src in mat_loads:
                sp.dma_start(dst, src).then_inc(s.loads_mats, 16)
            sp.wait_ge(s.onehot_frames, 3)
            sp.dma_start(ids, a["ids"][0]).then_inc(s.ids_in, 16)
            sp.wait_ge(s.stft, 6)
            sp.dma_start(quant, a["fc1_q"]).then_inc(s.loads_q1, 16)
            sp.dma_start(scale, a["fc1_scales"].partition_broadcast(128)).then_inc(s.loads_q1, 16)
            sp.wait_ge(s.enc_done, 2)
            for bb in range(4):
                sp.dma_start(rowe[:, bb::4, :],
                             enc[FR * bb:FR * bb + FR, :, :]).then_inc(s.rows_in, 16)
            sp.wait_ge(s.fc1_split, 2)
            sp.dma_start(quant, a["fc2_q"]).then_inc(s.loads_q2, 16)
            sp.dma_start(scale, a["fc2_scales"].partition_broadcast(128)).then_inc(s.loads_q2, 16)

            def step(i):
                c = i - 1
                for j in range(3):
                    sp.wait_ge(s.out_rows_done, 3 * c + j + 1)
                    sp.dma_start(out_v[c, :, 2 * j:2 * j + 2, :] if isinstance(c, int)
                                 else out_v[bass.ds(c, 1), :, 2 * j:2 * j + 2, :].rearrange("b p t c -> (b p) t c"),
                                 res[:, 2 * j:2 * j + 2, :]).then_inc(s.out_done, 16)

            def prefetch_ids(i):
                n = i + 1
                sp.wait_ge(s.onehot_done, 3 * i + 1)
                sp.dma_start(ids, a["ids"][n] if isinstance(n, int) else
                             a["ids"][bass.ds(n, 1)].rearrange("b p t -> (b p) t")).then_inc(s.ids_in, 16)

            def prefetch_x(i):
                n = i + 1
                sp.wait_ge(s.vf_ready, 6 * i + 6)
                sp.dma_start(xp[:], a["x"][n] if isinstance(n, int) else
                             a["x"][bass.ds(n, 1)].rearrange("b p k t -> (b p) k t")).then_inc(s.xp_in, 16)

            prefetch_ids(0)
            prefetch_x(0)
            with sp.Fori(1, B - 1) as i:
                prefetch_ids(i)
                prefetch_x(i)
                step(i)
            step(B - 1)
            for j in range(3):
                sp.wait_ge(s.out_rows_done, 3 * (B - 1) + j + 1)
                for lo, hi in SPREAD:
                    sp.dma_start(out_v[B - 1, lo:hi, 2 * j:2 * j + 2, :], res[lo:hi, 2 * j:2 * j + 2, :]
                                 ).then_inc(s.out_done, 16)
            sp.wait_ge(s.out_done, 16 * 3 * (B + 1))

        @block.tensor
        def _(pe):
            mm = nc.tensor.matmul

            def spectrum(ready, copied, i, j, bank0):
                for part in range(3):
                    n = 3 * j + part
                    if n >= 4:
                        pe.wait_ge(copied, 6 * i + n - 3)
                    bank = bk[0:T, bank0(n), :]
                    pieces = [(part, bank, 0, 2)] if part < 2 else \
                        [(0, bank[:, 0:D], 2, 3), (1, bank[:, D:2 * D], 2, 3)]
                    for p, dst, q0, q1 in pieces:
                        for r in range(2):
                            for wp, xq in PARTS:
                                o = mm(dst, dft[:, wp, r, 2 * j + p, :],
                                       vt[:, xq, r, q0:q1, :].rearrange("p q c -> p (q c)"),
                                       start=(r == 0 and (wp, xq) == PARTS[0]), stop=(r == 1 and (wp, xq) == PARTS[-1]))
                    o.then_inc(ready, 1)

            def patches_up(i):
                pe.wait_ge(s.xp_in, 16 * i + 16)
                for m in range(2):
                    for k in range(KP // 128):
                        o = mm(bk[:, 0, m * NPATCH:(m + 1) * NPATCH], w1[:, k, m * 128:(m + 1) * 128], xp[:, k, :],
                               start=(k == 0), stop=(k == KP // 128 - 1))
                    o.then_inc(s.h1_ready, 1)

            def rows(i):
                pe.wait_ge(s.onehot_done, 3 * i + 3)
                pe.wait_ge(s.h2_done, 3 * i)
                for t in range(NT):
                    dst = bk[0:T, 1 + t // 2, (t % 2) * D:(t % 2 + 1) * D]
                    if t == 0:
                        pe.wait_ge(s.h1_done, 2 * i + 2)
                    n = min(max(NPATCH - t * T, 0), T)
                    mm(dst, oht[:, t * T:(t + 1) * T], rowb[:, 0, :], start=True, stop=False)
                    for k in range(2 if n else 0):
                        mm(dst[0:n], h1t[:, k, t * T:t * T + n], w2[:, k, :], start=False, stop=False)
                    o = mm(dst, oht[:, t * T:(t + 1) * T], rowb[:, 1, :], start=False, stop=True)
                    if t % 2:
                        o.then_inc(s.h_ready, 1)

            def turn_pair(j, bank):
                for t in range(2):
                    for k in range(2):
                        o = nc.tensor.transpose(bk[:, bank, k * BL + t * T:k * BL + (t + 1) * T],
                                                ln[:, 2 * j + t, k * 128:(k + 1) * 128], ident[0:T, 0:T])
                return o

            def turn_front(i):
                for j in range(3):
                    pe.wait_ge(s.ln1_done, 6 * i + 2 * j + 2)
                    if j:
                        pe.wait_ge(s.h_done, 3 * i + j)
                    turn_pair(j, j).then_inc(s.xt_ready, 1)

            def gates(i, lo, hi):
                for u in range(lo, hi):
                    c, m = u // 6, (4, 5, 2, 3, 0, 1)[u % 6]
                    pe.wait_ge(s.xt_done, 3 * i + 2 + c)
                    if u == 0:
                        pe.wait_ge(s.h_done, 3 * i + 3)
                    if u == 3:
                        pe.wait_ge(s.xt_done, 3 * i + 3)
                    if u >= 4:
                        pe.wait_ge(s.u_done, 12 * i + u - 3)
                    for k in range(2):
                        for wp, xq in PARTS:
                            o = mm(bk[:, (3 + u) % 4, 0:CH + 2], win[:, wp, k, m * 128:(m + 1) * 128],
                                   xt[:, xq, k, c * CH:c * CH + CH + 2],
                                   start=(k == 0 and (wp, xq) == PARTS[0]), stop=(k == 1 and (wp, xq) == PARTS[-1]))
                    o.then_inc(s.u_ready, 1)

            def turn_v(i):
                for q in range(NQ):
                    pe.wait_ge(s.v_done, 2 * i + 1 + (q > 0))
                    pe.wait_ge(s.u_done, 12 * i + 9 + q)
                    for r in range(2):
                        for k in range(2):
                            t = 2 * q + r
                            o = nc.tensor.transpose(bk[0:T, (3 + q) % 4, r * D + k * 128:r * D + (k + 1) * 128],
                                                    uc[:, 4 + k, t * T:(t + 1) * T], ident)
                    o.then_inc(s.vt_ready, 1)

            def inverse(i, j):
                if j == 0:
                    pe.wait_ge(s.vf_done, 6 * i + 5)
                pe.wait_ge(s.pw_done, 23 * i + 12 * j + 12 - j)
                for q in range(NQ):
                    for k in range(2):
                        for f in (2 * j, 2 * j + 1):
                            o = mm(bk[:, q, k * BL:(k + 1) * BL], xf[j][:, f % 2, q, k * 128:(k + 1) * 128],
                                   idft[:, f, :], start=(f == 0 and k == 0), stop=(f == 3),
                                   skip_group_check=True)
                    if j == 1:
                        o.then_inc(s.y_ready, 1)

            def output(i):
                for j in range(3):
                    pe.wait_ge(s.y_done, 6 * i + 2 * j + 2)
                    for t in (2 * j, 2 * j + 1):
                        for k in range(2):
                            o = mm(bk[0:T, (3 + j) % 4, (t % 2) * D:(t % 2 + 1) * D],
                                   yt[:, k, t * T:(t + 1) * T], wout[:, k, :], start=(k == 0), stop=(k == 1))
                    o.then_inc(s.o_ready, 1)

            def turn_back(c):
                pe.wait_ge(s.out_rows_done, 3 * c)
                pe.wait_ge(s.f1_done, 16 * c)
                for j in range(3):
                    pe.wait_ge(s.ln2_done, 6 * c + 2 * j + 2)
                    turn_pair(j, 4 + j).then_inc(s.zt_ready, 1)

            def up(c, lo, hi):
                for u in range(lo, hi):
                    ch, m = u // 8, u % 8
                    pe.wait_ge(s.zt_done, 3 * c + 2 + ch)
                    if u == 3:
                        pe.wait_ge(s.zt_done, 3 * c + 3)
                    if u in (8, 9):
                        pe.wait_ge(s.f1_done, 16 * c + u - 1)
                    elif u == 10:
                        pe.wait_ge(s.out_rows_done, 3 * c + 1)
                    elif u >= 4:
                        pe.wait_ge(s.f1_done, 16 * c + u - (3 if u < 8 else 2))
                    for k in range(2):
                        for wp, xq in PARTS:
                            o = mm(bk[:, up_bank(u), 0:CH], fc1[:, wp, k, m * 128:(m + 1) * 128],
                                   zt[:, xq, k, ch * CH:(ch + 1) * CH],
                                   start=(k == 0 and (wp, xq) == PARTS[0]), stop=(k == 1 and (wp, xq) == PARTS[-1]))
                    o.then_inc(s.f1_ready, 1)

            def down(c, lo, hi):
                for t in range(lo, hi):
                    if t == 0:
                        pe.wait_ge(s.fc2_split, 2)
                        pe.wait_ge(s.f1_done, 16 * c + 5)
                    for k in range(8):
                        if t == 0 and k < 2:
                            pe.wait_ge(s.at_lo_first, 2 * c + k + 1)
                        elif t % 3 == 0:
                            pe.wait_ge(s.at_lo, 14 * c + 8 * (t // 3) + k - 1)
                        for ap, wq in PARTS:
                            o = mm(bk[0:T, down_bank(t), (t % 2) * D:(t % 2 + 1) * D],
                                   at[:, ap, k, (t % 3) * T:(t % 3 + 1) * T], fc2[:, wq, k, :],
                                   start=(k == 0 and (ap, wq) == PARTS[0]), stop=(k == 7 and (ap, wq) == PARTS[-1]))
                    if t % 2:
                        o.then_inc(s.f2_ready, 1)

            def step(i, front, back):
                c = i - 1
                if front:
                    pe.wait_ge(s.h2_done, 3 * i - 1)
                    patches_up(i)
                if back:
                    turn_back(c)
                if front:
                    rows(i)
                if back:
                    up(c, 0, 5)
                if front:
                    turn_front(i)
                if back:
                    up(c, 5, 7)
                if front:
                    gates(i, 0, 6)
                if back:
                    up(c, 7, 8)
                if front:
                    gates(i, 6, 12)
                if back:
                    down(c, 0, 1)
                if front:
                    turn_v(i)
                if back:
                    down(c, 1, 2)
                if front:
                    spectrum_v(i, 0)
                if back:
                    down(c, 2, 3)
                    up(c, 8, 13)
                if front:
                    spectrum_v(i, 1)
                if back:
                    up(c, 13, 16)
                if front:
                    inverse(i, 0)
                if back:
                    down(c, 3, 5)
                if front:
                    inverse(i, 1)
                    output(i)
                if back:
                    down(c, 5, 6)

            def spectrum_v(i, j):
                pe.wait_ge(s.vt_done, 3 * i + 3)
                pe.wait_ge(s.u_done, 12 * i + 12)
                spectrum(s.vf_ready, s.vf_done, i, j, lambda n: (2 + n) % 4)

            pe.wait_ge(s.loads_filter, FILTER)
            pe.wait_ge(s.memsets, 4)
            for c in range(2):
                mm(bk[0:HID, 4 + c, 0:CH], fw1, pet[:, c * CH:(c + 1) * CH], start=True, stop=True
                   ).then_inc(s.fil_ready, 1)
            pe.wait_ge(s.window_done, 1)
            for g in range(6):
                pe.wait_ge(s.onehot_frames, 1 + g // 2)
                if g >= 4:
                    pe.wait_ge(s.fil_steps, 3 * g - 11)
                for j in range(6):
                    jj = 6 * g + j
                    o = mm(bk[:, g, j * 2 * KF:(j + 1) * 2 * KF],
                           setup_all[0:NF, jj * 128:(jj + 1) * 128], dftw, start=True, stop=True)
                o.then_inc(s.stft, 1)
                if g in (2, 3):
                    c = g - 2
                    pe.wait_ge(s.sin_done, c + 1)
                    mm(bk[0:HID, 6 + c, 0:CH], fw2, fh1[:, c * CH:(c + 1) * CH], start=True, stop=True
                       ).then_inc(s.fil_ready, 1)
            pe.wait_ge(s.loads_up, UP)
            pe.wait_ge(s.squares, 1)
            patches_up(0)
            pe.wait_ge(s.squares, 6)
            for t in range(NT):
                pe.wait_ge(s.sin_done, 3 + t // 3)
                mm(bk[0:T, 4 + t // 2, (t % 2) * D:(t % 2 + 1) * D], fh2[:, t * T:(t + 1) * T], fw3,
                   start=True, stop=True).then_inc(s.kt_ready, 1)
            pe.wait_ge(s.loads_proj, PROJ)
            for k in range(KF):
                pe.wait_ge(s.mags, 4 * (k * PARTS_K // KF + 1))
                for g in range(2):
                    o = mm(bk[0:36, 2 + g, 0:DST], mag[V * g:V * g + V, :, k], proj[V * g:V * g + V, k, :],
                           start=(k == 0), stop=(k == KF - 1))
                    if k == KF - 1:
                        o.then_inc(s.enc_ready, 1)
            pe.wait_ge(s.kt_done, 9)
            spectrum(s.kraw_ready, s.kraw_done, 0, 0, lambda n: 4 + n % 4)
            pe.wait_ge(s.enc_done, 2)
            rows(0)
            spectrum(s.kraw_ready, s.kraw_done, 0, 1, lambda n: 4 + n % 4)
            turn_front(0)
            pe.wait_ge(s.win_split, 2)
            gates(0, 0, 12)
            turn_v(0)
            spectrum_v(0, 0)
            spectrum_v(0, 1)
            pe.wait_ge(s.fc1_raw, 1)
            pe.wait_ge(s.kraw_done, 6)
            for m in range(8):
                for k in range(2):
                    o = mm(bk[:, 7, m:m + 1], fc1_raw[:, k, m * 128:(m + 1) * 128], beta[:, k:k + 1],
                           start=(k == 0), stop=(k == 1))
            o.then_inc(s.fc1_bias, 1)
            pe.wait_ge(s.loads_mats, MATS)
            inverse(0, 0)
            inverse(0, 1)
            output(0)
            pe.wait_ge(s.fc1_fold, 3)
            pe.wait_ge(s.fc1_split, 2)
            step(1, True, True)
            with pe.Fori(2, B) as i:
                step(i, True, True)
            step(B, False, True)

        @block.scalar
        def _(act):
            A = nc.scalar.activation

            def spectrum_out(n, bank, done):
                j, part = n // 3, n % 3
                bank = bk[0:T, bank, :].rearrange("p (x c) -> p x c", x=2)
                A(vf[:, j, part, 0:2, :] if part < 2 else vf[:, j, :, 2, :], bank, ACT.Copy).then_inc(done, 1)

            for dst, src in filter_loads:
                act.dma_start(dst, src).then_inc(s.loads_filter, 16)
            for dst, src in spectrum_loads:
                act.dma_start(dst, src).then_inc(s.loads_spectrum, 16)

            def sine(c):
                act.wait_ge(s.reduced, c + 1)
                A((fh1 if c < 2 else fh2)[0:HID, (c % 2) * CH:(c % 2 + 1) * CH], ang[:, c % 2, :], ACT.Sin
                  ).then_inc(s.sin_done, 1)

            def patches(i):
                act.wait_ge(s.h_ready, 3 * i)
                act.wait_ge(s.h1_ready, 2 * i + 2)
                for m in range(2):
                    A(h1t[:, m, 0:NPATCH], bk[:, 0, m * NPATCH:(m + 1) * NPATCH], ACT.Silu, bias=b1[:, m:m + 1]
                      ).then_inc(s.h1_done, 1)

            def rows(i):
                act.wait_ge(s.h2_done, 3 * i)
                for j in range(3):
                    act.wait_ge(s.h_ready, 3 * i + j + 1)
                    A(h[:, 2 * j:2 * j + 2, :], bk[0:T, 1 + j, :], ACT.Copy).then_inc(s.h_done, 1)

            def xt_high(i):
                act.wait_ge(s.u_ready, 12 * i)
                for j in range(3):
                    act.wait_ge(s.xt_ready, 3 * i + j + 1)
                    A(xt[:, 0, :, 2 + j * BL:2 + (j + 1) * BL],
                      bk[:, j, 0:2 * BL].rearrange("p (k t) -> p k t", k=2), ACT.Copy).then_inc(s.xt_hi, 1)

            def last_tap(i, back, lo, hi):
                if lo == 0:
                    act.wait_ge(s.y_done, 6 * i)
                for u in range(lo, hi):
                    ch, m = u // 6, (4, 5, 2, 3, 0, 1)[u % 6]
                    act.wait_ge(s.u_ready, 12 * i + u + 1)
                    A(uc[:, m, ch * CH:(ch + 1) * CH], bk[:, (3 + u) % 4, 2:CH + 2], ACT.Identity,
                      scale=gate[:, m, 3:4], bias=gbias[:, m, 0:1]).then_inc(s.u_first, 1)
                    if back and u % 2:
                        residue(i - 1, u // 2)

            def vt_high(i):
                act.wait_ge(s.vf_ready, 6 * i)
                for q in range(NQ):
                    act.wait_ge(s.vt_ready, 3 * i + q + 1)
                    A(vt[:, 0, :, q, :], bk[0:T, (3 + q) % 4, :].rearrange("p (r c) -> p r c", r=2), ACT.Copy
                      ).then_inc(s.vt_hi, 1)

            def spectrum_v(i, j):
                if j == 0:
                    act.wait_ge(s.pw_done, 23 * i)
                    act.wait_ge(s.o_ready, 3 * i)
                for n in range(3 * j, 3 * j + 3):
                    act.wait_ge(s.vf_ready, 6 * i + n + 1)
                    spectrum_out(n, (2 + n) % 4, s.vf_done)

            def square(g):
                act.wait_ge(s.stft, g + 1)
                A(sqv[:, 6 * g:6 * g + 6, :], bk[:, g, 0:12 * KF].rearrange("p (g k) -> p g k", g=6), ACT.Square
                  ).then_inc(s.squares, 1)

            act.wait_ge(s.memsets, 4)
            sine(0)
            sine(1)
            square(0)
            square(1)
            square(2)
            sine(2)
            square(3)
            sine(3)
            square(4)
            square(5)
            act.wait_ge(s.sums, 1)
            A(root, mag, ACT.Sqrt).then_inc(s.roots, 1)
            act.wait_ge(s.loads_up, UP)
            patches(0)
            act.wait_ge(s.enc_ready, 2)
            for g in range(2):
                A(enc[:, g, :], bk[0:36, 2 + g, 0:DST], ACT.Copy).then_inc(s.enc_done, 1)
            act.wait_ge(s.win_split, 2)
            for n in range(6):
                if n == 3:
                    rows(0)
                act.wait_ge(s.kraw_ready, n + 1)
                spectrum_out(n, 4 + n % 4, s.kraw_done)
            xt_high(0)
            act.wait_ge(s.gbias_done, 6)
            last_tap(0, False, 0, 12)
            vt_high(0)
            act.wait_ge(s.kf_steps, 12)
            spectrum_v(0, 0)
            spectrum_v(0, 1)
            act.wait_ge(s.fc1_fold, 2)
            A(fc1[:, 0], fc1_raw, ACT.Copy).then_inc(s.fc1_split, 1)
            act.wait_ge(s.fc2_raw, 1)
            A(fc2[:, 0].rearrange("p a n -> p (a n)"), scale, ACT.Copy).then_inc(s.fc2_split, 1)

            def silu(c, lo, hi):
                for u in range(lo, hi):
                    bank = bk[:, up_bank(u), 0:CH]
                    if u == 0:
                        act.wait_ge(s.fc2_split, 2)
                    act.wait_ge(s.f1_ready, 16 * c + u + 1)
                    if u in (2, 3):
                        act.wait_ge(s.at_lo_first, 2 * c + u - 1)
                    else:
                        act.wait_ge(s.at_lo, 14 * c + max(u - 3, 0))
                    A(full[:, u % 2, :], bank, ACT.Silu, bias=fb1[:, u % 8:u % 8 + 1])
                    A(at[:, 0, u % 8, :], bank, ACT.Silu, bias=fb1[:, u % 8:u % 8 + 1]).then_inc(s.f1_done, 1)

            def residue(c, t):
                if t == 0:
                    act.wait_ge(s.coef_done, 2 * c + 2)
                    act.wait_ge(s.out_done, 48 * c)
                A(res[:, t, :], h2[:, t, :], ACT.Identity, scale=coef[:, 0, t:t + 1], bias=coef[:, 1, t:t + 1]
                  ).then_inc(s.res_norm_done, 1)

            def zt_high(c):
                act.wait_ge(s.f1_ready, 16 * c)
                for j in range(3):
                    act.wait_ge(s.zt_ready, 3 * c + j + 1)
                    A(zt[:, 0, :, j * BL:(j + 1) * BL], bk[:, 4 + j, 0:2 * BL].rearrange("p (k t) -> p k t", k=2),
                      ACT.Copy).then_inc(s.zt_hi, 1)

            def step(i, front, back):
                c = i - 1
                if front:
                    patches(i)
                if back:
                    zt_high(c)
                if front:
                    rows(i)
                if back:
                    act.wait_ge(s.f2_ready, 3 * c)
                    silu(c, 0, 5)
                if front:
                    xt_high(i)
                if back:
                    silu(c, 5, 7)
                if front:
                    last_tap(i, back, 0, 6)
                if back:
                    silu(c, 7, 8)
                if front:
                    last_tap(i, back, 6, 12)
                elif back:
                    for t in range(NT):
                        residue(c, t)
                if front:
                    vt_high(i)
                    spectrum_v(i, 0)
                if back:
                    silu(c, 8, 13)
                if front:
                    spectrum_v(i, 1)
                if back:
                    silu(c, 13, 16)

            act.wait_ge(s.fc1_fold, 3)
            step(1, True, True)
            with act.Fori(2, B) as i:
                step(i, True, True)
            step(B, False, True)

        @block.vector
        def _(dve):
            v = nc.vector
            v.memset(uc_all[HID:HID + 1, 36 * 2 * KF:36 * 2 * KF + 2 * L], 1.0).then_inc(s.memsets, 1)
            for p in range(2):
                v.memset(xt[:, p, :, 0:2].bitcast(F32), 0.0).then_inc(s.memsets, 1)

            def split(hi, lo, src, done, n):
                v.tensor_copy(hi, src).then_inc(done, 1)
                dve.wait_ge(done, n + 1)
                v.tensor_tensor(lo, src, hi.bitcast(F32), ALU.subtract).then_inc(done, 1)

            dve.wait_ge(s.loads_text, TEXT)
            v.tensor_scalar(dftw, dftw, wnd, None, ALU.mult).then_inc(s.window_done, 1)
            third = FR * B // 3
            for p in range(3):
                v.tensor_tensor(ohf[:, p * third:(p + 1) * third, :], bc(idf[:, p * third:(p + 1) * third], 2, V),
                                bc(iotar, 1, third), ALU.is_equal).then_inc(s.onehot_frames, 1)

            dve.wait_ge(s.loads_filter, FILTER)
            for c in range(4):
                dve.wait_ge(s.fil_ready, c + 1)
                x, n = ang[:, c % 2, :], turns[:, c % 2, :]
                if c >= 2:
                    dve.wait_ge(s.sin_done, c - 1)
                v.tensor_scalar(x, bk[0:HID, 4 + c, 0:CH], ffreq[:, c // 2:c // 2 + 1], None, ALU.mult
                                ).then_inc(s.fil_steps, 1)
                dve.wait_ge(s.fil_steps, 3 * c + 1)
                v.tensor_scalar(n, x, 1.0 / (2.0 * np.pi), MAGIC, ALU.mult, ALU.add).then_inc(s.fil_steps, 1)
                dve.wait_ge(s.fil_steps, 3 * c + 2)
                v.tensor_scalar(n, n, MAGIC, None, ALU.subtract).then_inc(s.fil_steps, 1)
                dve.wait_ge(s.fil_steps, 3 * c + 3)
                for p in range(2):
                    v.scalar_tensor_tensor(out=x, in0=n, scalar=-SIN_C[p], in1=x, op0=ALU.mult, op1=ALU.add
                                           ).then_inc(s.angle_steps, 1)
                    dve.wait_ge(s.angle_steps, 3 * c + p + 1)
                v.scalar_tensor_tensor(out=x, in0=n, scalar=-SIN_C[2], in1=x, op0=ALU.mult, op1=ALU.add
                                       ).then_inc(s.angle_steps, 1)
                dve.wait_ge(s.angle_steps, 3 * c + 3)
                v.tensor_scalar(x, x, float(np.float32(3.1415925)), -float(np.float32(3.1415925)), ALU.min, ALU.max
                                ).then_inc(s.reduced, 1)
            dve.wait_ge(s.loads_spectrum, SPECTRUM)
            split(dft[:, 0].rearrange("p r f m -> p (r f m)"), dft[:, 1].rearrange("p r f m -> p (r f m)"), dft_raw,
                  s.dft_split, 0)
            dve.wait_ge(s.loads_raw, RAW)
            dve.wait_ge(s.memsets, 4)
            split(rowb[:, 0, :], rowb[:, 1, :], row_raw, s.rows_split, 0)
            v.tensor_copy(oht[V:RB, :], oht_raw).then_inc(s.rows_split, 1)
            dve.wait_ge(s.squares, 6)
            v.tensor_tensor(mag, sqv[:, :, 0:KF], sqv[:, :, KF:2 * KF], ALU.add).then_inc(s.sums, 1)
            dve.wait_ge(s.roots, 1)
            for p in range(PARTS_K):
                ks = slice(-(-p * KF // PARTS_K), -(-(p + 1) * KF // PARTS_K))
                v.tensor_scalar(inv[:, :, ks], root[:, :, ks], 1e-30, None, ALU.max).then_inc(s.mags, 1)
                dve.wait_ge(s.mags, 4 * p + 1)
                v.reciprocal(inv[:, :, ks], inv[:, :, ks]).then_inc(s.mags, 1)
                dve.wait_ge(s.mags, 4 * p + 2)
                v.scalar_tensor_tensor(out=inv[:, :, ks], in0=mag[:, :, ks], scalar=0.5, in1=inv[:, :, ks],
                                       op0=ALU.mult, op1=ALU.mult).then_inc(s.mags, 1)
                dve.wait_ge(s.mags, 4 * p + 3)
                v.scalar_tensor_tensor(out=mag[:, :, ks], in0=root[:, :, ks], scalar=0.5, in1=inv[:, :, ks],
                                       op0=ALU.mult, op1=ALU.add).then_inc(s.mags, 1)
            for j in range(3):
                dve.wait_ge(s.kt_ready, 2 * j + 2)
                v.tensor_tensor(krt[:, :, j, :], bk[0:T, 4 + j, :].rearrange("p (r c) -> p r c", r=2),
                                decay[:, 2 * j:2 * j + 2, :], ALU.mult).then_inc(s.kt_done, 1)
                dve.wait_ge(s.kt_done, 3 * j + 1)
                split(vt[:, 0, :, j, :], vt[:, 1, :, j, :], krt[:, :, j, :], s.kt_done, 3 * j + 1)
            dve.wait_ge(s.loads_up, UP)
            G = lambda n: gate[:, :, n:n + 1]
            v.tensor_tensor(gbias[:, :, 1:2], G(1), G(2), ALU.add).then_inc(s.gbias_done, 1)
            dve.wait_ge(s.gbias_done, 1)
            v.tensor_tensor(gbias[:, :, 0:1], gbias[:, :, 1:2], G(3), ALU.add).then_inc(s.gbias_done, 1)
            dve.wait_ge(s.gbias_done, 2)
            v.tensor_tensor(gbias[:, :, 0:1], gbias[:, :, 0:1], G(0), ALU.mult).then_inc(s.gbias_done, 1)
            v.tensor_tensor(gbias[:, :, 1:2], gbias[:, :, 1:2], G(0), ALU.mult).then_inc(s.gbias_done, 1)
            dve.wait_ge(s.gbias_done, 4)
            v.tensor_tensor(gbias[:, :, 0:1], gbias[:, :, 0:1], G(4), ALU.add).then_inc(s.gbias_done, 1)
            v.tensor_tensor(gbias[:, :, 2:3], G(1), G(0), ALU.mult).then_inc(s.gbias_done, 1)
            v.memset(mhalf[:], -0.5).then_inc(s.pwr_const, 1)
            dve.wait_ge(s.loads_mats, MATS)
            v.tensor_scalar(fb2, fb2, 0.5, None, ALU.mult).then_inc(s.pwr_const, 1)

            def filter_spectrum(j):
                dve.wait_ge(s.kraw_done, 3 * j + 3)
                re, im = vf[:, j, 0], vf[:, j, 1]
                v.tensor_copy(kf[:, j, 0, 0, :], re[:, 0, :]).then_inc(s.kf_steps, 1)
                v.tensor_copy(kf[:, j, 0, 1, :], im[:, 0, :]).then_inc(s.kf_steps, 1)
                for d in (1, 2):
                    v.scalar_tensor_tensor(out=kf[:, j, d, 0, :], in0=im[:, d - 1, :], scalar=sgn[:, 1:2],
                                           in1=re[:, d, :], op0=ALU.mult, op1=ALU.add).then_inc(s.kf_steps, 1)
                    v.scalar_tensor_tensor(out=kf[:, j, d, 1, :], in0=re[:, d - 1, :], scalar=sgn[:, 0:1],
                                           in1=im[:, d, :], op0=ALU.mult, op1=ALU.add).then_inc(s.kf_steps, 1)

            def onehot(i):
                dve.wait_ge(s.ids_in, 16 * i + 16)
                dve.wait_ge(s.h_ready, 3 * i)
                v.tensor_scalar(oht[0:V, NPATCH:L], ids, iotap[:, 0:1], None, ALU.is_equal
                                ).then_inc(s.onehot_done, 1)
                src = rowe[:, i, :] if isinstance(i, int) else \
                    rowe[:, bass.ds(i, 1), :].rearrange("p b c -> p (b c)")
                split(rowb[V:V + FR, 0, DEMB:D], rowb[V:V + FR, 1, DEMB:D], src, s.onehot_done, 3 * i + 1)

            def moments(i, mv, rows_done, mv_done):
                dve.wait_ge(rows_done, 6 * i + 6)
                v.tensor_tensor(mv[:, :, 0], st[:, :, 1], st[:, :, 4], ALU.add).then_inc(mv_done, 1)
                v.tensor_tensor(dif[:, :, 0], st[:, :, 1], st[:, :, 4], ALU.subtract).then_inc(mv_done, 1)
                v.tensor_tensor(dif[:, :, 1], st[:, :, 2], st[:, :, 5], ALU.add).then_inc(mv_done, 1)
                dve.wait_ge(mv_done, 6 * i + 3)
                v.tensor_scalar(mv[:, :, 0], mv[:, :, 0], 0.5, None, ALU.mult).then_inc(mv_done, 1)
                v.scalar_tensor_tensor(out=dif[:, :, 0], in0=dif[:, :, 0], scalar=0.25, in1=dif[:, :, 0],
                                       op0=ALU.mult, op1=ALU.mult).then_inc(mv_done, 1)
                dve.wait_ge(mv_done, 6 * i + 5)
                v.scalar_tensor_tensor(out=mv[:, :, 1], in0=dif[:, :, 1], scalar=1.0 / D, in1=dif[:, :, 0],
                                       op0=ALU.mult, op1=ALU.add).then_inc(mv_done, 1)
                dve.wait_ge(mv_done, 6 * i + 6)

            def norm2(c):
                dve.wait_ge(s.res_done, c)
                moments(c, mv2, s.st2_done, s.mv2_done)
                v.tensor_scalar(va2[:, 0, :], mv2[:, :, 1], EPS, None, ALU.add).then_inc(s.va2_done, 1)
                v.tensor_scalar(va2[:, 1, :], mv2[:, :, 1], 1.0 + EPS, EPS * EPS, ALU.mult, ALU.add
                                ).then_inc(s.va2_done, 1)

            def apply2(c):
                dve.wait_ge(s.rs2_done, 2 * c + 1)
                dve.wait_ge(s.xt_ready, 3 * c + 3)
                for t in range(NT):
                    v.tensor_scalar(ln[:, t, :], h2[:, t, :], mv2[:, t, 0:1], rs2[:, 1, t:t + 1],
                                    ALU.subtract, ALU.mult).then_inc(s.ln2_done, 1)
                dve.wait_ge(s.rs2_done, 2 * c + 2)
                v.tensor_scalar(coef[:, 0, :], rs2[:, 0, :], 1.0, None, ALU.add).then_inc(s.coef_done, 1)
                v.scalar_tensor_tensor(out=coef[:, 1, :], in0=mv2[:, :, 0], scalar=-1.0, in1=rs2[:, 0, :],
                                       op0=ALU.mult, op1=ALU.mult).then_inc(s.coef_done, 1)

            def norm1(i):
                for t in range(NT):
                    dve.wait_ge(s.h_done, 3 * i + t // 2 + 1)
                    v.bn_stats(st[:, t, :], h[:, t, :]).then_inc(s.st1_done, 1)
                moments(i, mv1, s.st1_done, s.mv1_done)
                v.tensor_scalar(va1[:], mv1[:, :, 1], EPS, None, ALU.add).then_inc(s.va1_done, 1)

            def apply1(i):
                dve.wait_ge(s.rs1_done, 2 * i + 1)
                dve.wait_ge(s.zt_ready, 3 * i)
                dve.wait_ge(s.ln2_done, 6 * i)
                for t in range(NT):
                    if t == 2:
                        dve.wait_ge(s.rs1_done, 2 * i + 2)
                    v.tensor_scalar(ln[:, t, :], h[:, t, :], mv1[:, t, 0:1], rs1[:, t:t + 1],
                                    ALU.subtract, ALU.mult).then_inc(s.ln1_done, 1)

            def at_low(c):
                for u in range(2):
                    dve.wait_ge(s.f1_done, 16 * c + u + 1)
                    v.tensor_tensor(at[:, 1, u, :], full[:, u, :], at[:, 0, u, :].bitcast(F32), ALU.subtract
                                    ).then_inc(s.at_lo_first, 1)

            def xt_low(i):
                for j in range(3):
                    dve.wait_ge(s.xt_hi, 3 * i + j + 1)
                    cols = slice(2 + j * BL, 2 + (j + 1) * BL)
                    v.tensor_tensor(xt[:, 1, :, cols], bk[:, j, 0:2 * BL].rearrange("p (k t) -> p k t", k=2),
                                    xt[:, 0, :, cols].bitcast(F32), ALU.subtract).then_inc(s.xt_done, 1)

            def zt_low(c):
                for j in range(3):
                    dve.wait_ge(s.zt_hi, 3 * c + j + 1)
                    cols = slice(j * BL, (j + 1) * BL)
                    v.tensor_tensor(zt[:, 1, :, cols], bk[:, 4 + j, 0:2 * BL].rearrange("p (k t) -> p k t", k=2),
                                    zt[:, 0, :, cols].bitcast(F32), ALU.subtract).then_inc(s.zt_done, 1)

            def vt_low(i):
                for q in range(NQ):
                    dve.wait_ge(s.vt_hi, 3 * i + q + 1)
                    v.tensor_tensor(vt[:, 1, :, q, :], bk[0:T, (3 + q) % 4, :].rearrange("p (r c) -> p r c", r=2),
                                    vt[:, 0, :, q, :].bitcast(F32), ALU.subtract).then_inc(s.vt_done, 1)

            def taps(i):
                for u in range(12):
                    ch, m = u // 6, (4, 5, 2, 3, 0, 1)[u % 6]
                    dst = uc[:, m, ch * CH:(ch + 1) * CH]
                    dve.wait_ge(s.u_first, 12 * i + u + 1)
                    v.scalar_tensor_tensor(out=dst, in0=bk[:, (3 + u) % 4, 1:CH + 1], scalar=gate[:, m, 2:3],
                                           in1=dst, op0=ALU.mult, op1=ALU.add).then_inc(s.u_tap1, 1)
                    dve.wait_ge(s.u_tap1, 12 * i + u + 1)
                    v.scalar_tensor_tensor(out=dst, in0=bk[:, (3 + u) % 4, 0:CH], scalar=gate[:, m, 1:2],
                                           in1=dst, op0=ALU.mult, op1=ALU.add).then_inc(s.u_done, 1)
                    if u == 5:
                        dve.wait_ge(s.u_done, 12 * i + 6)
                        v.tensor_tensor(uc[:, :, 0:2], uc[:, :, 0:2], gbias[:, :, 1:3], ALU.subtract
                                        ).then_inc(s.u_edge, 1)

            def product(i, j, d):
                base = 23 * i + 12 * j + (0, 4, 9 - j)[d]
                if d == 0:
                    dve.wait_ge(s.vf_done, 6 * i + 3 + 3 * j)
                if d == 0 and j == 0:
                    dve.wait_ge(s.y_ready, 3 * i)
                    dve.wait_ge(s.res_done, i)
                    dve.wait_ge(s.xt_ready, 3 * i + 3)
                nq = NQ - d
                x = xf[j][:, :, d:NQ, :]
                if d < 2:
                    t0 = x if d == 0 else ta[:, :, 0:nq, :] if j == 0 else near
                    t1 = tb[:, :, 0:nq, :]
                    for part, t in ((0, t0), (1, t1)):
                        if (j, d, part) == (1, 1, 0):
                            continue
                        if d and part == 1:
                            dve.wait_ge(s.pw_done, base)
                        v.tensor_tensor(t, bc(vf[:, j, part, 0:nq, :], 1, 2), bc(kf[:, j, d, :, :], 2, nq), ALU.mult
                                        ).then_inc(s.pw_done, 1)
                    n = 2 - (j == 1 and d == 1)
                    dve.wait_ge(s.pw_done, base + n)
                    if (j, d) == (1, 1):
                        dve.wait_ge(s.near_done, i + 1)
                else:
                    t0, t1 = far[:, j, 0], far[:, j, 1]
                    n = 0
                    dve.wait_ge(s.far_done, 4 * i + 2 * j + 2)
                if d:
                    v.tensor_tensor(x, x, t0, ALU.add).then_inc(s.pw_done, 1)
                    n += 1
                    dve.wait_ge(s.pw_done, base + n)
                v.tensor_tensor(x[:, 0], x[:, 0], t1[:, 1], ALU.subtract).then_inc(s.pw_done, 1)
                v.tensor_tensor(x[:, 1], x[:, 1], t1[:, 0], ALU.add).then_inc(s.pw_done, 1)
                dve.wait_ge(s.pw_done, base + n + 2)

            def finish(c, j):
                dve.wait_ge(s.f2_ready, 3 * c + j + 1)
                if j == 0:
                    dve.wait_ge(s.res_done, c + 1)
                rows = res[:, 2 * j:2 * j + 2, :].rearrange("p t c -> p (t c)")
                v.scalar_tensor_tensor(out=rows, in0=bk[0:T, down_bank(2 * j), :], scalar=0.5, in1=rows,
                                       op0=ALU.mult, op1=ALU.add).then_inc(s.out_rows_done, 1)

            def gate_y(i):
                dve.wait_ge(s.u_done, 12 * i + 12)
                dve.wait_ge(s.u_edge, i + 1)
                for q in range(NQ):
                    dve.wait_ge(s.y_ready, 3 * i + q + 1)
                    for k in range(2):
                        v.scalar_tensor_tensor(out=yt[:, k, q * BL:(q + 1) * BL], in0=bk[:, q, k * BL:(k + 1) * BL],
                                               scalar=fbias[:, k:k + 1], in1=uc[:, k, q * BL:(q + 1) * BL],
                                               op0=ALU.add, op1=ALU.mult).then_inc(s.y_done, 1)

            def residual(i):
                for j in range(3):
                    dve.wait_ge(s.o_ready, 3 * i + j + 1)
                    if j == 0:
                        dve.wait_ge(s.h_bias_done, i + 1)
                        dve.wait_ge(s.res_done, i)
                    v.tensor_tensor(h2[:, 2 * j:2 * j + 2, :], bk[0:T, (3 + j) % 4, :].rearrange(
                        "p (t c) -> p t c", t=2), h[:, 2 * j:2 * j + 2, :], ALU.add).then_inc(s.h2_done, 1)
                    dve.wait_ge(s.h2_done, 3 * i + j + 1)
                    for t in (2 * j, 2 * j + 1):
                        v.bn_stats(st[:, t, :], h2[:, t, :]).then_inc(s.st2_done, 1)

            def step(i, front, back):
                c = i - 1
                if front:
                    onehot(i)
                if back:
                    apply2(c)
                    zt_low(c)
                if front:
                    norm1(i)
                if back:
                    at_low(c)
                if front:
                    apply1(i)
                    xt_low(i)
                    taps(i)
                    vt_low(i)
                if back:
                    finish(c, 0)
                if front:
                    for j in range(2):
                        for d in range(NQ):
                            product(i, j, d)
                if back:
                    finish(c, 1)
                if front:
                    gate_y(i)
                    residual(i)
                    norm2(i)
                if back:
                    finish(c, 2)

            dve.wait_ge(s.loads_q1, 32)
            v.scalar_tensor_tensor(out=scale, in0=quant, scalar=-128.0, in1=scale, op0=ALU.add, op1=ALU.mult
                                   ).then_inc(s.fc1_raw, 1)
            dve.wait_ge(s.rows_in, 16 * 4)
            onehot(0)
            norm1(0)
            filter_spectrum(0)
            apply1(0)
            xt_low(0)
            filter_spectrum(1)
            dve.wait_ge(s.gbias_done, 6)
            taps(0)
            vt_low(0)
            dve.wait_ge(s.kf_steps, 12)
            for d in range(NQ):
                product(0, 0, d)
            dve.wait_ge(s.fc1_bias, 1)
            for k in range(2):
                v.tensor_scalar(fc1_raw[:, k, :], fc1_raw[:, k, :], gamma[:, k:k + 1], None, ALU.mult
                                ).then_inc(s.fc1_fold, 1)
            v.tensor_tensor(fb1, bk[:, 7, 0:8], fb1, ALU.add).then_inc(s.fc1_fold, 1)
            for d in range(NQ):
                product(0, 1, d)
            gate_y(0)
            dve.wait_ge(s.loads_q2, 32)
            v.scalar_tensor_tensor(out=scale, in0=quant, scalar=-128.0, in1=scale, op0=ALU.add, op1=ALU.mult
                                   ).then_inc(s.fc2_raw, 1)
            residual(0)
            norm2(0)
            step(1, True, True)
            with dve.Fori(2, B) as i:
                step(i, True, True)
            step(B, False, True)

        @block.gpsimd
        def _(pool):
            g = nc.gpsimd
            g.memset(oht[:].bitcast(F32), 0.0).then_inc(s.memsets, 1)
            pool.wait_ge(s.loads_up, UP)
            g.tensor_copy(win[:, 0], win_raw).then_inc(s.win_split, 1)
            pool.wait_ge(s.win_split, 1)
            g.tensor_tensor(win[:, 1], win_raw, win[:, 0].bitcast(F32), ALU.subtract).then_inc(s.win_split, 1)
            pool.wait_ge(s.pwr_const, 2)
            pool.wait_ge(s.loads_mats, MATS)

            def far_product(i, j):
                pool.wait_ge(s.vf_done, 6 * i + 3 + 3 * j)
                pool.wait_ge(s.kf_steps, 12)
                for part in range(2):
                    g.tensor_tensor(far[:, j, part], bc(vf[:, j, part, 0:1, :], 1, 2), bc(kf[:, j, 2, :, :], 2, 1),
                                    ALU.mult).then_inc(s.far_done, 1)

            def at_low(c, lo, hi):
                for u in range(lo, hi):
                    pool.wait_ge(s.f1_done, 16 * c + u + 1)
                    g.tensor_tensor(at[:, 1, u % 8, :], full[:, u % 2, :], at[:, 0, u % 8, :].bitcast(F32),
                                    ALU.subtract).then_inc(s.at_lo, 1)

            def step(i, front, back):
                c = i - 1
                if back:
                    pool.wait_ge(s.va2_done, 2 * i)
                    for a in (1, 0):
                        g.tensor_tensor(rs2[:, a, :], va2[:, a, :], mhalf[:], ALU.pow).then_inc(s.rs2_done, 1)
                if front:
                    pool.wait_ge(s.va1_done, i + 1)
                    for lo, hi in ((0, 2), (2, NT)):
                        g.tensor_tensor(rs1[:, lo:hi], va1[:, lo:hi], mhalf[:, lo:hi], ALU.pow
                                        ).then_inc(s.rs1_done, 1)
                if back:
                    at_low(c, 2, 8)
                if front:
                    for ch in range(2):
                        pool.wait_ge(s.u_done, 12 * i + 6 * ch + 4)
                        pool.wait_ge(s.u_edge, i + 1)
                        vv = uc[:, 4:6, ch * CH:(ch + 1) * CH]
                        g.tensor_tensor(vv, vv, uc[:, 2:4, ch * CH:(ch + 1) * CH], ALU.mult
                                        ).then_inc(s.v_done, 1)
                if back:
                    pool.wait_ge(s.res_norm_done, 6 * i)
                    g.tensor_tensor(res[:], res[:], bc(fb2, 1, NT), ALU.add).then_inc(s.res_done, 1)
                if front:
                    far_product(i, 0)
                if back:
                    at_low(c, 8, 13)
                if front:
                    far_product(i, 1)
                    pool.wait_ge(s.pw_done, 23 * i + 12)
                    g.tensor_tensor(near, bc(vf[:, 1, 0, 0:2, :], 1, 2), bc(kf[:, 1, 1, :, :], 2, 2), ALU.mult
                                    ).then_inc(s.near_done, 1)
                if back:
                    at_low(c, 13, 16)
                if front:
                    pool.wait_ge(s.ln1_done, 6 * i + 6)
                    g.tensor_tensor(h, h, bc(bout, 1, NT), ALU.add).then_inc(s.h_bias_done, 1)

            step(0, True, False)
            pool.wait_ge(s.fc1_split, 1)
            g.tensor_tensor(fc1[:, 1], fc1_raw, fc1[:, 0].bitcast(F32), ALU.subtract).then_inc(s.fc1_split, 1)
            pool.wait_ge(s.fc2_split, 1)
            g.tensor_tensor(fc2[:, 1].rearrange("p a n -> p (a n)"), scale,
                            fc2[:, 0].rearrange("p a n -> p (a n)").bitcast(F32), ALU.subtract
                            ).then_inc(s.fc2_split, 1)
            step(1, True, True)
            with pool.Fori(2, B) as i:
                step(i, True, True)
            step(B, False, True)


def constants():
    f64 = np.float64
    n = np.arange(NF, dtype=f64)
    k = np.arange(KF, dtype=f64)
    w = 2.0 * np.pi * n[:, None] * k[None, :] / NF
    stft = np.concatenate([np.cos(w), -np.sin(w)], axis=1)
    t = np.arange(L, dtype=np.float32) / np.float32(L - 1)
    phase = np.float32(1e-4) * (np.float32(2.0 * np.pi) * np.arange(L, dtype=np.float32) / np.float32(L))
    features = np.stack([t, np.cos(phase), -np.sin(phase), np.ones_like(t)])[:, ::-1]
    delta = np.abs(np.linspace(np.log(0.01) / 0.3, np.log(0.01) / 1.5, D).astype(np.float32))
    decay = np.exp(-t[:, None] * delta[None, :])[::-1].reshape(NT, T, D).transpose(1, 0, 2)
    f = np.arange(BL, dtype=f64)
    th = np.pi * (2 * f[None, :] + 1) * np.arange(BL, dtype=f64)[:, None] / ND
    fwd = np.stack([np.cos(th), -np.sin(th)], axis=0).reshape(2, 2, T, 2, T)
    dft = fwd.transpose(2, 1, 3, 0, 4).reshape(T, 8 * T)
    inv = np.stack([np.cos(th), -np.sin(th)], axis=0) * (2.0 / ND)
    idft = inv.reshape(2, BL, 2, T).transpose(3, 2, 0, 1).reshape(T, 4, BL)
    sg = (-1.0) ** np.arange(T)
    coord = np.clip((np.arange(NTXT) + 0.5) * (FR / NTXT) - 0.5, 0.0, FR - 1.0)
    i0 = np.floor(coord).astype(int)
    i1 = np.minimum(i0 + 1, FR - 1)
    wt = (coord - i0).astype(np.float32)
    rows = np.zeros((FR + 2, L), np.float32)
    cols = NPATCH + np.arange(NTXT)
    np.add.at(rows, (i0, cols), np.float32(1.0) - wt)
    np.add.at(rows, (i1, cols), wt)
    rows[FR, NPATCH:] = 1.0
    rows[FR + 1, :NPATCH] = 1.0
    c = dict(stft_mat=stft, features=features, decay=decay, dft=dft, idft=idft,
             signs=np.stack([sg, -sg], axis=1), interp=rows, ident=np.eye(128),
             iota_row=np.tile(np.arange(V), (NF, 1)), iota_col=np.arange(V)[:, None])
    return {k: np.asarray(v, dtype=np.float32) for k, v in c.items()}


def layout(i):
    x = i["x"].reshape(B, 3, 14, 16, 14, 16).transpose(0, 1, 3, 5, 2, 4).reshape(B, KP // 128, 128, NPATCH)
    c = constants()
    pos = np.arange(FR)[None, :] * NF + np.arange(NF)[:, None] - NF // 2
    pos = np.abs(pos)
    pos = np.where(pos >= NTXT, 2 * (NTXT - 1) - pos, pos)
    frames = i["x_txt"][:, pos].transpose(1, 0, 2).reshape(NF, 2, 4 * FR).transpose(0, 2, 1).reshape(NF, B * FR)
    tiles = lambda w, k=128: w.reshape(w.shape[0] // k, k, w.shape[1]).transpose(1, 0, 2)
    cols = lambda v: v.reshape(-1, 128).T
    gate = np.stack([cols(i["L0_attn_b_in"]), *(cols(i["L0_attn_short_w"][:, t]) for t in range(3)),
                     cols(i["L0_attn_short_b"])], axis=2)
    rows = np.zeros((RB, D), np.float32)
    rows[0:V, 0:DEMB] = i["L0_txt_emb_table"]
    rows[V + FR, DEMB:] = i["L0_txt_proj_b"]
    rows[V + FR + 1] = i["L0_tok_b2"]
    small = dict(c, b1=cols(i["L0_tok_b1"]), fbias=cols(i["L0_attn_filter_bias"]), gate=gate.reshape(128, -1),
                 gamma=cols(i["L0_ffn_ln_gamma"]), beta=cols(i["L0_ffn_ln_beta"]), fb1=cols(i["L0_ffn_fc1_bias"]))
    small = [np.pad(small[n], ((0, 128 - small[n].shape[0]), (0, 0))) for n in SMALL]
    freqs = np.pad(np.stack([i["L0_attn_f1"], i["L0_attn_f2"]], axis=1), ((0, 1), (0, 0)))
    o = dict(
        x=x.transpose(0, 2, 1, 3), ids=np.repeat(i["x_txt"][:, None, :], V, axis=1), ids_frames=frames,
        frame_consts=np.concatenate([c["iota_row"], c["stft_mat"], i["L0_txt_window"][:, None]], axis=1),
        filter_first=np.concatenate([c["features"], np.vstack([i["L0_attn_W1"], i["L0_attn_b1"]])], axis=1),
        filter_hidden=np.concatenate([np.vstack([i["L0_attn_W2"], i["L0_attn_b2"]]),
                                      np.vstack([i["L0_attn_W3"], i["L0_attn_b3"]]), freqs], axis=1),
        dft=c["dft"], decay=c["decay"], interp=c["interp"], idft=c["idft"],
        small=np.concatenate(small, axis=1), rows=rows,
        proj=i["L0_txt_proj_w"].reshape(DST, KF, V).transpose(2, 1, 0),
        w1=tiles(i["L0_tok_W1"]), w2=tiles(i["L0_tok_W2"]), win=tiles(i["L0_attn_W_in"]),
        wout=tiles(i["L0_attn_W_out"]), biases=np.concatenate([i["L0_attn_b_out"], i["L0_ffn_fc2_bias"]]),
        fc1_q=tiles(i["L0_ffn_fc1_q"]).reshape(128, -1), fc2_q=tiles(i["L0_ffn_fc2_q"]).reshape(128, -1),
        fc1_scales=i["L0_ffn_fc1_scales"].reshape(-1), fc2_scales=i["L0_ffn_fc2_scales"].reshape(-1))
    return {k: np.ascontiguousarray(v) for k, v in o.items()}


def kernel(**inputs):
    import concourse.bacc as bacc
    from concourse.bass_utils import run_bass_kernel_spmd

    nc = bacc.Bacc("TRN2", target_bir_lowering=False, num_devices=1)
    data = layout({k: np.asarray(v) for k, v in inputs.items()})
    arrays = {"in_" + k: v for k, v in data.items()}
    aps = {k: nc.dram_tensor("in_" + k, v.shape, mybir.dt.from_np(v.dtype), kind="ExternalInput").ap()
           for k, v in data.items()}
    out = nc.dram_tensor("out", (B, L, D), F32, kind="ExternalOutput").ap()
    program(nc, aps, out)
    r = run_bass_kernel_spmd(nc, [arrays], core_ids=[0])
    return r.results[0]["out"]
```
